# Optimizing a Trainium2 kernel written in Bass

```python
import numpy as np
import jax
import jax.numpy as jnp

def _softmax(x, axis=-1):
    return jax.nn.softmax(x, axis=axis)

def _gelu(x):
    return jax.nn.gelu(x, approximate=True)

def _silu(x):
    return jax.nn.silu(x)

def _sigmoid(x):
    return jax.nn.sigmoid(x)

def _layernorm(x, axis=-1, eps=1e-05):
    m = jnp.mean(x, axis=axis, keepdims=True)
    v = jnp.var(x, axis=axis, keepdims=True)
    return (x - m) / jnp.sqrt(v + eps)

def _scatter_add(tgt, idx, src, axis=0):
    return tgt.at[idx].add(src)

def _segment_sum(src, seg, n):
    return jax.ops.segment_sum(src, seg, n)
kernel_name = 'mk_conv_attn_hybrid_d2_conv_nchw1024_r4_63558c'

def setup_inputs(seed: int=0):
    np.random.seed(seed)
    _w = jnp.asarray

    def _rec_inputs():
        import jax
        import jax.numpy as jnp
        _gk = jax.random.key(seed)
        x = -0.000125 + 0.9999 * jax.random.normal(jax.random.fold_in(_gk, 1), (8, 256, 16, 16), jnp.float32)
        return x
    x = _rec_inputs()

    def _L0_conv_setup():
        import jax, jax.numpy as jnp
        import numpy as np
        from jax import lax
        B, C, HW = (8, 256, 16)
        WS, NH, K = (8, 8, 8)
        HD = C // NH
        MLP_HID = 512
        EPS = 1e-05

        def _dct_mat(n):
            x = np.arange(n)
            u = np.arange(n)[:, None]
            D = np.cos((2 * x[None, :] + 1) * u * np.pi / (2 * n))
            D[0] *= np.sqrt(1.0 / n)
            D[1:] *= np.sqrt(2.0 / n)
            return jnp.asarray(D, dtype=jnp.float32)
        D8 = _dct_mat(K)

        def _rel_pos_index(Wh, Ww):
            seq1 = np.arange(0, (2 * Ww - 1) * Wh, 2 * Ww - 1)
            seq2 = np.arange(0, Ww)
            rel = (seq1[:, None] + seq2[None, :]).reshape(1, -1)
            idx = (rel + rel.T)[:, ::-1].copy()
            return jnp.asarray(idx, dtype=jnp.int32)
        REL_IDX = _rel_pos_index(WS, WS)

        def _ln_c(x, w, b):
            xp = x.transpose(0, 2, 3, 1)
            mu = xp.mean(-1, keepdims=True)
            var = ((xp - mu) ** 2).mean(-1, keepdims=True)
            return ((xp - mu) / jnp.sqrt(var + EPS) * w + b).transpose(0, 3, 1, 2)

        def _dct_rearrange(x):
            b, c, h, w = x.shape
            p = x.reshape(b, c, h // K, K, w // K, K)
            coef = jnp.einsum('ux,vy,bcixjy->bciujv', D8, D8, p)
            return coef.reshape(b, c, h, w)

        def _idct_rearrange(x):
            b, c, h, w = x.shape
            coef = x.reshape(b, c, h // K, K, w // K, K)
            p = jnp.einsum('ux,vy,bciujv->bcixjy', D8, D8, coef)
            return p.reshape(b, c, h, w)

        def _to_windows(x):
            xh = x.transpose(0, 2, 3, 1)
            xh = xh.reshape(B, HW // WS, WS, HW // WS, WS, C).transpose(0, 1, 3, 2, 4, 5)
            return xh.reshape(-1, WS * WS, C)

        def _from_windows(w):
            x = w.reshape(B, HW // WS, HW // WS, WS, WS, C).transpose(0, 1, 3, 2, 4, 5)
            return x.reshape(B, HW, HW, C).transpose(0, 3, 1, 2)

        def _win_attn(qx, kx, vx, wq, bq, wk, bk, wv, bv, wo, bo, bias_table):
            Bw, N, _ = qx.shape

            def proj(x, w, b):
                return (x @ w.T + b).reshape(Bw, N, NH, HD).transpose(0, 2, 1, 3)
            q = proj(qx, wq, bq) * HD ** (-0.5)
            k = proj(kx, wk, bk)
            v = proj(vx, wv, bv)
            attn = jnp.einsum('bhnd,bhmd->bhnm', q, k)
            bias = bias_table[REL_IDX.reshape(-1)].reshape(N, N, NH).transpose(2, 0, 1)
            attn = jax.nn.softmax(attn + bias[None], axis=-1)
            out = jnp.einsum('bhnm,bhmd->bhnd', attn, v).transpose(0, 2, 1, 3).reshape(Bw, N, C)
            return out @ wo.T + bo

        def _forward(feat, a1, a2, n1_w, n1_b, n2_w, n2_b, n3_w, n3_b, c1_w, c1_b, c2_w, c2_b, bn_g, bn_b, fc1_w, fc1_b, fc2_w, fc2_b):
            x_freq = _ln_c(_dct_rearrange(feat), n1_w, n1_b)
            x_spac = _ln_c(feat, n2_w, n2_b)
            fw = _to_windows(x_freq)
            sw = _to_windows(x_spac)
            stf = _idct_rearrange(_from_windows(_win_attn(sw, fw, fw, *a1)))
            fts = _from_windows(_win_attn(fw, sw, sw, *a2))
            y = jnp.concatenate([stf, fts], axis=1)
            y = jnp.einsum('oi,bihw->bohw', c1_w[:, :, 0, 0], y) + c1_b[None, :, None, None]
            y = lax.conv_general_dilated(y, c2_w, (1, 1), 'SAME', dimension_numbers=('NCHW', 'OIHW', 'NCHW')) + c2_b[None, :, None, None]
            mu = y.mean(axis=(0, 2, 3), keepdims=True)
            var = ((y - mu) ** 2).mean(axis=(0, 2, 3), keepdims=True)
            y = (y - mu) / jnp.sqrt(var + EPS) * bn_g[None, :, None, None] + bn_b[None, :, None, None]
            y = jax.nn.relu(y)
            out = feat + y
            t = out.reshape(B, C, HW * HW).transpose(0, 2, 1)
            mu = t.mean(-1, keepdims=True)
            var = ((t - mu) ** 2).mean(-1, keepdims=True)
            tn = (t - mu) / jnp.sqrt(var + EPS) * n3_w + n3_b
            h = jax.nn.gelu(tn @ fc1_w.T + fc1_b, approximate=False)
            t = t + (h @ fc2_w.T + fc2_b)
            return t.transpose(0, 2, 1).reshape(B, C, HW, HW)
        ks = iter(jax.random.split(jax.random.key(seed), 48))

        def rn(shape, s=0.02):
            return jax.random.normal(next(ks), shape, dtype=jnp.float32) * s
        inp = {'feat': jax.random.normal(next(ks), (B, C, HW, HW), dtype=jnp.float32), 'paddings': jnp.zeros((2,), dtype=jnp.int32)}
        T = (2 * WS - 1) ** 2
        for p in ('a1', 'a2'):
            for n in ('wq', 'wk', 'wv', 'wo'):
                inp[p + '_' + n] = rn((C, C))
            for n in ('bq', 'bk', 'bv', 'bo'):
                inp[p + '_' + n] = jnp.zeros((C,), jnp.float32)
            inp[p + '_bias'] = rn((T, NH))
        for n in ('n1', 'n2', 'n3'):
            inp[n + '_w'] = jnp.ones((C,), jnp.float32)
            inp[n + '_b'] = jnp.zeros((C,), jnp.float32)
        inp['c1_w'] = rn((C, 2 * C, 1, 1))
        inp['c1_b'] = jnp.zeros((C,), jnp.float32)
        inp['c2_w'] = rn((C, C, 3, 3))
        inp['c2_b'] = jnp.zeros((C,), jnp.float32)
        inp['bn_g'] = jnp.ones((C,), jnp.float32)
        inp['bn_b'] = jnp.zeros((C,), jnp.float32)
        inp['fc1_w'] = rn((MLP_HID, C))
        inp['fc1_b'] = jnp.zeros((MLP_HID,), jnp.float32)
        inp['fc2_w'] = rn((C, MLP_HID))
        inp['fc2_b'] = jnp.zeros((C,), jnp.float32)
        return inp
    _L0_conv_all = _L0_conv_setup()
    _L0_conv_in = {k: v for k, v in _L0_conv_all.items() if k in ('paddings', 'a1_wq', 'a1_bq', 'a1_wk', 'a1_bk', 'a1_wv', 'a1_bv', 'a1_wo', 'a1_bo', 'a1_bias', 'a2_wq', 'a2_bq', 'a2_wk', 'a2_bk', 'a2_wv', 'a2_bv', 'a2_wo', 'a2_bo', 'a2_bias', 'n1_w', 'n1_b', 'n2_w', 'n2_b', 'n3_w', 'n3_b', 'c1_w', 'c1_b', 'c2_w', 'c2_b', 'bn_g', 'bn_b', 'fc1_w', 'fc1_b', 'fc2_w', 'fc2_b')}
    del _L0_conv_all

    def _L1_attn_setup():
        import jax, jax.numpy as jnp
        import numpy as np
        NUM_HEADS = 16
        HEAD_DIM = 16
        ROPE_BASE = 10000.0

        def _rope_tables(seq_len, dtype=jnp.float32):
            inv_freq = 1.0 / ROPE_BASE ** (jnp.arange(0, HEAD_DIM, 2, dtype=jnp.float32) / HEAD_DIM)
            t = jnp.arange(seq_len, dtype=jnp.float32)
            freqs = jnp.einsum('i,j->ij', t, inv_freq)
            emb = jnp.concatenate([freqs, freqs], axis=-1)
            return (jnp.cos(emb).astype(dtype), jnp.sin(emb).astype(dtype))

        def _rotate_half(x):
            half = x.shape[-1] // 2
            return jnp.concatenate([-x[..., half:], x[..., :half]], axis=-1)
        key = jax.random.key(seed)
        k1, k2, k3 = jax.random.split(key, 3)
        hidden = NUM_HEADS * HEAD_DIM
        x = jax.random.normal(k1, (2, 512, hidden), dtype=jnp.float32)
        w_qkv = jax.random.normal(k2, (hidden, 3 * hidden), dtype=jnp.float32) * hidden ** (-0.5)
        w_out = jax.random.normal(k3, (hidden, hidden), dtype=jnp.float32) * hidden ** (-0.5)
        return {'x': x, 'w_qkv': w_qkv, 'w_out': w_out}
    _L1_attn_all = _L1_attn_setup()
    _L1_attn_in = {k: v for k, v in _L1_attn_all.items() if k in ('w_qkv', 'w_out')}
    del _L1_attn_all

    def _L1_ffn_setup():
        import jax, jax.numpy as jnp
        import numpy as np
        B, S, D, E, K = (4, 512, 256, 8, 2)
        key = jax.random.key(seed)
        k1, k2, k3 = jax.random.split(key, 3)
        x = jax.random.normal(k1, (B, S, D), dtype=jnp.float32)
        gate_w = jax.random.normal(k2, (E, D), dtype=jnp.float32) * (1.0 / np.sqrt(D))
        expert_w = jax.random.normal(k3, (E, D, D), dtype=jnp.float32) * (1.0 / np.sqrt(D))
        return {'x': x, 'gate_w': gate_w, 'expert_w': expert_w}
    _L1_ffn_all = _L1_ffn_setup()
    _L1_ffn_in = {k: v for k, v in _L1_ffn_all.items() if k in ('gate_w', 'expert_w')}
    del _L1_ffn_all
    return {'x': x, 'L0_conv_paddings': _L0_conv_in['paddings'], 'L0_conv_a1_wq': _L0_conv_in['a1_wq'], 'L0_conv_a1_bq': _L0_conv_in['a1_bq'], 'L0_conv_a1_wk': _L0_conv_in['a1_wk'], 'L0_conv_a1_bk': _L0_conv_in['a1_bk'], 'L0_conv_a1_wv': _L0_conv_in['a1_wv'], 'L0_conv_a1_bv': _L0_conv_in['a1_bv'], 'L0_conv_a1_wo': _L0_conv_in['a1_wo'], 'L0_conv_a1_bo': _L0_conv_in['a1_bo'], 'L0_conv_a1_bias': _L0_conv_in['a1_bias'], 'L0_conv_a2_wq': _L0_conv_in['a2_wq'], 'L0_conv_a2_bq': _L0_conv_in['a2_bq'], 'L0_conv_a2_wk': _L0_conv_in['a2_wk'], 'L0_conv_a2_bk': _L0_conv_in['a2_bk'], 'L0_conv_a2_wv': _L0_conv_in['a2_wv'], 'L0_conv_a2_bv': _L0_conv_in['a2_bv'], 'L0_conv_a2_wo': _L0_conv_in['a2_wo'], 'L0_conv_a2_bo': _L0_conv_in['a2_bo'], 'L0_conv_a2_bias': _L0_conv_in['a2_bias'], 'L0_conv_n1_w': _L0_conv_in['n1_w'], 'L0_conv_n1_b': _L0_conv_in['n1_b'], 'L0_conv_n2_w': _L0_conv_in['n2_w'], 'L0_conv_n2_b': _L0_conv_in['n2_b'], 'L0_conv_n3_w': _L0_conv_in['n3_w'], 'L0_conv_n3_b': _L0_conv_in['n3_b'], 'L0_conv_c1_w': _L0_conv_in['c1_w'], 'L0_conv_c1_b': _L0_conv_in['c1_b'], 'L0_conv_c2_w': _L0_conv_in['c2_w'], 'L0_conv_c2_b': _L0_conv_in['c2_b'], 'L0_conv_bn_g': _L0_conv_in['bn_g'], 'L0_conv_bn_b': _L0_conv_in['bn_b'], 'L0_conv_fc1_w': _L0_conv_in['fc1_w'], 'L0_conv_fc1_b': _L0_conv_in['fc1_b'], 'L0_conv_fc2_w': _L0_conv_in['fc2_w'], 'L0_conv_fc2_b': _L0_conv_in['fc2_b'], 'L1_attn_w_qkv': _L1_attn_in['w_qkv'], 'L1_attn_w_out': _L1_attn_in['w_out'], 'L1_ffn_gate_w': _L1_ffn_in['gate_w'], 'L1_ffn_expert_w': _L1_ffn_in['expert_w']}

def reference(x, L0_conv_paddings, L0_conv_a1_wq, L0_conv_a1_bq, L0_conv_a1_wk, L0_conv_a1_bk, L0_conv_a1_wv, L0_conv_a1_bv, L0_conv_a1_wo, L0_conv_a1_bo, L0_conv_a1_bias, L0_conv_a2_wq, L0_conv_a2_bq, L0_conv_a2_wk, L0_conv_a2_bk, L0_conv_a2_wv, L0_conv_a2_bv, L0_conv_a2_wo, L0_conv_a2_bo, L0_conv_a2_bias, L0_conv_n1_w, L0_conv_n1_b, L0_conv_n2_w, L0_conv_n2_b, L0_conv_n3_w, L0_conv_n3_b, L0_conv_c1_w, L0_conv_c1_b, L0_conv_c2_w, L0_conv_c2_b, L0_conv_bn_g, L0_conv_bn_b, L0_conv_fc1_w, L0_conv_fc1_b, L0_conv_fc2_w, L0_conv_fc2_b, L1_attn_w_qkv, L1_attn_w_out, L1_ffn_gate_w, L1_ffn_expert_w):
    import jax
    import jax.numpy as jnp

    def _L0_conv_ref(feat, paddings, a1_wq, a1_bq, a1_wk, a1_bk, a1_wv, a1_bv, a1_wo, a1_bo, a1_bias, a2_wq, a2_bq, a2_wk, a2_bk, a2_wv, a2_bv, a2_wo, a2_bo, a2_bias, n1_w, n1_b, n2_w, n2_b, n3_w, n3_b, c1_w, c1_b, c2_w, c2_b, bn_g, bn_b, fc1_w, fc1_b, fc2_w, fc2_b):
        import jax, jax.numpy as jnp
        import numpy as np
        from jax import lax
        B, C, HW = (8, 256, 16)
        WS, NH, K = (8, 8, 8)
        HD = C // NH
        MLP_HID = 512
        EPS = 1e-05

        def _dct_mat(n):
            x = np.arange(n)
            u = np.arange(n)[:, None]
            D = np.cos((2 * x[None, :] + 1) * u * np.pi / (2 * n))
            D[0] *= np.sqrt(1.0 / n)
            D[1:] *= np.sqrt(2.0 / n)
            return jnp.asarray(D, dtype=jnp.float32)
        D8 = _dct_mat(K)

        def _rel_pos_index(Wh, Ww):
            seq1 = np.arange(0, (2 * Ww - 1) * Wh, 2 * Ww - 1)
            seq2 = np.arange(0, Ww)
            rel = (seq1[:, None] + seq2[None, :]).reshape(1, -1)
            idx = (rel + rel.T)[:, ::-1].copy()
            return jnp.asarray(idx, dtype=jnp.int32)
        REL_IDX = _rel_pos_index(WS, WS)

        def _ln_c(x, w, b):
            xp = x.transpose(0, 2, 3, 1)
            mu = xp.mean(-1, keepdims=True)
            var = ((xp - mu) ** 2).mean(-1, keepdims=True)
            return ((xp - mu) / jnp.sqrt(var + EPS) * w + b).transpose(0, 3, 1, 2)

        def _dct_rearrange(x):
            b, c, h, w = x.shape
            p = x.reshape(b, c, h // K, K, w // K, K)
            coef = jnp.einsum('ux,vy,bcixjy->bciujv', D8, D8, p)
            return coef.reshape(b, c, h, w)

        def _idct_rearrange(x):
            b, c, h, w = x.shape
            coef = x.reshape(b, c, h // K, K, w // K, K)
            p = jnp.einsum('ux,vy,bciujv->bcixjy', D8, D8, coef)
            return p.reshape(b, c, h, w)

        def _to_windows(x):
            xh = x.transpose(0, 2, 3, 1)
            xh = xh.reshape(B, HW // WS, WS, HW // WS, WS, C).transpose(0, 1, 3, 2, 4, 5)
            return xh.reshape(-1, WS * WS, C)

        def _from_windows(w):
            x = w.reshape(B, HW // WS, HW // WS, WS, WS, C).transpose(0, 1, 3, 2, 4, 5)
            return x.reshape(B, HW, HW, C).transpose(0, 3, 1, 2)

        def _win_attn(qx, kx, vx, wq, bq, wk, bk, wv, bv, wo, bo, bias_table):
            Bw, N, _ = qx.shape

            def proj(x, w, b):
                return (x @ w.T + b).reshape(Bw, N, NH, HD).transpose(0, 2, 1, 3)
            q = proj(qx, wq, bq) * HD ** (-0.5)
            k = proj(kx, wk, bk)
            v = proj(vx, wv, bv)
            attn = jnp.einsum('bhnd,bhmd->bhnm', q, k)
            bias = bias_table[REL_IDX.reshape(-1)].reshape(N, N, NH).transpose(2, 0, 1)
            attn = jax.nn.softmax(attn + bias[None], axis=-1)
            out = jnp.einsum('bhnm,bhmd->bhnd', attn, v).transpose(0, 2, 1, 3).reshape(Bw, N, C)
            return out @ wo.T + bo

        def _forward(feat, a1, a2, n1_w, n1_b, n2_w, n2_b, n3_w, n3_b, c1_w, c1_b, c2_w, c2_b, bn_g, bn_b, fc1_w, fc1_b, fc2_w, fc2_b):
            x_freq = _ln_c(_dct_rearrange(feat), n1_w, n1_b)
            x_spac = _ln_c(feat, n2_w, n2_b)
            fw = _to_windows(x_freq)
            sw = _to_windows(x_spac)
            stf = _idct_rearrange(_from_windows(_win_attn(sw, fw, fw, *a1)))
            fts = _from_windows(_win_attn(fw, sw, sw, *a2))
            y = jnp.concatenate([stf, fts], axis=1)
            y = jnp.einsum('oi,bihw->bohw', c1_w[:, :, 0, 0], y) + c1_b[None, :, None, None]
            y = lax.conv_general_dilated(y, c2_w, (1, 1), 'SAME', dimension_numbers=('NCHW', 'OIHW', 'NCHW')) + c2_b[None, :, None, None]
            mu = y.mean(axis=(0, 2, 3), keepdims=True)
            var = ((y - mu) ** 2).mean(axis=(0, 2, 3), keepdims=True)
            y = (y - mu) / jnp.sqrt(var + EPS) * bn_g[None, :, None, None] + bn_b[None, :, None, None]
            y = jax.nn.relu(y)
            out = feat + y
            t = out.reshape(B, C, HW * HW).transpose(0, 2, 1)
            mu = t.mean(-1, keepdims=True)
            var = ((t - mu) ** 2).mean(-1, keepdims=True)
            tn = (t - mu) / jnp.sqrt(var + EPS) * n3_w + n3_b
            h = jax.nn.gelu(tn @ fc1_w.T + fc1_b, approximate=False)
            t = t + (h @ fc2_w.T + fc2_b)
            return t.transpose(0, 2, 1).reshape(B, C, HW, HW)
        a1 = (a1_wq, a1_bq, a1_wk, a1_bk, a1_wv, a1_bv, a1_wo, a1_bo, a1_bias)
        a2 = (a2_wq, a2_bq, a2_wk, a2_bk, a2_wv, a2_bv, a2_wo, a2_bo, a2_bias)
        return _forward(feat, a1, a2, n1_w, n1_b, n2_w, n2_b, n3_w, n3_b, c1_w, c1_b, c2_w, c2_b, bn_g, bn_b, fc1_w, fc1_b, fc2_w, fc2_b)

    def _L1_attn_ref(x, w_qkv, w_out):
        import jax, jax.numpy as jnp
        import numpy as np
        NUM_HEADS = 16
        HEAD_DIM = 16
        ROPE_BASE = 10000.0

        def _rope_tables(seq_len, dtype=jnp.float32):
            inv_freq = 1.0 / ROPE_BASE ** (jnp.arange(0, HEAD_DIM, 2, dtype=jnp.float32) / HEAD_DIM)
            t = jnp.arange(seq_len, dtype=jnp.float32)
            freqs = jnp.einsum('i,j->ij', t, inv_freq)
            emb = jnp.concatenate([freqs, freqs], axis=-1)
            return (jnp.cos(emb).astype(dtype), jnp.sin(emb).astype(dtype))

        def _rotate_half(x):
            half = x.shape[-1] // 2
            return jnp.concatenate([-x[..., half:], x[..., :half]], axis=-1)
        batch, seq_len, hidden = x.shape
        scale = HEAD_DIM ** (-0.5)
        qkv = x @ w_qkv
        qkv = qkv.reshape(batch, seq_len, 3, NUM_HEADS, HEAD_DIM)
        q, k, v = jnp.moveaxis(qkv, 2, 0)
        q = jnp.transpose(q, (0, 2, 1, 3))
        k = jnp.transpose(k, (0, 2, 1, 3))
        v = jnp.transpose(v, (0, 2, 1, 3))
        cos, sin = _rope_tables(seq_len, x.dtype)
        cos = cos[None, None]
        sin = sin[None, None]
        q = q * cos + _rotate_half(q) * sin
        k = k * cos + _rotate_half(k) * sin
        scores = jnp.einsum('bhqd,bhkd->bhqk', q, k) * scale
        causal = jnp.triu(jnp.ones((seq_len, seq_len), dtype=bool), k=1)
        scores = jnp.where(causal, -jnp.inf, scores)
        probs = jax.nn.softmax(scores, axis=-1)
        out = jnp.einsum('bhqk,bhkd->bhqd', probs, v)
        out = jnp.transpose(out, (0, 2, 1, 3)).reshape(batch, seq_len, hidden)
        return out @ w_out

    def _L1_ffn_ref(x, gate_w, expert_w):
        import jax, jax.numpy as jnp
        import numpy as np
        B, S, D, E, K = (4, 512, 256, 8, 2)
        batch, seq, dim = x.shape
        T = batch * seq
        x_flat = x.reshape(T, dim)
        logits = x_flat @ gate_w.T
        weights, indices = jax.lax.top_k(logits, K)
        weights = jax.nn.softmax(weights, axis=-1)
        combine = jnp.zeros((T, E), dtype=x.dtype).at[jnp.arange(T)[:, None], indices].add(weights)
        out = jnp.zeros((T, dim), dtype=x.dtype)
        for e in range(E):
            out = out + combine[:, e:e + 1] * (x_flat @ expert_w[e].T)
        return out.reshape(batch, seq, dim)

    def _gn(v, G=32, eps=1e-05):
        B_, C_, H_, W_ = v.shape
        g = v.reshape(B_, G, C_ // G, H_, W_)
        m = jnp.mean(g, axis=(2, 3, 4), keepdims=True)
        s = jnp.var(g, axis=(2, 3, 4), keepdims=True)
        return ((g - m) / jnp.sqrt(s + eps)).reshape(v.shape)

    def _ln_c(v, eps=1e-06):
        m = jnp.mean(v, axis=1, keepdims=True)
        s = jnp.var(v, axis=1, keepdims=True)
        return (v - m) / jnp.sqrt(s + eps)

    def _ln_t(v, eps=1e-05):
        m = jnp.mean(v, axis=-1, keepdims=True)
        s = jnp.var(v, axis=-1, keepdims=True)
        return (v - m) / jnp.sqrt(s + eps)

    def _to_tokens(v):
        B_, C_, H_, W_ = v.shape
        return v.reshape(B_, C_, H_ * W_).transpose(0, 2, 1)

    def _from_tokens(t, like):
        B_, C_, H_, W_ = like.shape
        return t.transpose(0, 2, 1).reshape(B_, C_, H_, W_)
    x = _L0_conv_ref(x, L0_conv_paddings, L0_conv_a1_wq, L0_conv_a1_bq, L0_conv_a1_wk, L0_conv_a1_bk, L0_conv_a1_wv, L0_conv_a1_bv, L0_conv_a1_wo, L0_conv_a1_bo, L0_conv_a1_bias, L0_conv_a2_wq, L0_conv_a2_bq, L0_conv_a2_wk, L0_conv_a2_bk, L0_conv_a2_wv, L0_conv_a2_bv, L0_conv_a2_wo, L0_conv_a2_bo, L0_conv_a2_bias, L0_conv_n1_w, L0_conv_n1_b, L0_conv_n2_w, L0_conv_n2_b, L0_conv_n3_w, L0_conv_n3_b, L0_conv_c1_w, L0_conv_c1_b, L0_conv_c2_w, L0_conv_c2_b, L0_conv_bn_g, L0_conv_bn_b, L0_conv_fc1_w, L0_conv_fc1_b, L0_conv_fc2_w, L0_conv_fc2_b)
    t = _to_tokens(x)
    t = t + _L1_attn_ref(_ln_t(t), L1_attn_w_qkv, L1_attn_w_out)
    t = t + _L1_ffn_ref(_ln_t(t), L1_ffn_gate_w, L1_ffn_expert_w)
    x = _from_tokens(t, x)
    return x

_drawn_inputs = setup_inputs


def setup_inputs(seed=0):
    import zlib

    import numpy as np

    out = dict(_drawn_inputs(seed))
    spreads = {'L0_conv_a1_bq': (0.0, 1.022),
     'L0_conv_a1_bk': (0.0, 2.0),
     'L0_conv_a1_bv': (0.0, 0.1),
     'L0_conv_a1_bo': (0.0, 0.1),
     'L0_conv_a2_bq': (0.0, 0.3),
     'L0_conv_a2_bk': (0.0, 2.0),
     'L0_conv_a2_bv': (0.0, 0.1),
     'L0_conv_a2_bo': (0.0, 0.1),
     'L0_conv_n1_w': (1.0, 0.2),
     'L0_conv_n1_b': (0.0, 0.1),
     'L0_conv_n2_w': (1.0, 0.2),
     'L0_conv_n2_b': (0.0, 0.1),
     'L0_conv_n3_w': (1.0, 0.2),
     'L0_conv_n3_b': (0.0, 0.1),
     'L0_conv_c1_b': (0.0, 0.1),
     'L0_conv_c2_b': (0.0, 2.0),
     'L0_conv_bn_g': (1.0, 0.2),
     'L0_conv_bn_b': (0.0, 0.1),
     'L0_conv_fc1_b': (0.0, 0.1),
     'L0_conv_fc2_b': (0.0, 0.1)}
    factors = {'L0_conv_a1_bias': 3.128, 'L0_conv_a2_bias': 9.658}
    for name, (base, spread) in spreads.items():
        noise = np.random.default_rng([zlib.crc32(name.encode()), seed]).standard_normal(out[name].shape)
        drawn = base * np.exp(spread * noise) if base else spread * noise
        out[name] = jnp.asarray(drawn.astype(out[name].dtype))
    for name, factor in factors.items():
        out[name] = (out[name] * factor).astype(out[name].dtype)
    return out
```

```python
import math
from contextlib import ExitStack

import concourse.bass as bass
import numpy as np
from concourse import mybir

B, C, HW = 8, 256, 16
TOK = HW * HW
P = 128
HALVES = C // P
TILES = TOK // P
WS = 8
WTOK = WS * WS
NH, HD = 8, 32
HID = 512
L1H, L1D = 16, 16
EXPERTS = 8
PAD = HW + 2
TAPS = 9
GROUPS, GH = 4, 4
S = 256.0
YS = 16.0
EPS = 1e-5
BANK = 512
ITERS = B // 2

VEC = {}
for _name, _n in (("bqk", 8), ("nw", 4), ("nb", 4), ("bv", 4), ("bo", 4), ("c1b", 2), ("c2b", 2), ("bng", 2),
                  ("bnb", 2), ("n3w", 2), ("n3b", 2), ("fc1b", 4)):
    VEC[_name] = (sum(n for _, n in VEC.values()), _n)
NVEC = sum(n for _, n in VEC.values())
CST = {}
for _name, _n in (("ident", P), ("dct", P), ("idct", P), ("dcsum", WTOK), ("causal", P), ("before", 64),
                  ("cos", TOK), ("sin", 2 * TOK)):
    CST[_name] = (sum(n for _, n in CST.values()), _n)
NCST = sum(n for _, n in CST.values())
W_FIRST = {"wqk": 4 * 2 * C, "wv": 2 * 2 * C, "wconv": TAPS * 2 * C}
W_SECOND = {"wfc1": 2 * HID, "wfc2": 4 * C, "wqkv": 3 * 2 * C, "wout": 2 * C, "wgate": 2 * EXPERTS,
            "wexp": EXPERTS * 2 * C}
CHUNK = 1024
STAGES = 4


def build(nc, a, out):
    f32, f16, bf16 = mybir.dt.float32, mybir.dt.float16, mybir.dt.bfloat16
    ALU, ACT, AX = mybir.AluOpType, mybir.ActivationFunctionType, mybir.AxisListType.X
    ds = bass.ds
    scratch = nc.dram_tensor("rope_scratch", [2, 2, 4, P, TOK], f16, kind="Internal").ap()

    keep = ExitStack()
    with keep:
        def sb(stack, name, shape, dt=f32):
            return stack.enter_context(nc.sbuf_tensor(name, shape, dt))

        in_use = []

        def sem(name):
            in_use.append(nc.alloc_semaphore(name=name))
            return in_use[-1]

        def sems(name):
            return [sem(f"{name}{p}") for p in range(2)]

        def release_sems():
            nc.clear_and_free_semaphores(list(in_use))
            in_use.clear()
            nc.all_engine_barrier()

        vec = sb(keep, "vec", [P, NVEC])
        cst = sb(keep, "cst", [P, NCST])
        sbqk = sb(keep, "sbqk", [P, 8])
        identb = sb(keep, "identb", [P, P], bf16)
        maskb = sb(keep, "maskb", [P, 2 * P], bf16)
        fc2b = sb(keep, "fc2b", [P, C])
        z = sb(keep, "z", [P, HALVES, B * TOK])
        zst = sb(keep, "zst", [P, HALVES, B, 6])
        small = sb(keep, "small", [P, 64])
        hi, lo = {}, {}
        for name, n in W_SECOND.items():
            hi[name], lo[name] = sb(keep, name + "h", [P, n], f16), sb(keep, name + "l", [P, n], f16)
        psum = [keep.enter_context(nc.psum_tensor(f"ps{p}", [P, 4 * BANK], f32)) for p in range(2)]

        def col(name, k=0, n=1):
            return vec[:, VEC[name][0] + k:VEC[name][0] + k + n]

        def const(name):
            return cst[:, CST[name][0]:CST[name][0] + CST[name][1]]

        ident = const("ident")

        def bank(p, k, n=1):
            return psum[p][:, k * BANK:(k + n) * BANK]

        shared = dict(f32=f32, f16=f16, ALU=ALU, ACT=ACT, AX=AX, ds=ds, hi=hi, lo=lo, psum=psum, sb=sb, sem=sem, sems=sems,
                      col=col, const=const, bank=bank, ident=ident, vec=vec, cst=cst, sbqk=sbqk, identb=identb,
                      maskb=maskb, fc2b=fc2b, z=z, zst=zst, small=small, scratch=scratch)
        first = ExitStack()
        with first:
            for name, n in {**W_FIRST, "wfused": 2 * 2 * C}.items():
                hi[name], lo[name] = sb(first, name + "h", [P, n], f16), sb(first, name + "l", [P, n], f16)
            relb = sb(first, "relb", [P, 2, 4, P])
            ybias = sb(first, "ybias", [P, HALVES, WTOK])
            prepare(nc, a, {**shared, "relb": relb, "ybias": ybias})
            release_sems()
            windows(nc, a, {**shared, "relb": relb, "ybias": ybias})
            release_sems()
        images(nc, a, out, shared)


def prepare(nc, a, k):
    f32, ALU, ACT = k["f32"], k["ALU"], k["ACT"]
    hi, lo, vec, cst, small, psum, sem = k["hi"], k["lo"], k["vec"], k["cst"], k["small"], k["psum"], k["sem"]
    col, const, bank = k["col"], k["const"], k["bank"]
    relb, ybias, sbqk, identb, maskb, fc2b = (k[n] for n in ("relb", "ybias", "sbqk", "identb", "maskb", "fc2b"))

    chunks = []
    for name, n in {**W_FIRST, **W_SECOND}.items():
        for c0 in range(0, n, CHUNK):
            chunks.append((name, c0, min(CHUNK, n - c0)))

    with ExitStack() as own:
        stage = [k["sb"](own, f"stage{s}", [P, CHUNK]) for s in range(STAGES)]
        wo = k["sb"](own, "wo", [P, 2, 2, C])
        c1 = k["sb"](own, "c1", [P, 2, 2, C])
        wf = k["sb"](own, "wf", [P, 2, 2, C])
        chunk_loaded = [sem(f"chunk_loaded{s}") for s in range(STAGES)]
        vec_loaded, cst_loaded, wo_loaded, tiles_loaded = (sem(n) for n in
                                                           ("vec_loaded", "cst_loaded", "wo_loaded", "tiles_loaded"))
        chunk_hi, chunk_lo = sem("chunk_hi"), sem("chunk_lo")
        fused_done, wf_ready, wf_hi, fold_done, const_step = (sem(n) for n in
                                                              ("fused_done", "wf_ready", "wf_hi", "fold_done",
                                                               "const_step"))
        block = own.enter_context(nc.Block())

        @block.sync
        def _(sp):
            sp.dma_start(vec[:], a["vec"]).then_inc(vec_loaded, 16)
            sp.dma_start(wo[:], a["wo"]).then_inc(wo_loaded, 16)
            sp.dma_start(c1[:], a["c1"]).then_inc(wo_loaded, 16)
            sp.dma_start(cst[:], a["cst"]).then_inc(cst_loaded, 16)
            for n, (name, c0, w) in enumerate(chunks):
                if n >= STAGES:
                    sp.wait_ge(chunk_lo, n - STAGES + 1)
                sp.dma_start(stage[n % STAGES][:, :w], a[name][:, c0:c0 + w]).then_inc(chunk_loaded[n % STAGES], 16)
            sp.dma_start(relb[:], a["relb"]).then_inc(tiles_loaded, 16)
            sp.dma_start(fc2b[:], a["fc2b"]).then_inc(tiles_loaded, 16)
            sp.wait_ge(tiles_loaded, 32)

        @block.tensor
        def _(pe):
            pe.wait_ge(wo_loaded, 32)
            for at in range(2):
                for ih in range(HALVES):
                    for jh in range(HALVES):
                        last = nc.tensor.matmul(bank(0, at)[:, ih * C:(ih + 1) * C],
                                                wo[:, at, jh, ih * P:(ih + 1) * P], c1[:, at, jh, :],
                                                start=jh == 0, stop=jh == HALVES - 1)
                last.then_inc(fused_done, 1)
            pe.wait_ge(wf_ready, 2)
            pe.wait_ge(vec_loaded, 16)
            for at in range(2):
                for oh in range(HALVES):
                    o = slice(oh * P, (oh + 1) * P)
                    for n, (w, v) in enumerate([(wf, "bv"), (c1, "bo")]):
                        for h in range(HALVES):
                            last = nc.tensor.matmul(bank(0, 2)[:, at * 2 + oh:at * 2 + oh + 1], w[:, at, h, o],
                                                    col(v, at * 2 + h), start=(n, h) == (0, 0), stop=(n, h) == (1, 1))
            last.then_inc(fold_done, 1)

        @block.scalar
        def _(act):
            act.wait_ge(vec_loaded, 16)
            nc.scalar.activation(sbqk[:], col("bqk", 0, 8), ACT.Copy, scale=S).then_inc(const_step, 1)
            for at in range(2):
                act.wait_ge(fused_done, at + 1)
                nc.scalar.activation(wf[:, at], bank(0, at).rearrange("p (h o) -> p h o", h=HALVES),
                                     ACT.Copy).then_inc(wf_ready, 1)
            act.wait_ge(wf_ready, 2)
            nc.scalar.activation(hi["wfused"][:], wf[:].rearrange("p a h o -> p (a h o)"), ACT.Copy,
                                 scale=S).then_inc(wf_hi, 1)
            for n, (name, c0, w) in enumerate(chunks):
                act.wait_ge(chunk_loaded[n % STAGES], 16 * (n // STAGES + 1))
                nc.scalar.activation(hi[name][:, c0:c0 + w], stage[n % STAGES][:, :w], ACT.Copy,
                                     scale=S).then_inc(chunk_hi, 1)

        @block.vector
        def _(dve):
            dve.wait_ge(wf_hi, 1)
            nc.vector.scalar_tensor_tensor(lo["wfused"][:], wf[:].rearrange("p a h o -> p (a h o)"), S,
                                           hi["wfused"][:], ALU.mult, ALU.subtract)
            dve.wait_ge(fold_done, 1)
            fold = small[:, 0:4]
            nc.vector.tensor_scalar(fold, bank(0, 2)[:, 0:4], YS, None, ALU.mult).then_inc(const_step, 1)
            dve.wait_ge(const_step, 2)
            nc.vector.scalar_tensor_tensor(small[:, 4:6], col("c1b", 0, 2), YS, small[:, 2:4], ALU.mult,
                                           ALU.add).then_inc(const_step, 1)
            dve.wait_ge(const_step, 3)
            dve.wait_ge(cst_loaded, 16)
            for oh in range(HALVES):
                nc.vector.tensor_scalar(ybias[:, oh, :], const("dcsum"), small[:, oh:oh + 1],
                                        small[:, 4 + oh:5 + oh], ALU.mult, ALU.add)
            nc.vector.tensor_copy(identb[:], const("ident"))
            nc.vector.memset(maskb[:, 0:P], 0.0)
            nc.vector.tensor_copy(maskb[:, P:2 * P], const("causal"))
            for n, (name, c0, w) in enumerate(chunks):
                dve.wait_ge(chunk_hi, n + 1)
                nc.vector.scalar_tensor_tensor(lo[name][:, c0:c0 + w], stage[n % STAGES][:, :w], S,
                                               hi[name][:, c0:c0 + w], ALU.mult, ALU.subtract).then_inc(chunk_lo, 1)


def windows(nc, a, k):
    f32, f16, ALU, ACT, AX, ds = k["f32"], k["f16"], k["ALU"], k["ACT"], k["AX"], k["ds"]
    hi, lo, psum, sems, sb, sem = k["hi"], k["lo"], k["psum"], k["sems"], k["sb"], k["sem"]
    col, const, bank, ident = k["col"], k["const"], k["bank"], k["ident"]
    relb, ybias, sbqk, z, zst = (k[n] for n in ("relb", "ybias", "sbqk", "z", "zst"))
    R2 = range(2)
    SRC_Q = [0, 1, 1, 0]
    SRC_V = [1, 0]

    with ExitStack() as own:
        def pair(name, shape, dt=f32):
            return [sb(own, f"{name}{p}", shape, dt) for p in R2]

        xw = pair("xw", [P, TILES, C])
        st, mv, rstd = pair("st", [P, 4, 6]), pair("mv", [P, 4, 2]), pair("rstd", [P, 4])
        xn = pair("xn", [P, 2, TILES, C])
        xh, xl = pair("xh", [P, 2, HALVES, TOK], f16), pair("xl", [P, 2, HALVES, TOK], f16)
        qkh, qkl = pair("qkh", [P, 4, HALVES, TOK], f16), pair("qkl", [P, 4, HALVES, TOK], f16)
        vh, vl = pair("vh", [P, 2, 4, 4, HD + 1], f16), pair("vl", [P, 2, 4, 4, HD], f16)
        prob = pair("prob", [P, 4 * BANK])
        mx = pair("mx", [P, 32])
        eh, el = pair("eh", [P, 4 * BANK], f16), pair("el", [P, 4 * BANK], f16)
        rs = pair("rs", [P, 2, 2, 8])
        o = pair("o", [P, 2, TILES, C])
        och, ocl = pair("och", [P, 2 * BANK], f16), pair("ocl", [P, 2 * BANK], f16)
        y = pair("y", [P, HALVES, TOK])
        yh, yl = pair("yh", [P, HALVES, PAD, PAD], f16), pair("yl", [P, HALVES, PAD, PAD], f16)
        half, eps = sb(own, "half", [P, 4]), sb(own, "eps", [P, 4])

        (x_loaded, dct_done, stats_done, mv_done, eps_added, rstd_done, norm_done, tr_done, affine_done, xh_done,
         xl_done, qk_done, qkh_done, qkl_done, v_done, vh_done, vl_done, scores_done, biased, max_done, shifted,
         exp_done, et_done, eh_done, el_done, pv_done, recip_done, o_done, oc_done, och_done, ocl_done, y_done,
         y32_done, yh_done, yl_done, conv_done, z_done) = (
            sems(n) for n in ("x_loaded", "dct_done", "stats_done", "mv_done", "eps_added", "rstd_done", "norm_done",
                              "tr_done", "affine_done", "xh_done", "xl_done", "qk_done", "qkh_done", "qkl_done",
                              "v_done", "vh_done", "vl_done", "scores_done", "biased", "max_done", "shifted",
                              "exp_done", "et_done", "eh_done", "el_done", "pv_done", "recip_done", "o_done",
                              "oc_done", "och_done", "ocl_done", "y_done", "y32_done", "yh_done", "yl_done",
                              "conv_done", "z_done"))
        ones_set, pads_set, half_set = sem("ones_set"), sem("pads_set"), sem("half_set")

        def image(im, oh, wi):
            return im[:, oh, 1 + wi * WS:1 + (wi + 1) * WS, 1:1 + HW].rearrange("p x (j y) -> p j x y", j=2)

        def window_rows(t, oh, wi):
            return t[:, oh, wi * P:(wi + 1) * P].rearrange("p (j x y) -> p j x y", j=2, x=WS)

        def affine(p):
            return prob[p][:, 0:2 * BANK].rearrange("p (s h t) -> p s h t", s=2, h=HALVES)

        block = own.enter_context(nc.Block())

        @block.sync
        def _(sp):
            with sp.Fori(0, ITERS) as i:
                for p in R2:
                    sp.wait_ge(dct_done[p], i + 1)
                    sp.wait_ge(norm_done[p], i + 1)
                    sp.dma_start(xw[p][:], a["xw"][ds((i * 2 + p) * P, P)]).then_inc(x_loaded[p], 16)

        @block.tensor
        def _(pe):
            def split_products(out_ap, pairs, left=(0, 1, 0), right=(0, 0, 1)):
                n = len(pairs) * 3
                done = 0
                for lhs, rhs in pairs:
                    for x, w in zip(left, right):
                        last = nc.tensor.matmul(out_ap, lhs[x], rhs[w], start=done == 0, stop=done == n - 1)
                        done += 1
                return last

            for p in R2:
                pe.sem_inc(dct_done[p], 1)
            with pe.Fori(0, ITERS) as i:
                for p in R2:
                    pe.wait_ge(x_loaded[p], i * 16 + 16)
                    for t in range(TILES):
                        last = nc.tensor.matmul(bank(p, 0)[:, t * C:(t + 1) * C], const("dct"), xw[p][:, t, :],
                                                start=True, stop=True)
                    last.then_inc(dct_done[p], 1)
                for p in R2:
                    pe.wait_ge(norm_done[p], i + 2)
                    pe.wait_ge(z_done[p], i * 2 + 1)
                    for s in range(2):
                        for t in range(TILES):
                            for h in range(HALVES):
                                last = nc.tensor.transpose(bank(p, 1 + s)[:, h * TOK + t * P:h * TOK + (t + 1) * P],
                                                           xn[p][:, s, t, h * P:(h + 1) * P], ident)
                    last.then_inc(tr_done[p], 1)
                for p in R2:
                    pe.wait_ge(xl_done[p], i + 1)
                    for j in range(4):
                        for oh in range(HALVES):
                            last = split_products(
                                bank(p, j)[:, oh * TOK:(oh + 1) * TOK],
                                [([w["wqk"][:, (j * 2 + h) * C + oh * P:(j * 2 + h) * C + (oh + 1) * P]
                                   for w in (hi, lo)], [x[p][:, SRC_Q[j], h, :] for x in (xh, xl)])
                                 for h in range(HALVES)])
                        last.then_inc(qk_done[p], 1)
                for p in R2:
                    pe.wait_ge(qkl_done[p], i * 8 + 4)
                    for at in range(2):
                        for w in range(4):
                            for hh in range(2):
                                last = split_products(
                                    bank(p, at)[64 * hh:64 * hh + 64, w * P:(w + 1) * P],
                                    [([x[p][:, SRC_V[at], h, w * WTOK:(w + 1) * WTOK] for x in (xh, xl)],
                                      [wt["wv"][:, (at * 2 + h) * C + hh * P:(at * 2 + h) * C + (hh + 1) * P]
                                       for wt in (hi, lo)]) for h in range(HALVES)])
                        last.then_inc(v_done[p], 1)
                for p in R2:
                    pe.wait_ge(vl_done[p], i * 2 + 2)
                    pe.wait_ge(qkl_done[p], i * 8 + 8)
                    for at in range(2):
                        for t in range(TILES):
                            for w in range(2):
                                tok = slice(t * P + w * WTOK, t * P + (w + 1) * WTOK)
                                for hh in range(2):
                                    c0 = (at * 2 + t) * P + hh * WTOK
                                    for n, (q, kk) in enumerate([(qkh, qkh), (qkl, qkh), (qkh, qkl)]):
                                        for r in range(4):
                                            rows = slice(32 * r, 32 * r + 32)
                                            last = nc.tensor.matmul(
                                                bank(p, r)[64 * w:64 * w + 64, c0:c0 + WTOK],
                                                q[p][rows, at * 2, hh, tok], kk[p][rows, at * 2 + 1, hh, tok],
                                                start=n == 0, stop=n == 2)
                    last.then_inc(scores_done[p], 1)
                for p in R2:
                    pe.wait_ge(biased[p], i * 4 + 4)
                    for at in range(2):
                        pe.wait_ge(exp_done[p], i * 2 + at + 1)
                        for t in range(TILES):
                            for r in range(4):
                                c0 = (at * 2 + t) * BANK + r * P
                                last = nc.tensor.transpose(psum[p][:, c0:c0 + P], prob[p][:, c0:c0 + P], ident)
                            last.then_inc(et_done[p], 1)
                for p in R2:
                    pe.wait_ge(half_set, 1)
                    pe.wait_ge(el_done[p], i * 4 + 4)
                    for at in range(2):
                        for w in range(4):
                            t, wj = divmod(w, 2)
                            for r in range(4):
                                for n, (e, v, width) in enumerate([(eh, vh, HD + 1), (eh, vl, HD), (el, vh, HD + 1)]):
                                    for hh in range(2):
                                        rows = slice(64 * hh, 64 * hh + 64)
                                        c0 = (at * 2 + t) * BANK + r * P + wj * WTOK
                                        d0 = (t * 4 + r) * (HD + 1)
                                        last = nc.tensor.matmul(
                                            bank(p, at * 2 + hh)[64 * wj:64 * wj + 64, d0:d0 + width],
                                            e[p][rows, c0:c0 + WTOK], v[p][rows, at, w, r, 0:width],
                                            start=n == 0, stop=n == 2)
                        last.then_inc(pv_done[p], 1)
                for p in R2:
                    pe.wait_ge(o_done[p], i * 4 + 4)
                    for h in range(HALVES):
                        for t in range(TILES):
                            nc.tensor.matmul(bank(p, 0)[:, h * TOK + t * P:h * TOK + (t + 1) * P],
                                             o[p][:, 0, t, h * P:(h + 1) * P], const("idct"), start=True, stop=True)
                    for h in range(HALVES):
                        for t in range(TILES):
                            last = nc.tensor.transpose(bank(p, 1)[:, h * TOK + t * P:h * TOK + (t + 1) * P],
                                                       o[p][:, 1, t, h * P:(h + 1) * P], ident)
                    last.then_inc(oc_done[p], 1)
                for p in R2:
                    pe.wait_ge(ocl_done[p], i + 1)
                    for oh in range(HALVES):
                        last = split_products(
                            bank(p, 2)[:, oh * TOK:(oh + 1) * TOK],
                            [([w["wfused"][:, n * C + oh * P:n * C + (oh + 1) * P] for w in (hi, lo)],
                              [x[p][:, n * TOK:(n + 1) * TOK] for x in (och, ocl)]) for n in range(4)])
                    last.then_inc(y_done[p], 1)
                for p in R2:
                    pe.wait_ge(yl_done[p], i * 4 + 4)
                    for oh in range(HALVES):
                        prods = []
                        for tap in range(TAPS):
                            dy, dx = divmod(tap, 3)
                            for h in range(HALVES):
                                c0 = (tap * 2 + h) * C + oh * P
                                prods.append(([w["wconv"][:, c0:c0 + P] for w in (hi, lo)],
                                              [im[p][:, h, dy:dy + HW, dx:dx + HW] for im in (yh, yl)]))
                        last = split_products(bank(p, 2 + oh)[:, 0:TOK], prods)
                        last.then_inc(conv_done[p], 1)

        @block.scalar
        def _(act):
            for p in R2:
                act.sem_inc(z_done[p], 1)
            with act.Fori(0, ITERS) as i:
                for p in R2:
                    act.wait_ge(tr_done[p], i + 1)
                    for s in range(2):
                        for h in range(HALVES):
                            nc.scalar.activation(affine(p)[:, s, h, :], bank(p, 1 + s)[:, h * TOK:(h + 1) * TOK],
                                                 ACT.Identity, scale=col("nw", s * 2 + h),
                                                 bias=col("nb", s * 2 + h)).then_inc(affine_done[p], 1)
                for p in R2:
                    act.wait_ge(affine_done[p], i * 4 + 4)
                    nc.scalar.activation(xh[p][:], affine(p), ACT.Copy).then_inc(xh_done[p], 1)
                for p in R2:
                    for j in range(4):
                        act.wait_ge(qk_done[p], i * 4 + j + 1)
                        for oh in range(HALVES):
                            nc.scalar.activation(qkh[p][:, j, oh, :], bank(p, j)[:, oh * TOK:(oh + 1) * TOK],
                                                 ACT.Identity,
                                                 bias=sbqk[:, j * 2 + oh:j * 2 + oh + 1]).then_inc(qkh_done[p], 1)
                for p in R2:
                    for at in range(2):
                        act.wait_ge(v_done[p], i * 2 + at + 1)
                        nc.scalar.activation(vh[p][:, at, :, :, 0:HD],
                                             bank(p, at).rearrange("p (w r d) -> p w r d", w=4, r=4),
                                             ACT.Copy).then_inc(vh_done[p], 1)
                for p in R2:
                    for at in range(2):
                        act.wait_ge(shifted[p], i * 2 + at + 1)
                        e = prob[p][:, at * 2 * BANK:(at + 1) * 2 * BANK]
                        nc.scalar.activation(e, e, ACT.Exp).then_inc(exp_done[p], 1)
                for p in R2:
                    for n in range(4):
                        act.wait_ge(et_done[p], i * 4 + n + 1)
                        nc.scalar.activation(eh[p][:, n * BANK:(n + 1) * BANK], bank(p, n),
                                             ACT.Copy).then_inc(eh_done[p], 1)
                for p in R2:
                    act.wait_ge(oc_done[p], i + 1)
                    nc.scalar.activation(och[p][:], bank(p, 0, 2), ACT.Copy).then_inc(och_done[p], 1)
                for p in R2:
                    act.wait_ge(y32_done[p], i * 2 + 2)
                    for oh in range(HALVES):
                        for wi in range(2):
                            nc.scalar.activation(image(yh[p], oh, wi), window_rows(y[p], oh, wi),
                                                 ACT.Copy).then_inc(yh_done[p], 1)
                for p in R2:
                    for oh in range(HALVES):
                        act.wait_ge(conv_done[p], i * 2 + oh + 1)
                        nc.scalar.activation(z[:, oh, ds((i * 2 + p) * TOK, TOK)],
                                             bank(p, 2 + oh)[:, 0:TOK], ACT.Identity,
                                             scale=1.0 / (S * YS), bias=col("c2b", oh)).then_inc(z_done[p], 1)

        @block.gpsimd
        def _(pool):
            for p in R2:
                nc.gpsimd.memset(yh[p][:], 0.0).then_inc(pads_set, 1)
                nc.gpsimd.memset(yl[p][:], 0.0).then_inc(pads_set, 1)
                nc.gpsimd.memset(vh[p][:], 1.0).then_inc(ones_set, 1)
            nc.gpsimd.memset(half[:], -0.5).then_inc(half_set, 1)
            nc.gpsimd.memset(eps[:], EPS).then_inc(half_set, 1)
            pool.wait_ge(half_set, 2)
            with pool.Fori(0, ITERS) as i:
                for p in R2:
                    pool.wait_ge(mv_done[p], i + 1)
                    nc.gpsimd.tensor_tensor(rstd[p][:], mv[p][:, :, 1], eps[:], ALU.add).then_inc(eps_added[p], 1)
                    pool.wait_ge(eps_added[p], i + 1)
                    nc.gpsimd.tensor_tensor(rstd[p][:], rstd[p][:], half[:], ALU.pow).then_inc(rstd_done[p], 1)

        @block.vector
        def _(dve):
            dve.wait_ge(ones_set, 2)
            dve.wait_ge(pads_set, 4)
            for p in R2:
                dve.sem_inc(norm_done[p], 1)
                dve.sem_inc(stats_done[p], 1)
            with dve.Fori(0, ITERS) as i:
                def tokens(p, s, t):
                    return xw[p][:, t, :] if s == 0 else bank(p, 0)[:, t * C:(t + 1) * C]

                for p in R2:
                    dve.wait_ge(x_loaded[p], i * 16 + 16)
                    for s in range(2):
                        if s:
                            dve.wait_ge(dct_done[p], i + 2)
                        for t in range(TILES):
                            last = nc.vector.bn_stats(st[p][:, s * 2 + t, :], tokens(p, s, t))
                    last.then_inc(stats_done[p], 1)
                    dve.wait_ge(half_set, 1)
                    dve.wait_ge(stats_done[p], i + 2)
                    for n in range(4):
                        last = nc.vector.bn_aggr(mv[p][:, n, :], st[p][:, n, :])
                    last.then_inc(mv_done[p], 1)
                for p in R2:
                    dve.wait_ge(rstd_done[p], i + 1)
                    for s in range(2):
                        for t in range(TILES):
                            n = s * 2 + t
                            last = nc.vector.tensor_scalar(xn[p][:, s, t, :], tokens(p, s, t), mv[p][:, n, 0:1],
                                                           rstd[p][:, n:n + 1], ALU.subtract, ALU.mult)
                    last.then_inc(norm_done[p], 1)
                for p in R2:
                    dve.wait_ge(xh_done[p], i + 1)
                    nc.vector.tensor_tensor(xl[p][:], affine(p), xh[p][:], ALU.subtract).then_inc(xl_done[p], 1)
                for p in R2:
                    for j in range(4):
                        for oh in range(HALVES):
                            n = j * 2 + oh
                            if oh == 0:
                                dve.wait_ge(qkh_done[p], i * 8 + n + 2)
                            nc.vector.scalar_tensor_tensor(qkl[p][:, j, oh, :], bank(p, j)[:, oh * TOK:(oh + 1) * TOK],
                                                           sbqk[:, n:n + 1], qkh[p][:, j, oh, :], ALU.add,
                                                           ALU.subtract).then_inc(qkl_done[p], 1)
                for p in R2:
                    for at in range(2):
                        dve.wait_ge(vh_done[p], i * 2 + at + 1)
                        nc.vector.tensor_tensor(vl[p][:, at], bank(p, at).rearrange("p (w r d) -> p w r d", w=4, r=4),
                                                vh[p][:, at, :, :, 0:HD], ALU.subtract).then_inc(vl_done[p], 1)
                for p in R2:
                    banks = psum[p][:].rearrange("p (r c) -> p r c", r=4)
                    dve.wait_ge(scores_done[p], i + 1)
                    for n in range(4):
                        nc.vector.scalar_tensor_tensor(
                            prob[p][:, n * BANK:(n + 1) * BANK].rearrange("p (r c) -> p r c", r=4),
                            banks[:, :, n * P:(n + 1) * P], HD ** -0.5 / (S * S), relb[:, n // 2], ALU.mult,
                            ALU.add).then_inc(biased[p], 1)
                    rows = prob[p][:].rearrange("p (a g m) -> p a g m", a=2, m=WTOK)
                    for at in range(2):
                        dve.wait_ge(biased[p], i * 4 + at * 2 + 2)
                        nc.vector.tensor_reduce(mx[p][:, at * 16:(at + 1) * 16], rows[:, at], op=ALU.max,
                                                axis=AX).then_inc(max_done[p], 1)
                    for at in range(2):
                        dve.wait_ge(max_done[p], i * 2 + at + 1)
                        nc.vector.tensor_tensor(rows[:, at], rows[:, at],
                                                mx[p][:, at * 16:(at + 1) * 16].unsqueeze(2).to_broadcast([P, 16, WTOK]),
                                                ALU.subtract).then_inc(shifted[p], 1)
                for p in R2:
                    for n in range(4):
                        dve.wait_ge(eh_done[p], i * 4 + n + 1)
                        nc.vector.tensor_tensor(el[p][:, n * BANK:(n + 1) * BANK], bank(p, n),
                                                eh[p][:, n * BANK:(n + 1) * BANK],
                                                ALU.subtract).then_inc(el_done[p], 1)
                for p in R2:
                    for at in range(2):
                        dve.wait_ge(pv_done[p], i * 2 + at + 1)
                        pv = bank(p, at * 2, 2).rearrange("p (h c) -> p h c", h=2)[:, :, 0:8 * (HD + 1)]
                        pv = pv.rearrange("p h (g d) -> p h g d", d=HD + 1)
                        nc.vector.reciprocal(rs[p][:, at], pv[:, :, :, HD]).then_inc(recip_done[p], 1)
                        dve.wait_ge(recip_done[p], i * 2 + at + 1)
                        for hh in range(2):
                            nc.vector.tensor_tensor(
                                o[p][:, at, :, hh * P:(hh + 1) * P].rearrange("p t (r d) -> p t r d", r=4),
                                pv[:, hh, :, 0:HD].rearrange("p (t r) d -> p t r d", t=2),
                                rs[p][:, at, hh, :].rearrange("p (t r) -> p t r", t=2).unsqueeze(3)
                                .to_broadcast([P, 2, 4, HD]), ALU.mult).then_inc(o_done[p], 1)
                for p in R2:
                    dve.wait_ge(och_done[p], i + 1)
                    nc.vector.tensor_tensor(ocl[p][:], bank(p, 0, 2), och[p][:], ALU.subtract).then_inc(ocl_done[p], 1)
                for p in R2:
                    dve.wait_ge(y_done[p], i + 1)
                    for oh in range(HALVES):
                        nc.vector.scalar_tensor_tensor(
                            y[p][:, oh, :].rearrange("p (w t) -> p w t", w=4),
                            bank(p, 2)[:, oh * TOK:(oh + 1) * TOK].rearrange("p (w t) -> p w t", w=4), YS / (S * S),
                            ybias[:, oh, :].unsqueeze(1).to_broadcast([P, 4, WTOK]), ALU.mult,
                            ALU.add).then_inc(y32_done[p], 1)
                    for oh in range(HALVES):
                        for wi in range(2):
                            dve.wait_ge(yh_done[p], i * 4 + oh * 2 + wi + 1)
                            nc.vector.tensor_tensor(image(yl[p], oh, wi), window_rows(y[p], oh, wi),
                                                    image(yh[p], oh, wi), ALU.subtract).then_inc(yl_done[p], 1)
                for p in R2:
                    for oh in range(HALVES):
                        dve.wait_ge(z_done[p], i * 2 + oh + 2)
                        nc.vector.bn_stats(zst[:, oh, ds(i * 2 + p, 1), :], z[:, oh, ds((i * 2 + p) * TOK, TOK)])


def images(nc, a, out, k):
    f32, f16, ALU, ACT, AX, ds = k["f32"], k["f16"], k["ALU"], k["ACT"], k["AX"], k["ds"]
    hi, lo, psum, sems, sb, sem = k["hi"], k["lo"], k["psum"], k["sems"], k["sb"], k["sem"]
    col, const, bank, ident = k["col"], k["const"], k["bank"], k["ident"]
    z, zst, small, identb, maskb, fc2b, scratch = (k[n] for n in ("z", "zst", "small", "identb", "maskb", "fc2b",
                                                                   "scratch"))
    R2 = range(2)
    KSTACK = 3 * L1D
    GW = 3 * GH * P
    D1 = L1D + 1

    with ExitStack() as own:
        def pair(name, shape, dt=f32):
            return [sb(own, f"{name}{p}", shape, dt) for p in R2]

        xc = pair("xc", [P, HALVES, TOK])
        relu = pair("relu", [P, HALVES, TOK])
        t1 = pair("t1", [P, TILES, C])
        t2 = pair("t2", [P, TILES, C])
        acc = pair("acc", [P, TILES, C])
        tn = pair("tn", [P, TILES, C])
        wide = pair("wide", [P, 4, TOK])
        rot = pair("rot", [P, 4, TOK])
        ch, cl = pair("ch", [P, HALVES, TOK], f16), pair("cl", [P, HALVES, TOK], f16)
        hh_, hl_ = pair("hh", [P, 4, TOK], f16), pair("hl", [P, 4, TOK], f16)
        qs, ks = pair("qs", [KSTACK, L1H, TOK], f16), pair("ks", [KSTACK, L1H, TOK], f16)
        vh, vl = pair("v2h", [P, TILES, L1H, D1], f16), pair("v2l", [P, TILES, L1H, L1D], f16)
        prob = pair("prob2", [P, GW])
        eh, el = pair("e2h", [P, GW], f16), pair("e2l", [P, GW], f16)
        st, mv, rstd = pair("st2", [P, 2, 6]), pair("mv2", [P, 2, 2]), pair("rstd2", [P, 2])
        mx, rs = pair("mx2", [P, 2 * GH]), pair("rs2", [P, 2 * GH])
        lg, gate = pair("lg", [P, TILES, EXPERTS]), pair("gate", [P, TILES, EXPERTS])
        cmp, eq = pair("cmp", [P, TILES, EXPERTS * EXPERTS]), pair("eq", [P, TILES, EXPERTS * EXPERTS])
        rank, g1 = pair("rank", [P, TILES, EXPERTS]), pair("g1", [P, 2 * TILES])
        half, eps = sb(own, "half2", [P, 4]), sb(own, "eps2", [P, 4])
        bn = sb(own, "bn", [P, HALVES, 6])

        names = ("xc_loaded", "relu_done", "t0_done", "t0_tr", "t1_done", "fc2_base", "affine2", "mlp_hi", "mlp_lo",
                 "fc1_done", "gelu_done", "hid_hi", "hid_lo", "fc2_done", "t2_done", "n2_hi", "n2_lo", "qk2_done",
                 "v2_done", "v2_hi", "v2_lo", "rope_a", "rope_b", "rot_done", "rot_hi", "rot_lo", "spilled",
                 "stacked", "scores2", "max2", "shift2", "exp2", "et2", "e2_hi", "e2_lo", "pv2", "recip2", "o2_done",
                 "o2_tr", "o2_hi", "o2_lo", "out_done", "t3_done", "n3_hi", "n3_lo", "logits", "gate_step",
                 "gate_max", "gate_exp", "expert_done", "acc_done", "stored")
        g = {n: sems(n) for n in names}
        ln = {n: sems(f"ln_{n}") for n in ("mv", "eps", "rstd", "norm", "tr")}
        ln_stats = [sems(f"ln_stats{m}_") for m in range(3)]
        bn_step, half_set, ones_set = sem("bn_step"), sem("half_set2"), sem("ones_set2")


        block = own.enter_context(nc.Block())

        @block.sync
        def _(sp):
            with sp.Fori(0, ITERS) as i:
                for p in R2:
                    sp.wait_ge(g["t0_tr"][p], i + 1)
                    sp.dma_start(xc[p][:], a["xc"][ds((i * 2 + p) * P, P)]).then_inc(g["xc_loaded"][p], 16)
                for p in R2:
                    for n, part in enumerate((hh_, hl_)):
                        sp.wait_ge(g["rot_hi" if n == 0 else "rot_lo"][p], i + 1)
                        if n == 0:
                            sp.wait_ge(g["scores2"][p], i * GROUPS + 1)
                        sp.dma_start(scratch[p, n].rearrange("j c t -> c j t"), part[p][:]).then_inc(g["spilled"][p], 16)
                    sp.wait_ge(g["spilled"][p], i * 32 + 32)
                    for qk, dst, parts in ((0, qs, (0, 1, 0)), (1, ks, (0, 0, 1))):
                        for n, part in enumerate(parts):
                            for j in range(2):
                                src = scratch[p, part, qk * 2 + j].rearrange("(h d) t -> d h t", h=L1H)
                                r0 = n * L1D + j * 8
                                sp.dma_start(dst[p][r0:r0 + 8], src).then_inc(g["stacked"][p], 16)
                for p in R2:
                    sp.wait_ge(g["acc_done"][p], i * 16 + 17)
                    sp.dma_start(out[ds((i * 2 + p) * P, P)], acc[p][:]).then_inc(g["stored"][p], 16)
            for p in R2:
                sp.wait_ge(g["stored"][p], ITERS * 16)

        @block.tensor
        def _(pe):
            def split_products(out_ap, pairs):
                n, done = len(pairs) * 3, 0
                for lhs, rhs in pairs:
                    for x, w in ((0, 0), (1, 0), (0, 1)):
                        last = nc.tensor.matmul(out_ap, lhs[x], rhs[w], start=done == 0, stop=done == n - 1)
                        done += 1
                return last

            def to_channels(p, k, src):
                for t in range(TILES):
                    for h in range(HALVES):
                        last = nc.tensor.transpose(bank(p, k)[:, h * TOK + t * P:h * TOK + (t + 1) * P],
                                                   src[p][:, t, h * P:(h + 1) * P], ident)
                return last

            for p in R2:
                pe.sem_inc(g["t0_tr"][p], 1)
                pe.sem_inc(g["scores2"][p], 1)
            with pe.Fori(0, ITERS) as i:
                for p in R2:
                    pe.wait_ge(g["t0_done"][p], i + 1)
                    for t in range(TILES):
                        for h in range(HALVES):
                            last = nc.tensor.transpose(bank(p, 0)[:, t * C + h * P:t * C + (h + 1) * P],
                                                       xc[p][:, h, t * P:(t + 1) * P], ident)
                    last.then_inc(g["t0_tr"][p], 1)
                for p in R2:
                    pe.wait_ge(ln["norm"][p], i * 6 + 2)
                    to_channels(p, 1, tn).then_inc(ln["tr"][p], 1)
                for p in R2:
                    pe.wait_ge(g["mlp_lo"][p], i + 1)
                    pe.wait_ge(g["acc_done"][p], i * 16 + 1)
                    for m in range(4):
                        last = split_products(
                            bank(p, 2, 2)[:, m * TOK:(m + 1) * TOK],
                            [([w["wfc1"][:, h * HID + m * P:h * HID + (m + 1) * P] for w in (hi, lo)],
                              [x[p][:, h, :] for x in (ch, cl)]) for h in range(HALVES)])
                        if m % 2:
                            last.then_inc(g["fc1_done"][p], 1)
                for p in R2:
                    pe.wait_ge(g["hid_lo"][p], i + 1)
                    for t in range(TILES):
                        last = split_products(
                            bank(p, 0)[:, t * C:(t + 1) * C],
                            [([x[p][:, m, t * P:(t + 1) * P] for x in (hh_, hl_)],
                              [w["wfc2"][:, m * C:(m + 1) * C] for w in (hi, lo)]) for m in range(4)])
                    last.then_inc(g["fc2_done"][p], 1)
                for p in R2:
                    pe.wait_ge(ln["norm"][p], i * 6 + 4)
                    to_channels(p, 1, tn).then_inc(ln["tr"][p], 1)
                for p in R2:
                    pe.wait_ge(g["n2_lo"][p], i + 1)
                    pe.wait_ge(g["gelu_done"][p], i * 4 + 4)
                    pe.wait_ge(g["t2_done"][p], i + 1)
                    for j in range(2):
                        for m in range(HALVES):
                            last = split_products(
                                bank(p, 2 + j)[:, m * TOK:(m + 1) * TOK],
                                [([w["wqkv"][:, (j * 2 + h) * C + m * P:(j * 2 + h) * C + (m + 1) * P]
                                   for w in (hi, lo)], [x[p][:, h, :] for x in (ch, cl)]) for h in range(HALVES)])
                        last.then_inc(g["qk2_done"][p], 1)
                    for t in range(TILES):
                        last = split_products(
                            bank(p, 0)[:, t * C:(t + 1) * C],
                            [([x[p][:, h, t * P:(t + 1) * P] for x in (ch, cl)],
                              [w["wqkv"][:, (4 + h) * C:(5 + h) * C] for w in (hi, lo)]) for h in range(HALVES)])
                    last.then_inc(g["v2_done"][p], 1)
                for gr in range(GROUPS):
                    for p in R2:
                        if gr == 0:
                            pe.wait_ge(g["stacked"][p], (i + 1) * 12 * 16)
                            pe.wait_ge(g["v2_lo"][p], i + 1)
                            pe.wait_ge(g["rope_b"][p], i * 4 + 4)
                        else:
                            pe.wait_ge(g["e2_lo"][p], i * GROUPS + gr)
                        causal = maskb[:, P:2 * P].unsqueeze(1).to_broadcast([P, GH, P])
                        nc.tensor.matmul(bank(p, 0).rearrange("p (h m) -> p h m", h=GH), identb[:], causal,
                                         start=True, stop=False)
                        for b in (1, 2):
                            nc.tensor.matmul(bank(p, b).rearrange("p (h m) -> p h m", h=2), identb[:],
                                             maskb[:].unsqueeze(1).to_broadcast([P, 2, 2 * P]), start=True, stop=False)
                        for h in range(GH):
                            nc.tensor.matmul(bank(p, 0)[:, h * P:(h + 1) * P], qs[p][:, gr * GH + h, 0:P],
                                             ks[p][:, gr * GH + h, 0:P], start=False, stop=h == GH - 1)
                        for h in range(GH):
                            last = nc.tensor.matmul(bank(p, 1 + h // 2)[:, h % 2 * TOK:(h % 2 + 1) * TOK],
                                                    qs[p][:, gr * GH + h, P:2 * P], ks[p][:, gr * GH + h, :],
                                                    start=False, stop=h % 2 == 1)
                        last.then_inc(g["scores2"][p], 1)
                    for p in R2:
                        pe.wait_ge(g["exp2"][p], i * GROUPS + gr + 1)
                        for n in range(3):
                            for h in range(GH):
                                c0 = h * P if n == 0 else BANK + h * TOK + (n - 1) * P
                                last = nc.tensor.transpose(bank(p, n)[:, h * P:(h + 1) * P], prob[p][:, c0:c0 + P],
                                                           ident)
                        last.then_inc(g["et2"][p], 1)
                    for p in R2:
                        pe.wait_ge(g["e2_lo"][p], i * GROUPS + gr + 1)
                        if gr:
                            pe.wait_ge(g["o2_done"][p], i * GROUPS + gr)
                        for t in range(TILES):
                            for h in range(GH):
                                c0 = (t * GH + h) * D1
                                blocks = [(0, 0)] if t == 0 else [(1, 0), (2, 1)]
                                for n, (kind, kt) in enumerate(blocks):
                                    e0 = kind * BANK + h * P
                                    for m, (e, v, w) in enumerate(((eh, vh, D1), (eh, vl, L1D), (el, vh, D1))):
                                        last = nc.tensor.matmul(bank(p, 3)[:, c0:c0 + w], e[p][:, e0:e0 + P],
                                                                v[p][:, kt, gr * GH + h, 0:w], start=(n, m) == (0, 0),
                                                                stop=(n, m) == (len(blocks) - 1, 2))
                        last.then_inc(g["pv2"][p], 1)
                for p in R2:
                    pe.wait_ge(g["o2_done"][p], i * GROUPS + GROUPS)
                    to_channels(p, 0, acc).then_inc(g["o2_tr"][p], 1)
                for p in R2:
                    pe.wait_ge(g["o2_lo"][p], i + 1)
                    for t in range(TILES):
                        last = split_products(
                            bank(p, 1)[:, t * C:(t + 1) * C],
                            [([x[p][:, h, t * P:(t + 1) * P] for x in (ch, cl)],
                              [w["wout"][:, h * C:(h + 1) * C] for w in (hi, lo)]) for h in range(HALVES)])
                    last.then_inc(g["out_done"][p], 1)
                for p in R2:
                    pe.wait_ge(ln["norm"][p], i * 6 + 6)
                    to_channels(p, 2, tn).then_inc(ln["tr"][p], 1)
                for p in R2:
                    pe.wait_ge(g["n3_lo"][p], i + 1)
                    for t in range(TILES):
                        last = split_products(
                            bank(p, 3)[:, t * EXPERTS:(t + 1) * EXPERTS],
                            [([x[p][:, h, t * P:(t + 1) * P] for x in (ch, cl)],
                              [w["wgate"][:, h * EXPERTS:(h + 1) * EXPERTS] for w in (hi, lo)])
                             for h in range(HALVES)])
                    last.then_inc(g["logits"][p], 1)
                for e in range(EXPERTS):
                    for p in R2:
                        if e >= 3:
                            pe.wait_ge(g["acc_done"][p], i * 16 + (e - 2) * 2 + 1)
                        for t in range(TILES):
                            last = split_products(
                                bank(p, e % 3)[:, t * C:(t + 1) * C],
                                [([x[p][:, h, t * P:(t + 1) * P] for x in (ch, cl)],
                                  [w["wexp"][:, (e * 2 + h) * C:(e * 2 + h + 1) * C] for w in (hi, lo)])
                                 for h in range(HALVES)])
                        last.then_inc(g["expert_done"][p], 1)

        @block.scalar
        def _(act):
            act.wait_ge(bn_step, 8)
            with act.Fori(0, ITERS) as i:
                for p in R2:
                    for h in range(HALVES):
                        nc.scalar.activation(relu[p][:, h, :], z[:, h, ds((i * 2 + p) * TOK, TOK)], ACT.Relu,
                                             scale=bn[:, h, 3:4], bias=bn[:, h, 4:5]).then_inc(g["relu_done"][p], 1)
                for p in R2:
                    act.wait_ge(g["t0_tr"][p], i + 2)
                    nc.scalar.activation(t1[p][:].rearrange("p t c -> p (t c)"), bank(p, 0),
                                         ACT.Copy).then_inc(g["t1_done"][p], 1)
                for p in R2:
                    act.wait_ge(ln["tr"][p], i * 3 + 1)
                    for h in range(HALVES):
                        nc.scalar.activation(wide[p][:, h, :], bank(p, 1)[:, h * TOK:(h + 1) * TOK], ACT.Identity,
                                             scale=col("n3w", h), bias=col("n3b", h)).then_inc(g["affine2"][p], 1)
                for p in R2:
                    act.wait_ge(g["affine2"][p], i * 2 + 2)
                    nc.scalar.activation(ch[p][:], wide[p][:, 0:2, :], ACT.Copy).then_inc(g["mlp_hi"][p], 1)
                for p in R2:
                    for m in range(4):
                        act.wait_ge(g["fc1_done"][p], i * 2 + m // 2 + 1)
                        if m == 0:
                            act.wait_ge(g["mlp_lo"][p], i + 1)
                        nc.scalar.activation(wide[p][:, m, :], bank(p, 2, 2)[:, m * TOK:(m + 1) * TOK], ACT.Gelu,
                                             scale=1.0 / S, bias=col("fc1b", m)).then_inc(g["gelu_done"][p], 1)
                for p in R2:
                    act.wait_ge(g["gelu_done"][p], i * 4 + 4)
                    nc.scalar.activation(hh_[p][:], wide[p][:], ACT.Copy).then_inc(g["hid_hi"][p], 1)
                for p in R2:
                    act.wait_ge(ln["tr"][p], i * 3 + 2)
                    nc.scalar.activation(ch[p][:].rearrange("p h t -> p (h t)"), bank(p, 1),
                                         ACT.Copy).then_inc(g["n2_hi"][p], 1)
                for p in R2:
                    act.wait_ge(g["v2_done"][p], i + 1)
                    nc.scalar.activation(vh[p][:, :, :, 0:L1D],
                                         bank(p, 0).rearrange("p (t h d) -> p t h d", t=TILES, h=L1H),
                                         ACT.Copy).then_inc(g["v2_hi"][p], 1)
                for p in R2:
                    act.wait_ge(g["rot_done"][p], i + 1)
                    nc.scalar.activation(hh_[p][:], rot[p][:], ACT.Copy).then_inc(g["rot_hi"][p], 1)
                for gr in range(GROUPS):
                    for p in R2:
                        act.wait_ge(g["shift2"][p], i * GROUPS * 2 + gr * 2 + 2)
                        nc.scalar.activation(prob[p][:], prob[p][:], ACT.Exp,
                                             scale=L1D ** -0.5 / (S * S)).then_inc(g["exp2"][p], 1)
                    for p in R2:
                        act.wait_ge(g["et2"][p], i * GROUPS + gr + 1)
                        nc.scalar.activation(eh[p][:], bank(p, 0, 3), ACT.Copy).then_inc(g["e2_hi"][p], 1)
                for p in R2:
                    act.wait_ge(g["o2_tr"][p], i + 1)
                    nc.scalar.activation(ch[p][:].rearrange("p h t -> p (h t)"), bank(p, 0),
                                         ACT.Copy).then_inc(g["o2_hi"][p], 1)
                for p in R2:
                    act.wait_ge(ln["tr"][p], i * 3 + 3)
                    act.wait_ge(g["out_done"][p], i + 1)
                    nc.scalar.activation(ch[p][:].rearrange("p h t -> p (h t)"), bank(p, 2),
                                         ACT.Copy).then_inc(g["n3_hi"][p], 1)
                for p in R2:
                    act.wait_ge(g["gate_max"][p], i + 1)
                    nc.scalar.activation(gate[p][:], gate[p][:], ACT.Exp, scale=1.0 / S).then_inc(g["gate_exp"][p], 1)

        @block.gpsimd
        def _(pool):
            nc.gpsimd.memset(half[:], -0.5).then_inc(half_set, 1)
            nc.gpsimd.memset(eps[:], EPS).then_inc(half_set, 1)
            for p in R2:
                nc.gpsimd.memset(vh[p][:], 1.0).then_inc(ones_set, 1)
            pool.wait_ge(half_set, 2)
            pool.wait_ge(bn_step, 3)
            nc.gpsimd.tensor_tensor(bn[:, :, 2], bn[:, :, 2], half[:, 0:2], ALU.pow).then_inc(bn_step, 1)

            def deviation(i, p, m):
                pool.wait_ge(ln["mv"][p], i * 6 + m * 2 + 2)
                nc.gpsimd.tensor_tensor(rstd[p][:], mv[p][:, :, 1], eps[:, 0:2], ALU.add).then_inc(ln["eps"][p], 1)
                pool.wait_ge(ln["eps"][p], i * 3 + m + 1)
                nc.gpsimd.tensor_tensor(rstd[p][:], rstd[p][:], half[:, 0:2], ALU.pow).then_inc(ln["rstd"][p], 1)

            with pool.Fori(0, ITERS) as i:
                for p in R2:
                    pool.wait_ge(g["xc_loaded"][p], i * 16 + 16)
                    pool.wait_ge(g["relu_done"][p], i * 2 + 2)
                    nc.gpsimd.tensor_tensor(xc[p][:], xc[p][:], relu[p][:], ALU.add).then_inc(g["t0_done"][p], 1)
                for p in R2:
                    deviation(i, p, 0)
                for p in R2:
                    pool.wait_ge(g["t1_done"][p], i + 1)
                    pool.wait_ge(ln["norm"][p], i * 6 + 2)
                    nc.gpsimd.tensor_tensor(t1[p][:], t1[p][:], fc2b[:].unsqueeze(1).to_broadcast([P, TILES, C]),
                                            ALU.add).then_inc(g["fc2_base"][p], 1)
                for p in R2:
                    deviation(i, p, 1)
                for p in R2:
                    pool.wait_ge(g["rope_b"][p], i * 4 + 4)
                    pool.wait_ge(g["rope_a"][p], i * 2 + 2)
                    nc.gpsimd.tensor_tensor(rot[p][:], rot[p][:], wide[p][:], ALU.add).then_inc(g["rot_done"][p], 1)
                for p in R2:
                    deviation(i, p, 2)

        @block.vector
        def _(dve):
            for h in range(HALVES):
                nc.vector.bn_aggr(bn[:, h, 0:2], zst[:, h].rearrange("p b s -> p (b s)")).then_inc(bn_step, 1)
            dve.wait_ge(bn_step, 2)
            nc.vector.tensor_scalar(bn[:, :, 2], bn[:, :, 1], EPS, None, ALU.add).then_inc(bn_step, 1)
            dve.wait_ge(bn_step, 4)
            nc.vector.tensor_tensor(bn[:, :, 3], bn[:, :, 2], col("bng", 0, 2), ALU.mult).then_inc(bn_step, 1)
            dve.wait_ge(bn_step, 5)
            nc.vector.tensor_tensor(bn[:, :, 5], bn[:, :, 0], bn[:, :, 3], ALU.mult).then_inc(bn_step, 1)
            dve.wait_ge(bn_step, 6)
            nc.vector.tensor_tensor(bn[:, :, 4], col("bnb", 0, 2), bn[:, :, 5], ALU.subtract).then_inc(bn_step, 2)
            dve.wait_ge(ones_set, 2)
            for p in R2:
                dve.sem_inc(g["acc_done"][p], 1)

            def layernorm(i, m, src, ready):
                for p in R2:
                    ready(p)
                    for t in range(TILES):
                        last = nc.vector.bn_stats(st[p][:, t, :], src[p][:, t, :])
                    last.then_inc(ln_stats[m][p], 1)
                    dve.wait_ge(half_set, 1)
                    dve.wait_ge(ln_stats[m][p], i + 1)
                    for t in range(TILES):
                        nc.vector.bn_aggr(mv[p][:, t, :], st[p][:, t, :]).then_inc(ln["mv"][p], 1)
                for p in R2:
                    dve.wait_ge(ln["rstd"][p], i * 3 + m + 1)
                    for t in range(TILES):
                        nc.vector.tensor_scalar(tn[p][:, t, :], src[p][:, t, :], mv[p][:, t, 0:1],
                                                rstd[p][:, t:t + 1], ALU.subtract, ALU.mult).then_inc(ln["norm"][p], 1)

            def low_part(p, k, dst, high, ready, done):
                dve.wait_ge(*ready)
                nc.vector.tensor_tensor(dst, k, high, ALU.subtract).then_inc(done[p], 1)

            with dve.Fori(0, ITERS) as i:
                layernorm(i, 0, t1, lambda p: dve.wait_ge(g["t1_done"][p], i + 1))
                for p in R2:
                    low_part(p, wide[p][:, 0:2, :], cl[p][:], ch[p][:], (g["mlp_hi"][p], i + 1), g["mlp_lo"])
                for p in R2:
                    low_part(p, wide[p][:], hl_[p][:], hh_[p][:], (g["hid_hi"][p], i + 1), g["hid_lo"])
                for p in R2:
                    dve.wait_ge(g["fc2_done"][p], i + 1)
                    dve.wait_ge(g["fc2_base"][p], i + 1)
                    nc.vector.scalar_tensor_tensor(t2[p][:].rearrange("p t c -> p (t c)"), bank(p, 0), 1.0 / S,
                                                   t1[p][:].rearrange("p t c -> p (t c)"), ALU.mult,
                                                   ALU.add).then_inc(g["t2_done"][p], 1)
                layernorm(i, 1, t2, lambda p: dve.wait_ge(g["t2_done"][p], i + 1))
                for p in R2:
                    low_part(p, bank(p, 1), cl[p][:].rearrange("p h t -> p (h t)"),
                             ch[p][:].rearrange("p h t -> p (h t)"), (g["n2_hi"][p], i + 1), g["n2_lo"])
                for p in R2:
                    for j in range(2):
                        dve.wait_ge(g["qk2_done"][p], i * 2 + j + 1)
                        x = bank(p, 2 + j).rearrange("p (m t) -> p m t", m=2)
                        sin = const("sin").rearrange("p (m t) -> p m t", m=2)
                        nc.vector.tensor_tensor(rot[p][:, 2 * j:2 * j + 2, :], x,
                                                const("cos").unsqueeze(1).to_broadcast([P, 2, TOK]),
                                                ALU.mult).then_inc(g["rope_a"][p], 1)
                        for m in range(2):
                            nc.vector.tensor_tensor(wide[p][:, 2 * j + m, :], x[:, 1 - m, :], sin[:, m, :],
                                                    ALU.mult).then_inc(g["rope_b"][p], 1)
                for p in R2:
                    low_part(p, bank(p, 0).rearrange("p (t h d) -> p t h d", t=TILES, h=L1H), vl[p][:],
                             vh[p][:, :, :, 0:L1D], (g["v2_hi"][p], i + 1), g["v2_lo"])
                for p in R2:
                    low_part(p, rot[p][:], hl_[p][:], hh_[p][:], (g["rot_hi"][p], i + 1), g["rot_lo"])
                for gr in range(GROUPS):
                    for p in R2:
                        tiles = [(bank(p, 0).rearrange("p (h m) -> p h m", h=GH), prob[p][:, 0:BANK], P, 0),
                                 (bank(p, 1, 2).rearrange("p (h m) -> p h m", h=GH), prob[p][:, BANK:GW], TOK, GH)]
                        dve.wait_ge(g["scores2"][p], i * GROUPS + gr + 2)
                        for x, _, w, m0 in tiles:
                            nc.vector.tensor_reduce(mx[p][:, m0:m0 + GH], x, op=ALU.max,
                                                    axis=AX).then_inc(g["max2"][p], 1)
                        for n, (x, dst, w, m0) in enumerate(tiles):
                            dve.wait_ge(g["max2"][p], i * GROUPS * 2 + gr * 2 + n + 1)
                            nc.vector.tensor_tensor(dst.rearrange("p (h m) -> p h m", h=GH), x,
                                                    mx[p][:, m0:m0 + GH].unsqueeze(2).to_broadcast([P, GH, w]),
                                                    ALU.subtract).then_inc(g["shift2"][p], 1)
                    for p in R2:
                        low_part(p, bank(p, 0, 3), el[p][:], eh[p][:], (g["e2_hi"][p], i * GROUPS + gr + 1),
                                 g["e2_lo"])
                    for p in R2:
                        dve.wait_ge(g["pv2"][p], i * GROUPS + gr + 1)
                        pv = bank(p, 3)[:, 0:2 * GH * D1].rearrange("p (t h d) -> p t h d", t=TILES, h=GH)
                        sums = rs[p][:].rearrange("p (t h) -> p t h", t=TILES)
                        nc.vector.reciprocal(sums, pv[:, :, :, L1D]).then_inc(g["recip2"][p], 1)
                        dve.wait_ge(g["recip2"][p], i * GROUPS + gr + 1)
                        nc.vector.tensor_tensor(
                            acc[p][:, :, gr * GH * L1D:(gr + 1) * GH * L1D].rearrange("p t (h d) -> p t h d", h=GH),
                            pv[:, :, :, 0:L1D], sums.unsqueeze(3).to_broadcast([P, TILES, GH, L1D]),
                            ALU.mult).then_inc(g["o2_done"][p], 1)
                for p in R2:
                    low_part(p, bank(p, 0), cl[p][:].rearrange("p h t -> p (h t)"),
                             ch[p][:].rearrange("p h t -> p (h t)"), (g["o2_hi"][p], i + 1), g["o2_lo"])
                for p in R2:
                    dve.wait_ge(g["out_done"][p], i + 1)
                    nc.vector.scalar_tensor_tensor(t2[p][:].rearrange("p t c -> p (t c)"), bank(p, 1), 1.0 / (S * S),
                                                   t2[p][:].rearrange("p t c -> p (t c)"), ALU.mult,
                                                   ALU.add).then_inc(g["t3_done"][p], 1)
                layernorm(i, 2, t2, lambda p: dve.wait_ge(g["t3_done"][p], i + 1))
                for p in R2:
                    low_part(p, bank(p, 2), cl[p][:].rearrange("p h t -> p (h t)"),
                             ch[p][:].rearrange("p h t -> p (h t)"), (g["n3_hi"][p], i + 1), g["n3_lo"])
                for p in R2:
                    def step(ins, n):
                        ins.then_inc(g["gate_step"][p], 1)
                        dve.wait_ge(g["gate_step"][p], i * 9 + n)

                    grid = [P, TILES, EXPERTS, EXPERTS]
                    of = lambda t: t[:].unsqueeze(3).to_broadcast(grid)
                    against = lambda t: t[:].unsqueeze(2).to_broadcast(grid)
                    pairs = lambda t: t[:].rearrange("p t (e j) -> p t e j", e=EXPERTS)
                    before = const("before").unsqueeze(1).to_broadcast([P, TILES, EXPERTS * EXPERTS])
                    dve.wait_ge(g["logits"][p], i + 1)
                    step(nc.vector.tensor_copy(lg[p][:], bank(p, 3)[:, 0:TILES * EXPERTS]
                                               .rearrange("p (t e) -> p t e", t=TILES)), 1)
                    nc.vector.tensor_reduce(g1[p][:, 0:TILES], lg[p][:], op=ALU.max, axis=AX)
                    nc.vector.tensor_tensor(pairs(cmp[p]), against(lg[p]), of(lg[p]), ALU.is_gt)
                    step(nc.vector.tensor_tensor(pairs(eq[p]), against(lg[p]), of(lg[p]), ALU.is_equal), 2)
                    nc.vector.tensor_tensor(gate[p][:], lg[p][:],
                                            g1[p][:, 0:TILES].unsqueeze(2).to_broadcast([P, TILES, EXPERTS]),
                                            ALU.subtract).then_inc(g["gate_max"][p], 1)
                    step(nc.vector.tensor_tensor(eq[p][:], eq[p][:], before, ALU.mult), 3)
                    step(nc.vector.tensor_tensor(cmp[p][:], cmp[p][:], eq[p][:], ALU.add), 4)
                    step(nc.vector.tensor_reduce(rank[p][:], pairs(cmp[p]), op=ALU.add, axis=AX), 5)
                    dve.wait_ge(g["gate_exp"][p], i + 1)
                    step(nc.vector.scalar_tensor_tensor(gate[p][:], rank[p][:], 2.0, gate[p][:], ALU.is_lt,
                                                        ALU.mult), 6)
                    step(nc.vector.tensor_reduce(g1[p][:, 0:TILES], gate[p][:], op=ALU.add, axis=AX), 7)
                    step(nc.vector.reciprocal(g1[p][:, TILES:2 * TILES], g1[p][:, 0:TILES]), 8)
                    step(nc.vector.scalar_tensor_tensor(
                        gate[p][:], gate[p][:], 1.0 / S,
                        g1[p][:, TILES:2 * TILES].unsqueeze(2).to_broadcast([P, TILES, EXPERTS]), ALU.mult,
                        ALU.mult), 9)
                for e in range(EXPERTS):
                    for p in R2:
                        dve.wait_ge(g["expert_done"][p], i * EXPERTS + e + 1)
                        for t in range(TILES):
                            if e:
                                dve.wait_ge(g["acc_done"][p], i * 16 + (e - 1) * 2 + t + 2)
                            before_ = t2 if e == 0 else acc
                            nc.vector.scalar_tensor_tensor(acc[p][:, t, :], bank(p, e % 3)[:, t * C:(t + 1) * C],
                                                           gate[p][:, t, e:e + 1], before_[p][:, t, :], ALU.mult,
                                                           ALU.add).then_inc(g["acc_done"][p], 1)


def constants():
    n = np.arange(WS)
    d = np.cos((2 * n[None, :] + 1) * n[:, None] * np.pi / (2 * WS))
    d[0] *= np.sqrt(1.0 / WS)
    d[1:] *= np.sqrt(2.0 / WS)
    d = d.astype(np.float32)
    kr = np.kron(d, d)
    kd = np.kron(np.eye(2, dtype=np.float32), kr)
    c = np.zeros((P, NCST), np.float32)

    def put(name, x):
        c[:, CST[name][0]:CST[name][0] + CST[name][1]] = x

    put("ident", np.eye(P))
    put("dct", kd.T)
    put("idct", kd)
    put("dcsum", kr.astype(np.float64).sum(0)[None, :])
    put("causal", np.where(np.arange(P)[None, :] > np.arange(P)[:, None], -1e30, 0.0))
    put("before", (np.arange(EXPERTS)[None, :] < np.arange(EXPERTS)[:, None]).reshape(1, -1))
    inv = (1.0 / 10000.0 ** (np.arange(0, L1D, 2, dtype=np.float32) / np.float32(L1D))).astype(np.float32)
    ang = np.tile((np.arange(TOK, dtype=np.float32)[None, :] * inv[:, None]).astype(np.float64), (L1H, 1))
    put("cos", np.cos(ang))
    put("sin", np.concatenate([-np.sin(ang), np.sin(ang)], 1))
    return c


def halves(w):
    return w.reshape(-1, P, w.shape[1]).transpose(1, 0, 2)


def layouts(v):
    g = lambda n: np.asarray(v[n])
    L = lambda n: g("L0_conv_" + n)
    cols = lambda x: x.reshape(-1, P).T
    r = {}
    x = g("x")
    xw = x.reshape(B, C, 2, WS, 2, WS).transpose(0, 4, 3, 5, 2, 1)
    r["xw"] = xw.reshape(B * P, TILES, C)
    r["xc"] = x.reshape(B, HALVES, P, TOK).transpose(0, 2, 1, 3).reshape(B * P, HALVES, TOK)
    parts = {"bqk": ["a1_bq", "a1_bk", "a2_bq", "a2_bk"], "nw": ["n2_w", "n1_w"], "nb": ["n2_b", "n1_b"],
             "bv": ["a1_bv", "a2_bv"], "bo": ["a1_bo", "a2_bo"], "c1b": ["c1_b"], "c2b": ["c2_b"], "bng": ["bn_g"],
             "bnb": ["bn_b"], "n3w": ["n3_w"], "n3b": ["n3_b"], "fc1b": ["fc1_b"]}
    r["vec"] = np.concatenate([cols(L(n)) for k in VEC for n in parts[k]], 1)
    stack = lambda ws: np.concatenate([halves(w).reshape(P, -1) for w in ws], 1)
    r["wqk"] = stack([L(n).T for n in ("a1_wq", "a1_wk", "a2_wq", "a2_wk")])
    r["wv"] = stack([L(n).T for n in ("a1_wv", "a2_wv")])
    r["wo"] = stack([L(n) for n in ("a1_wo", "a2_wo")]).reshape(P, 2, 2, C)
    c1 = L("c1_w")[:, :, 0, 0]
    r["c1"] = stack([c1[:, :C].T, c1[:, C:].T]).reshape(P, 2, 2, C)
    c2 = L("c2_w")
    r["wconv"] = stack([c2[:, :, t // 3, t % 3].T for t in range(TAPS)])
    r["wfc1"], r["wfc2"] = stack([L("fc1_w").T]), stack([L("fc2_w").T])
    w = g("L1_attn_w_qkv")
    order = lambda m: m.reshape(C, L1H, 2, 8).transpose(0, 2, 1, 3).reshape(C, C)
    r["wqkv"] = stack([order(w[:, :C]), order(w[:, C:2 * C]), w[:, 2 * C:]])
    r["wout"] = stack([g("L1_attn_w_out")])
    r["wgate"] = stack([g("L1_ffn_gate_w").T])
    r["wexp"] = stack([e.T for e in g("L1_ffn_expert_w")])
    r["fc2b"] = np.tile(L("fc2_b"), (P, 1))
    rel = (np.arange(0, (2 * WS - 1) * WS, 2 * WS - 1)[:, None] + np.arange(WS)[None, :]).reshape(1, -1)
    idx = (rel + rel.T)[:, ::-1]
    tabs = [L(n)[idx].reshape(WTOK, WTOK, 2, 4).transpose(0, 3, 2, 1).reshape(WTOK, 4, P)
            for n in ("a1_bias", "a2_bias")]
    r["relb"] = np.concatenate([np.stack(tabs, 1)] * 2, 0)
    r["cst"] = constants()
    return {n: np.ascontiguousarray(m) for n, m in r.items()}


def kernel(**inputs):
    import concourse.bacc as bacc
    from concourse.bass_utils import run_bass_kernel_spmd as run

    nc = bacc.Bacc("TRN2", target_bir_lowering=False, num_devices=1)
    arrays = layouts(inputs)
    a = {n: nc.dram_tensor("in_" + n, m.shape, mybir.dt.from_np(m.dtype), kind="ExternalInput").ap()
         for n, m in arrays.items()}
    out = nc.dram_tensor("out", (B * P, TILES, C), mybir.dt.float32, kind="ExternalOutput").ap()
    build(nc, a, out)
    r = run(nc, [{"in_" + n: m for n, m in arrays.items()}], core_ids=[0])
    got = r.results[0]["out"].reshape(B, P, TILES, C).transpose(0, 3, 2, 1)
    return np.ascontiguousarray(got).reshape(B, C, HW, HW)
```

```python
import math
from contextlib import ExitStack

import concourse.bass as bass
import numpy as np
from concourse import mybir

B, C, HW = 8, 256, 16
TOK = HW * HW
P = 128
HALVES = C // P
TILES = TOK // P
WS = 8
WTOK = WS * WS
NH, HD = 8, 32
HID = 512
L1H, L1D = 16, 16
EXPERTS = 8
PAD = HW + 2
TAPS = 9
GROUPS, GH = 4, 4
S = 256.0
YS = 16.0
EPS = 1e-5
BANK = 512
ITERS = B // 2

VEC = {}
for _name, _n in (("bqk", 8), ("nw", 4), ("nb", 4), ("bv", 4), ("bo", 4), ("c1b", 2), ("c2b", 2), ("bng", 2),
                  ("bnb", 2), ("n3w", 2), ("n3b", 2), ("fc1b", 4)):
    VEC[_name] = (sum(n for _, n in VEC.values()), _n)
NVEC = sum(n for _, n in VEC.values())
CST = {}
for _name, _n in (("ident", P), ("dct", P), ("idct", P), ("dcsum", WTOK), ("causal", P), ("before", 64),
                  ("cos", TOK), ("sin", 2 * TOK)):
    CST[_name] = (sum(n for _, n in CST.values()), _n)
NCST = sum(n for _, n in CST.values())
W_FIRST = {"wqk": 4 * 2 * C, "wv": 2 * 2 * C, "wconv": TAPS * 2 * C}
W_SECOND = {"wfc1": 2 * HID, "wfc2": 4 * C, "wqkv": 3 * 2 * C, "wout": 2 * C, "wgate": 2 * EXPERTS,
            "wexp": EXPERTS * 2 * C}
CHUNK = 1024
STAGES = 4


def build(nc, a, out):
    f32, f16, bf16 = mybir.dt.float32, mybir.dt.float16, mybir.dt.bfloat16
    ALU, ACT, AX = mybir.AluOpType, mybir.ActivationFunctionType, mybir.AxisListType.X
    ds = bass.ds
    scratch = nc.dram_tensor("rope_scratch", [2, 2, 4, P, TOK], f16, kind="Internal").ap()

    keep = ExitStack()
    with keep:
        def sb(stack, name, shape, dt=f32):
            return stack.enter_context(nc.sbuf_tensor(name, shape, dt))

        in_use = []

        def sem(name):
            in_use.append(nc.alloc_semaphore(name=name))
            return in_use[-1]

        def sems(name):
            return [sem(f"{name}{p}") for p in range(2)]

        def release_sems():
            nc.clear_and_free_semaphores(list(in_use))
            in_use.clear()
            nc.all_engine_barrier()

        vec = sb(keep, "vec", [P, NVEC])
        cst = sb(keep, "cst", [P, NCST])
        sbqk = sb(keep, "sbqk", [P, 8])
        identb = sb(keep, "identb", [P, P], bf16)
        maskb = sb(keep, "maskb", [P, 2 * P], bf16)
        fc2b = sb(keep, "fc2b", [P, C])
        z = sb(keep, "z", [P, HALVES, B * TOK])
        zst = sb(keep, "zst", [P, HALVES, B, 6])
        small = sb(keep, "small", [P, 64])
        hi, lo = {}, {}
        for name, n in W_SECOND.items():
            hi[name], lo[name] = sb(keep, name + "h", [P, n], f16), sb(keep, name + "l", [P, n], f16)
        psum = [keep.enter_context(nc.psum_tensor(f"ps{p}", [P, 4 * BANK], f32)) for p in range(2)]

        def col(name, k=0, n=1):
            return vec[:, VEC[name][0] + k:VEC[name][0] + k + n]

        def const(name):
            return cst[:, CST[name][0]:CST[name][0] + CST[name][1]]

        ident = const("ident")

        def bank(p, k, n=1):
            return psum[p][:, k * BANK:(k + n) * BANK]

        shared = dict(f32=f32, f16=f16, ALU=ALU, ACT=ACT, AX=AX, ds=ds, hi=hi, lo=lo, psum=psum, sb=sb, sem=sem, sems=sems,
                      col=col, const=const, bank=bank, ident=ident, vec=vec, cst=cst, sbqk=sbqk, identb=identb,
                      maskb=maskb, fc2b=fc2b, z=z, zst=zst, small=small, scratch=scratch)
        first = ExitStack()
        with first:
            for name, n in {**W_FIRST, "wfused": 2 * 2 * C}.items():
                hi[name], lo[name] = sb(first, name + "h", [P, n], f16), sb(first, name + "l", [P, n], f16)
            relb = sb(first, "relb", [P, 2, 4, P])
            ybias = sb(first, "ybias", [P, HALVES, WTOK])
            prepare(nc, a, {**shared, "relb": relb, "ybias": ybias})
            release_sems()
            windows(nc, a, {**shared, "relb": relb, "ybias": ybias})
            release_sems()
        images(nc, a, out, shared)


FRONT, ATTENTION, BACK = range(3)
WINDOW_AHEAD = (1, 0, -1)
WINDOW_LOOP = (1, ITERS, (-1, 0))
WINDOW_ORDER = [
    (FRONT, "load"), (BACK, "out_channels"), (ATTENTION, "scores"), (FRONT, "dct"), (BACK, "project"),
    (FRONT, "normalise"), (BACK, "conv", 0), (ATTENTION, "turn"), (FRONT, "to_channels"), (BACK, "conv", 1),
    (ATTENTION, "weigh"), (FRONT, "values"), (FRONT, "queries")]
MLP, QKV, CAUSAL, MOE = range(4)
IMAGE_AHEAD = (2, 1, 0, -1)
IMAGE_LOOP = (1, ITERS - 1, (0, 1))
IMAGE_ORDER = [
    (MLP, "load"), (MOE, "to_channels"), (CAUSAL, "scores", 0), (QKV, "statistics"), (MOE, "out_split"),
    (MLP, "tokens"), (MOE, "out_project"), (QKV, "to_channels"), (CAUSAL, "turn", 0), (MOE, "statistics"),
    (QKV, "rotate", 0), (CAUSAL, "scores", 1), (CAUSAL, "weigh", 0), (MLP, "to_channels"), (MOE, "norm_channels"),
    (QKV, "rotate", 1), (CAUSAL, "turn", 1), (MLP, "widen"), (MOE, "logits"), (QKV, "stack"),
    (CAUSAL, "scores", 2), (CAUSAL, "weigh", 1), (MOE, "expert", 0), (QKV, "values"), (MOE, "expert", 1),
    (CAUSAL, "turn", 2), (MLP, "narrow"), (MOE, "expert", 2), (CAUSAL, "scores", 3), (CAUSAL, "weigh", 2),
    (MOE, "expert", 3), (MOE, "expert", 4), (CAUSAL, "turn", 3), (MOE, "expert", 5), (MOE, "expert", 6),
    (CAUSAL, "weigh", 3), (MOE, "expert", 7), (MOE, "store")]


def pipeline(eng, order, ahead, loop, steps):
    def part(k, c):
        for kind, name, *which in order:
            half, p = divmod(c + ahead[kind], 2)
            i = k + half if half else k
            step = steps.get((name, kind), steps.get(name))
            if step and not (isinstance(i, int) and not 0 <= 2 * i + p < B):
                step(p, i, *which)

    first, end, offsets = loop
    for c in range(-max(ahead), 2 * first + offsets[0]):
        part(0, c)
    with eng.Fori(first, end) as i:
        for c in offsets:
            part(i, c)
    for c in range(2 * end + offsets[0], B - min(ahead)):
        part(0, c)


def freed(eng, semaphore, value):
    if not (isinstance(value, int) and value <= 0):
        eng.wait_ge(semaphore, value)


def split_products(nc, out_ap, pairs):
    n, done = len(pairs) * 3, 0
    for lhs, rhs in pairs:
        for x, w in ((0, 0), (1, 0), (0, 1)):
            last = nc.tensor.matmul(out_ap, lhs[x], rhs[w], start=done == 0, stop=done == n - 1)
            done += 1
    return last


def prepare(nc, a, k):
    f32, ALU, ACT = k["f32"], k["ALU"], k["ACT"]
    hi, lo, vec, cst, small, psum, sem = k["hi"], k["lo"], k["vec"], k["cst"], k["small"], k["psum"], k["sem"]
    col, const, bank = k["col"], k["const"], k["bank"]
    relb, ybias, sbqk, identb, maskb, fc2b = (k[n] for n in ("relb", "ybias", "sbqk", "identb", "maskb", "fc2b"))

    chunks = []
    for name, n in {**W_FIRST, **W_SECOND}.items():
        for c0 in range(0, n, CHUNK):
            chunks.append((name, c0, min(CHUNK, n - c0)))

    with ExitStack() as own:
        stage = [k["sb"](own, f"stage{s}", [P, CHUNK]) for s in range(STAGES)]
        wo = k["sb"](own, "wo", [P, 2, 2, C])
        c1 = k["sb"](own, "c1", [P, 2, 2, C])
        wf = k["sb"](own, "wf", [P, 2, 2, C])
        chunk_loaded = [sem(f"chunk_loaded{s}") for s in range(STAGES)]
        vec_loaded, cst_loaded, wo_loaded, tiles_loaded = (sem(n) for n in
                                                           ("vec_loaded", "cst_loaded", "wo_loaded", "tiles_loaded"))
        chunk_hi, chunk_lo = sem("chunk_hi"), sem("chunk_lo")
        fused_done, wf_ready, wf_hi, fold_done, const_step = (sem(n) for n in
                                                              ("fused_done", "wf_ready", "wf_hi", "fold_done",
                                                               "const_step"))
        block = own.enter_context(nc.Block())

        @block.sync
        def _(sp):
            sp.dma_start(vec[:], a["vec"]).then_inc(vec_loaded, 16)
            sp.dma_start(wo[:], a["wo"]).then_inc(wo_loaded, 16)
            sp.dma_start(c1[:], a["c1"]).then_inc(wo_loaded, 16)
            sp.dma_start(cst[:], a["cst"]).then_inc(cst_loaded, 16)
            for n, (name, c0, w) in enumerate(chunks):
                if n >= STAGES:
                    sp.wait_ge(chunk_lo, n - STAGES + 1)
                sp.dma_start(stage[n % STAGES][:, :w], a[name][:, c0:c0 + w]).then_inc(chunk_loaded[n % STAGES], 16)
            sp.dma_start(relb[:], a["relb"]).then_inc(tiles_loaded, 16)
            sp.dma_start(fc2b[:], a["fc2b"]).then_inc(tiles_loaded, 16)
            sp.wait_ge(tiles_loaded, 32)

        @block.tensor
        def _(pe):
            pe.wait_ge(wo_loaded, 32)
            for at in range(2):
                for ih in range(HALVES):
                    for jh in range(HALVES):
                        last = nc.tensor.matmul(bank(0, at)[:, ih * C:(ih + 1) * C],
                                                wo[:, at, jh, ih * P:(ih + 1) * P], c1[:, at, jh, :],
                                                start=jh == 0, stop=jh == HALVES - 1)
                last.then_inc(fused_done, 1)
            pe.wait_ge(wf_ready, 2)
            pe.wait_ge(vec_loaded, 16)
            for at in range(2):
                for oh in range(HALVES):
                    o = slice(oh * P, (oh + 1) * P)
                    for n, (w, v) in enumerate([(wf, "bv"), (c1, "bo")]):
                        for h in range(HALVES):
                            last = nc.tensor.matmul(bank(0, 2)[:, at * 2 + oh:at * 2 + oh + 1], w[:, at, h, o],
                                                    col(v, at * 2 + h), start=(n, h) == (0, 0), stop=(n, h) == (1, 1))
            last.then_inc(fold_done, 1)

        @block.scalar
        def _(act):
            act.wait_ge(vec_loaded, 16)
            nc.scalar.activation(sbqk[:], col("bqk", 0, 8), ACT.Copy, scale=S).then_inc(const_step, 1)
            for at in range(2):
                act.wait_ge(fused_done, at + 1)
                nc.scalar.activation(wf[:, at], bank(0, at).rearrange("p (h o) -> p h o", h=HALVES),
                                     ACT.Copy).then_inc(wf_ready, 1)
            act.wait_ge(wf_ready, 2)
            nc.scalar.activation(hi["wfused"][:], wf[:].rearrange("p a h o -> p (a h o)"), ACT.Copy,
                                 scale=S).then_inc(wf_hi, 1)
            for n, (name, c0, w) in enumerate(chunks):
                act.wait_ge(chunk_loaded[n % STAGES], 16 * (n // STAGES + 1))
                nc.scalar.activation(hi[name][:, c0:c0 + w], stage[n % STAGES][:, :w], ACT.Copy,
                                     scale=S).then_inc(chunk_hi, 1)

        @block.vector
        def _(dve):
            dve.wait_ge(wf_hi, 1)
            nc.vector.scalar_tensor_tensor(lo["wfused"][:], wf[:].rearrange("p a h o -> p (a h o)"), S,
                                           hi["wfused"][:], ALU.mult, ALU.subtract)
            dve.wait_ge(fold_done, 1)
            fold = small[:, 0:4]
            nc.vector.tensor_scalar(fold, bank(0, 2)[:, 0:4], YS, None, ALU.mult).then_inc(const_step, 1)
            dve.wait_ge(const_step, 2)
            nc.vector.scalar_tensor_tensor(small[:, 4:6], col("c1b", 0, 2), YS, small[:, 2:4], ALU.mult,
                                           ALU.add).then_inc(const_step, 1)
            dve.wait_ge(const_step, 3)
            dve.wait_ge(cst_loaded, 16)
            for oh in range(HALVES):
                nc.vector.tensor_scalar(ybias[:, oh, :], const("dcsum"), small[:, oh:oh + 1],
                                        small[:, 4 + oh:5 + oh], ALU.mult, ALU.add)
            nc.vector.tensor_copy(identb[:], const("ident"))
            nc.vector.memset(maskb[:, 0:P], 0.0)
            nc.vector.tensor_copy(maskb[:, P:2 * P], const("causal"))
            for n, (name, c0, w) in enumerate(chunks):
                dve.wait_ge(chunk_hi, n + 1)
                nc.vector.scalar_tensor_tensor(lo[name][:, c0:c0 + w], stage[n % STAGES][:, :w], S,
                                               hi[name][:, c0:c0 + w], ALU.mult, ALU.subtract).then_inc(chunk_lo, 1)


def windows(nc, a, k):
    f32, f16, ALU, ACT, AX, ds = k["f32"], k["f16"], k["ALU"], k["ACT"], k["AX"], k["ds"]
    hi, lo, psum, sems, sb, sem = k["hi"], k["lo"], k["psum"], k["sems"], k["sb"], k["sem"]
    col, const, bank, ident = k["col"], k["const"], k["bank"], k["ident"]
    relb, ybias, sbqk, z, zst = (k[n] for n in ("relb", "ybias", "sbqk", "z", "zst"))
    R2 = range(2)
    SRC_Q = [0, 1, 1, 0]
    SRC_V = [1, 0]

    with ExitStack() as own:
        def pair(name, shape, dt=f32):
            return [sb(own, f"{name}{p}", shape, dt) for p in R2]

        xw = pair("xw", [P, TILES, C])
        st, mv, rstd = pair("st", [P, 4, 6]), pair("mv", [P, 4, 2]), pair("rstd", [P, 4])
        xn = pair("xn", [P, 2, TILES, C])
        xh, xl = pair("xh", [P, 2, HALVES, TOK], f16), pair("xl", [P, 2, HALVES, TOK], f16)
        qkh, qkl = pair("qkh", [P, 4, HALVES, TOK], f16), pair("qkl", [P, 4, HALVES, TOK], f16)
        vh, vl = pair("vh", [P, 2, TILES, 4, 2 * HD], f16), pair("vl", [P, 2, TILES, 4, 2 * HD], f16)
        prob = pair("prob", [P, 4 * BANK])
        mx = pair("mx", [P, 32])
        eh, el = pair("eh", [P, 4 * BANK], f16), pair("el", [P, 4 * BANK], f16)
        rs = pair("rs", [P, 32])
        o = pair("o", [P, 2, TILES, C])
        och, ocl = pair("och", [P, 2 * BANK], f16), pair("ocl", [P, 2 * BANK], f16)
        y = pair("y", [P, HALVES, TOK])
        yh, yl = pair("yh", [P, HALVES, PAD, PAD], f16), pair("yl", [P, HALVES, PAD, PAD], f16)
        half, eps = sb(own, "half", [P, 4]), sb(own, "eps", [P, 4])

        (x_loaded, dct_done, stats_done, mv_done, eps_added, rstd_done, norm_done, tr_done, affine_done, xh_done,
         xl_done, qk_done, qkh_done, qkl_done, v_done, vh_done, vl_done, scores_done, biased, max_done, shifted,
         exp_done, et_done, eh_done, el_done, pv_done, recip_done, o_done, oc_done, och_done, ocl_done, y_done,
         y32_done, yh_done, yl_done, conv_done, z_done) = (
            sems(n) for n in ("x_loaded", "dct_done", "stats_done", "mv_done", "eps_added", "rstd_done", "norm_done",
                              "tr_done", "affine_done", "xh_done", "xl_done", "qk_done", "qkh_done", "qkl_done",
                              "v_done", "vh_done", "vl_done", "scores_done", "biased", "max_done", "shifted",
                              "exp_done", "et_done", "eh_done", "el_done", "pv_done", "recip_done", "o_done",
                              "oc_done", "och_done", "ocl_done", "y_done", "y32_done", "yh_done", "yl_done",
                              "conv_done", "z_done"))
        sum_done = sems("sum_done")
        pads_set, half_set = sem("pads_set"), sem("half_set")

        def v_bank(p, at, t):
            return bank(p, at)[:, t * TOK:(t + 1) * TOK].rearrange("p (w r d) -> p w r d", w=2, r=4)

        def by_window(v, p, at, t):
            return v[p][:, at, t].rearrange("p r (w d) -> p w r d", w=2)

        def image(im, oh, wi):
            return im[:, oh, 1 + wi * WS:1 + (wi + 1) * WS, 1:1 + HW].rearrange("p x (j y) -> p j x y", j=2)

        def window_rows(t, oh, wi):
            return t[:, oh, wi * P:(wi + 1) * P].rearrange("p (j x y) -> p j x y", j=2, x=WS)

        def affine(p):
            return prob[p][:, 0:2 * BANK].rearrange("p (s h t) -> p s h t", s=2, h=HALVES)

        block = own.enter_context(nc.Block())

        @block.sync
        def _(sp):
            def load(p, i):
                freed(sp, dct_done[p], i)
                freed(sp, norm_done[p], i)
                sp.dma_start(xw[p][:], a["xw"][ds((i * 2 + p) * P, P)]).then_inc(x_loaded[p], 16)

            pipeline(sp, WINDOW_ORDER, WINDOW_AHEAD, WINDOW_LOOP, {"load": load})

        @block.tensor
        def _(pe):
            def dct(p, i):
                pe.wait_ge(x_loaded[p], i * 16 + 16)
                freed(pe, ocl_done[p], i)
                for t in range(TILES):
                    last = nc.tensor.matmul(bank(p, 0)[:, t * C:(t + 1) * C], const("dct"), xw[p][:, t, :],
                                            start=True, stop=True)
                last.then_inc(dct_done[p], 1)

            def to_channels(p, i):
                pe.wait_ge(norm_done[p], i + 1)
                for s in range(2):
                    for t in range(TILES):
                        for h in range(HALVES):
                            last = nc.tensor.transpose(bank(p, 1 - s)[:, h * TOK + t * P:h * TOK + (t + 1) * P],
                                                       xn[p][:, s, t, h * P:(h + 1) * P], ident)
                last.then_inc(tr_done[p], 1)

            def values(p, i):
                pe.wait_ge(xl_done[p], i + 1)
                for at in range(2):
                    for w in range(4):
                        for hh in range(2):
                            last = split_products(
                                nc, bank(p, at)[64 * hh:64 * hh + 64, w * P:(w + 1) * P],
                                [([x[p][:, SRC_V[at], h, w * WTOK:(w + 1) * WTOK] for x in (xh, xl)],
                                  [wt["wv"][:, (at * 2 + h) * C + hh * P:(at * 2 + h) * C + (hh + 1) * P]
                                   for wt in (hi, lo)]) for h in range(HALVES)])
                    last.then_inc(v_done[p], 1)

            def queries(p, i):
                freed(pe, z_done[p], i * 2)
                for j in (2, 3, 0, 1):
                    if j < 2:
                        pe.wait_ge(vl_done[p], i * 2 + j + 1)
                    for oh in range(HALVES):
                        last = split_products(
                            nc, bank(p, j)[:, oh * TOK:(oh + 1) * TOK],
                            [([w["wqk"][:, (j * 2 + h) * C + oh * P:(j * 2 + h) * C + (oh + 1) * P]
                               for w in (hi, lo)], [x[p][:, SRC_Q[j], h, :] for x in (xh, xl)])
                             for h in range(HALVES)])
                    last.then_inc(qk_done[p], 1)

            def scores(p, i):
                pe.wait_ge(qkl_done[p], i * 8 + 8)
                for at in range(2):
                    for t in range(TILES):
                        for w in range(2):
                            tok = slice(t * P + w * WTOK, t * P + (w + 1) * WTOK)
                            for hh in range(2):
                                c0 = (at * 2 + t) * P + hh * WTOK
                                for n, (q, kk) in enumerate([(qkh, qkh), (qkl, qkh), (qkh, qkl)]):
                                    for r in range(4):
                                        rows = slice(32 * r, 32 * r + 32)
                                        last = nc.tensor.matmul(
                                            bank(p, r)[64 * w:64 * w + 64, c0:c0 + WTOK],
                                            q[p][rows, at * 2, hh, tok], kk[p][rows, at * 2 + 1, hh, tok],
                                            start=n == 0, stop=n == 2)
                last.then_inc(scores_done[p], 1)

            def turn(p, i):
                pe.wait_ge(biased[p], i * 4 + 4)
                for at in range(2):
                    pe.wait_ge(exp_done[p], i * 2 + at + 1)
                    for t in range(TILES):
                        for r in range(4):
                            c0 = (at * 2 + t) * BANK + r * P
                            last = nc.tensor.transpose(psum[p][:, c0:c0 + P], prob[p][:, c0:c0 + P], ident)
                        last.then_inc(et_done[p], 1)

            def weigh(p, i):
                pe.wait_ge(half_set, 1)
                pe.wait_ge(el_done[p], i * 4 + 4)
                for at in range(2):
                    for t in range(TILES):
                        for r in range(4):
                            for n, (e, v) in enumerate([(eh, vh), (eh, vl), (el, vh)]):
                                for hh in range(2):
                                    rows = slice(64 * hh, 64 * hh + 64)
                                    c0 = (at * 2 + t) * BANK + r * P
                                    d0 = (t * 4 + r) * 2 * HD
                                    last = nc.tensor.matmul(bank(p, at * 2 + hh)[:, d0:d0 + 2 * HD],
                                                            e[p][rows, c0:c0 + P], v[p][rows, at, t, r],
                                                            start=n == 0, stop=n == 2)
                    last.then_inc(pv_done[p], 1)

            def out_channels(p, i):
                pe.wait_ge(o_done[p], i * 8 + 8)
                for h in range(HALVES):
                    for t in range(TILES):
                        nc.tensor.matmul(bank(p, 0)[:, h * TOK + t * P:h * TOK + (t + 1) * P],
                                         o[p][:, 0, t, h * P:(h + 1) * P], const("idct"), start=True, stop=True)
                for h in range(HALVES):
                    for t in range(TILES):
                        last = nc.tensor.transpose(bank(p, 1)[:, h * TOK + t * P:h * TOK + (t + 1) * P],
                                                   o[p][:, 1, t, h * P:(h + 1) * P], ident)
                last.then_inc(oc_done[p], 1)

            def project(p, i):
                pe.wait_ge(ocl_done[p], i + 1)
                for oh in range(HALVES):
                    last = split_products(
                        nc, bank(p, 2)[:, oh * TOK:(oh + 1) * TOK],
                        [([w["wfused"][:, n * C + oh * P:n * C + (oh + 1) * P] for w in (hi, lo)],
                          [x[p][:, n * TOK:(n + 1) * TOK] for x in (och, ocl)]) for n in range(4)])
                last.then_inc(y_done[p], 1)

            def conv(p, i, oh):
                if oh == 0:
                    pe.wait_ge(yl_done[p], i * 4 + 4)
                prods = []
                for tap in range(TAPS):
                    dy, dx = divmod(tap, 3)
                    for h in range(HALVES):
                        c0 = (tap * 2 + h) * C + oh * P
                        prods.append(([w["wconv"][:, c0:c0 + P] for w in (hi, lo)],
                                      [im[p][:, h, dy:dy + HW, dx:dx + HW] for im in (yh, yl)]))
                split_products(nc, bank(p, 2 + oh)[:, 0:TOK], prods).then_inc(conv_done[p], 1)

            pipeline(pe, WINDOW_ORDER, WINDOW_AHEAD, WINDOW_LOOP, {
                "dct": dct, "to_channels": to_channels, "values": values, "queries": queries, "scores": scores,
                "turn": turn, "weigh": weigh, "out_channels": out_channels, "project": project, "conv": conv})

        @block.scalar
        def _(act):
            def to_channels(p, i):
                act.wait_ge(tr_done[p], i + 1)
                for s in range(2):
                    for h in range(HALVES):
                        nc.scalar.activation(affine(p)[:, s, h, :], bank(p, 1 - s)[:, h * TOK:(h + 1) * TOK],
                                             ACT.Identity, scale=col("nw", s * 2 + h),
                                             bias=col("nb", s * 2 + h)).then_inc(affine_done[p], 1)
                act.wait_ge(affine_done[p], i * 4 + 4)
                nc.scalar.activation(xh[p][:], affine(p), ACT.Copy).then_inc(xh_done[p], 1)

            def values(p, i):
                for at in range(2):
                    act.wait_ge(v_done[p], i * 2 + at + 1)
                    for t in range(TILES):
                        nc.scalar.activation(by_window(vh, p, at, t), v_bank(p, at, t), ACT.Copy)\
                            .then_inc(vh_done[p], 1)

            def queries(p, i):
                for n, j in enumerate((2, 3, 0, 1)):
                    act.wait_ge(qk_done[p], i * 4 + n + 1)
                    for oh in range(HALVES):
                        nc.scalar.activation(qkh[p][:, j, oh, :], bank(p, j)[:, oh * TOK:(oh + 1) * TOK],
                                             ACT.Identity,
                                             bias=sbqk[:, j * 2 + oh:j * 2 + oh + 1]).then_inc(qkh_done[p], 1)

            def scores(p, i):
                for at in range(2):
                    act.wait_ge(shifted[p], i * 2 + at + 1)
                    e = prob[p][:, at * 2 * BANK:(at + 1) * 2 * BANK]
                    nc.scalar.activation(e, e, ACT.Exp).then_inc(exp_done[p], 1)

            def turn(p, i):
                for n in range(4):
                    act.wait_ge(et_done[p], i * 4 + n + 1)
                    nc.scalar.activation(eh[p][:, n * BANK:(n + 1) * BANK], bank(p, n), ACT.Copy)\
                        .then_inc(eh_done[p], 1)

            def out_channels(p, i):
                act.wait_ge(oc_done[p], i + 1)
                nc.scalar.activation(och[p][:], bank(p, 0, 2), ACT.Copy).then_inc(och_done[p], 1)

            def project(p, i):
                act.wait_ge(y32_done[p], i * 2 + 2)
                for oh in range(HALVES):
                    for wi in range(2):
                        nc.scalar.activation(image(yh[p], oh, wi), window_rows(y[p], oh, wi), ACT.Copy)\
                            .then_inc(yh_done[p], 1)

            def conv(p, i, oh):
                act.wait_ge(conv_done[p], i * 2 + oh + 1)
                nc.scalar.activation(z[:, oh, ds((i * 2 + p) * TOK, TOK)], bank(p, 2 + oh)[:, 0:TOK], ACT.Identity,
                                     scale=1.0 / (S * YS), bias=col("c2b", oh)).then_inc(z_done[p], 1)

            pipeline(act, WINDOW_ORDER, WINDOW_AHEAD, WINDOW_LOOP, {
                "to_channels": to_channels, "values": values, "queries": queries, "scores": scores, "turn": turn,
                "out_channels": out_channels, "project": project, "conv": conv})

        @block.gpsimd
        def _(pool):
            for p in R2:
                nc.gpsimd.memset(yh[p][:], 0.0).then_inc(pads_set, 1)
                nc.gpsimd.memset(yl[p][:], 0.0).then_inc(pads_set, 1)
            nc.gpsimd.memset(half[:], -0.5).then_inc(half_set, 1)
            nc.gpsimd.memset(eps[:], EPS).then_inc(half_set, 1)
            pool.wait_ge(half_set, 2)

            def dct(p, i):
                pool.wait_ge(mv_done[p], i + 1)
                nc.gpsimd.tensor_tensor(rstd[p][:], mv[p][:, :, 1], eps[:], ALU.add).then_inc(eps_added[p], 1)
                pool.wait_ge(eps_added[p], i + 1)
                nc.gpsimd.tensor_tensor(rstd[p][:], rstd[p][:], half[:], ALU.pow).then_inc(rstd_done[p], 1)

            pipeline(pool, WINDOW_ORDER, WINDOW_AHEAD, WINDOW_LOOP, {"dct": dct})

        @block.vector
        def _(dve):
            dve.wait_ge(pads_set, 4)

            def tokens(p, s, t):
                return xw[p][:, t, :] if s == 0 else bank(p, 0)[:, t * C:(t + 1) * C]

            def dct(p, i):
                dve.wait_ge(x_loaded[p], i * 16 + 16)
                for s in range(2):
                    if s:
                        dve.wait_ge(dct_done[p], i + 1)
                    for t in range(TILES):
                        last = nc.vector.bn_stats(st[p][:, s * 2 + t, :], tokens(p, s, t))
                last.then_inc(stats_done[p], 1)
                dve.wait_ge(half_set, 1)
                dve.wait_ge(stats_done[p], i + 1)
                for n in range(4):
                    last = nc.vector.bn_aggr(mv[p][:, n, :], st[p][:, n, :])
                last.then_inc(mv_done[p], 1)

            def normalise(p, i):
                dve.wait_ge(rstd_done[p], i + 1)
                for s in range(2):
                    for t in range(TILES):
                        n = s * 2 + t
                        last = nc.vector.tensor_scalar(xn[p][:, s, t, :], tokens(p, s, t), mv[p][:, n, 0:1],
                                                       rstd[p][:, n:n + 1], ALU.subtract, ALU.mult)
                last.then_inc(norm_done[p], 1)

            def to_channels(p, i):
                dve.wait_ge(xh_done[p], i + 1)
                nc.vector.tensor_tensor(xl[p][:], affine(p), xh[p][:], ALU.subtract).then_inc(xl_done[p], 1)

            def values(p, i):
                for at in range(2):
                    dve.wait_ge(vh_done[p], i * 4 + at * 2 + 2)
                    for t in range(TILES):
                        last = nc.vector.tensor_tensor(by_window(vl, p, at, t), v_bank(p, at, t),
                                                       by_window(vh, p, at, t), ALU.subtract)
                    last.then_inc(vl_done[p], 1)

            def queries(p, i):
                for n, j in enumerate((2, 3, 0, 1)):
                    dve.wait_ge(qkh_done[p], i * 8 + n * 2 + 2)
                    for oh in range(HALVES):
                        m = j * 2 + oh
                        nc.vector.scalar_tensor_tensor(qkl[p][:, j, oh, :], bank(p, j)[:, oh * TOK:(oh + 1) * TOK],
                                                       sbqk[:, m:m + 1], qkh[p][:, j, oh, :], ALU.add,
                                                       ALU.subtract).then_inc(qkl_done[p], 1)

            def scores(p, i):
                banks = psum[p][:].rearrange("p (r c) -> p r c", r=4)
                dve.wait_ge(scores_done[p], i + 1)
                for n in range(4):
                    nc.vector.scalar_tensor_tensor(
                        prob[p][:, n * BANK:(n + 1) * BANK].rearrange("p (r c) -> p r c", r=4),
                        banks[:, :, n * P:(n + 1) * P], HD ** -0.5 / (S * S), relb[:, n // 2], ALU.mult,
                        ALU.add).then_inc(biased[p], 1)
                rows = prob[p][:].rearrange("p (a g m) -> p a g m", a=2, m=WTOK)
                for at in range(2):
                    dve.wait_ge(biased[p], i * 4 + at * 2 + 2)
                    nc.vector.tensor_reduce(mx[p][:, at * 16:(at + 1) * 16], rows[:, at], op=ALU.max,
                                            axis=AX).then_inc(max_done[p], 1)
                for at in range(2):
                    dve.wait_ge(max_done[p], i * 2 + at + 1)
                    nc.vector.tensor_tensor(rows[:, at], rows[:, at],
                                            mx[p][:, at * 16:(at + 1) * 16].unsqueeze(2).to_broadcast([P, 16, WTOK]),
                                            ALU.subtract).then_inc(shifted[p], 1)

            def turn(p, i):
                rows = prob[p][:].rearrange("p (g m) -> p g m", m=WTOK)
                dve.wait_ge(exp_done[p], i * 2 + 2)
                nc.vector.tensor_reduce(mx[p][:], rows, op=ALU.add, axis=AX).then_inc(sum_done[p], 1)
                dve.wait_ge(sum_done[p], i + 1)
                nc.vector.reciprocal(rs[p][:], mx[p][:]).then_inc(recip_done[p], 1)
                for n in range(4):
                    dve.wait_ge(eh_done[p], i * 4 + n + 1)
                    nc.vector.tensor_tensor(el[p][:, n * BANK:(n + 1) * BANK], bank(p, n),
                                            eh[p][:, n * BANK:(n + 1) * BANK], ALU.subtract).then_inc(el_done[p], 1)

            def weigh(p, i):
                dve.wait_ge(recip_done[p], i + 1)
                sums = rs[p][:].rearrange("p (a t r h) -> p a t r h", a=2, t=2, r=4)
                for at in range(2):
                    dve.wait_ge(pv_done[p], i * 2 + at + 1)
                    for hh in range(2):
                        pv = bank(p, at * 2 + hh).rearrange("p (t r w d) -> p t r w d", t=2, r=4, w=2)
                        for w in range(2):
                            rows = slice(64 * w, 64 * w + 64)
                            nc.vector.tensor_tensor(
                                o[p][rows, at, :, hh * P:(hh + 1) * P].rearrange("p t (r d) -> p t r d", r=4),
                                pv[rows, :, :, w, :],
                                sums[rows, at, :, :, hh].unsqueeze(3).to_broadcast([64, 2, 4, HD]),
                                ALU.mult).then_inc(o_done[p], 1)

            def out_channels(p, i):
                dve.wait_ge(och_done[p], i + 1)
                nc.vector.tensor_tensor(ocl[p][:], bank(p, 0, 2), och[p][:], ALU.subtract).then_inc(ocl_done[p], 1)

            def project(p, i):
                dve.wait_ge(y_done[p], i + 1)
                for oh in range(HALVES):
                    nc.vector.scalar_tensor_tensor(
                        y[p][:, oh, :].rearrange("p (w t) -> p w t", w=4),
                        bank(p, 2)[:, oh * TOK:(oh + 1) * TOK].rearrange("p (w t) -> p w t", w=4), YS / (S * S),
                        ybias[:, oh, :].unsqueeze(1).to_broadcast([P, 4, WTOK]), ALU.mult,
                        ALU.add).then_inc(y32_done[p], 1)
                for oh in range(HALVES):
                    for wi in range(2):
                        dve.wait_ge(yh_done[p], i * 4 + oh * 2 + wi + 1)
                        nc.vector.tensor_tensor(image(yl[p], oh, wi), window_rows(y[p], oh, wi),
                                                image(yh[p], oh, wi), ALU.subtract).then_inc(yl_done[p], 1)

            def conv(p, i, oh):
                dve.wait_ge(z_done[p], i * 2 + oh + 1)
                nc.vector.bn_stats(zst[:, oh, ds(i * 2 + p, 1), :], z[:, oh, ds((i * 2 + p) * TOK, TOK)])

            pipeline(dve, WINDOW_ORDER, WINDOW_AHEAD, WINDOW_LOOP, {
                "dct": dct, "normalise": normalise, "to_channels": to_channels, "values": values, "queries": queries,
                "scores": scores, "turn": turn, "weigh": weigh, "out_channels": out_channels, "project": project,
                "conv": conv})


def images(nc, a, out, k):
    f32, f16, ALU, ACT, AX, ds = k["f32"], k["f16"], k["ALU"], k["ACT"], k["AX"], k["ds"]
    hi, lo, psum, sems, sb, sem = k["hi"], k["lo"], k["psum"], k["sems"], k["sb"], k["sem"]
    col, const, bank, ident = k["col"], k["const"], k["bank"], k["ident"]
    z, zst, identb, maskb, fc2b, scratch = (k[n] for n in ("z", "zst", "identb", "maskb", "fc2b", "scratch"))
    R2 = range(2)
    KSTACK = 3 * L1D
    GW = 3 * BANK
    D1 = L1D + 1
    SOFTMAX_SCALE = L1D ** -0.5 / (S * S)
    FIRST_IN_3 = 3
    LNS = {MLP: 0, QKV: 1, MOE: 2}

    def expert_bank(e):
        return 3 if e >= FIRST_IN_3 and e % 2 else 1

    def count(p, i, per, plus=0):
        return i * (2 * per) + (p * per + plus)

    with ExitStack() as own:
        def pair(name, shape, dt=f32):
            return [sb(own, f"{name}{p}", shape, dt) for p in R2]

        def one(name, shape, dt=f32):
            return sb(own, name, shape, dt)

        xc = one("xc", [P, HALVES, TOK])
        relu = one("relu", [P, HALVES, TOK])
        t1, t2, t3 = (one(n, [P, TILES, C]) for n in ("t1", "t2", "t3"))
        res, acc = pair("res", [P, TILES, C]), pair("acc", [P, TILES, C])
        tn = [one(f"tn{m}", [P, TILES, C]) for m in range(3)]
        st = [one(f"st2{m}", [P, 2, 6]) for m in range(3)]
        mv = [one(f"mv2{m}", [P, 2, 2]) for m in range(3)]
        rstd = [one(f"rstd2{m}", [P, 2]) for m in range(3)]
        ch = [one(f"ch{m}", [P, HALVES, TOK], f16) for m in range(3)]
        cl = [one(f"cl{m}", [P, HALVES, TOK], f16) for m in range(3)]
        wide = one("wide", [P, 4, TOK])
        hh, hl = one("hh", [P, 4, TOK], f16), one("hl", [P, 4, TOK], f16)
        rot, turned = one("rot", [P, 4, TOK]), one("turned", [P, 4, TOK])
        rh, rl = one("rh", [P, 4, TOK], f16), one("rl", [P, 4, TOK], f16)
        qs, ks = pair("qs", [KSTACK, L1H, TOK], f16), pair("ks", [KSTACK, L1H, TOK], f16)
        vh, vl = pair("v2h", [P, TILES, L1H, D1], f16), pair("v2l", [P, TILES, L1H, L1D], f16)
        prob = one("prob2", [P, GW])
        eh, el = one("e2h", [P, GW], f16), one("e2l", [P, GW], f16)
        mx, nmx, rs = (one(n, [P, 2 * GH]) for n in ("mx2", "nmx2", "rs2"))
        o2 = one("o2", [P, TILES, C])
        lg, gate, rank = (one(n, [P, TILES, EXPERTS]) for n in ("lg", "gate", "rank"))
        cmp, eq = (one(n, [P, TILES, EXPERTS * EXPERTS]) for n in ("cmp", "eq"))
        g1 = one("g1", [P, 2 * TILES])
        half, eps = one("half2", [P, 4]), one("eps2", [P, 4])
        bn = one("bn", [P, HALVES, 6])

        xc_loaded, spilled, stacked, stored = (sems(n) for n in ("xc_loaded", "spilled", "stacked", "stored"))
        ln = {n: [sem(f"ln_{n}{m}_") for m in range(3)] for n in ("stats", "mv", "eps", "rstd", "norm", "tr")}
        (relu_done, t0_done, t0_tr, t1_done, fc2_base, affine2, mlp_hi, mlp_lo, fc1_done, gelu_done, hid_hi, hid_lo,
         fc2_done, t2_done, res_done, n2_hi, n2_lo, qk2_done, v2_done, v2_hi, v2_lo, rope_a, rope_b, rot_done,
         rot_hi, rot_lo, scores2, max2, bias2, exp2, et2, e2_hi, e2_lo, pv2, recip2, o2_done, o2_tr, o2_hi, o2_lo,
         out_done, t3_done, n3_hi, n3_lo, logits, gate_step, gate_max, gate_exp, expert_done, acc_done, bn_step,
         half_set, ones_set) = (sem(n) for n in (
             "relu_done", "t0_done", "t0_tr", "t1_done", "fc2_base", "affine2", "mlp_hi", "mlp_lo", "fc1_done",
             "gelu_done", "hid_hi", "hid_lo", "fc2_done", "t2_done", "res_done", "n2_hi", "n2_lo", "qk2_done",
             "v2_done", "v2_hi", "v2_lo", "rope_a", "rope_b", "rot_done", "rot_hi", "rot_lo", "scores2", "max2",
             "bias2", "exp2", "et2", "e2_hi", "e2_lo", "pv2", "recip2", "o2_done", "o2_tr", "o2_hi", "o2_lo",
             "out_done", "t3_done", "n3_hi", "n3_lo", "logits", "gate_step", "gate_max", "gate_exp",
             "expert_done", "acc_done", "bn_step", "half_set2", "ones_set2"))

        def run(eng, steps):
            pipeline(eng, IMAGE_ORDER, IMAGE_AHEAD, IMAGE_LOOP, steps)

        flat = lambda t: t[:].rearrange("p h t -> p (h t)")
        SCORE_BANKS = [((0, 1, 2, 3), P, 0), ((0, 1), TOK, P), ((2, 3), TOK, P)]

        block = own.enter_context(nc.Block())

        @block.sync
        def _(sp):
            def load(p, i):
                freed(sp, t0_tr, count(p, i, 1))
                sp.dma_start(xc[:], a["xc"][ds((i * 2 + p) * P, P)]).then_inc(xc_loaded[p], 16)

            def stack(p, i):
                for n, (part, ready) in enumerate(((rh, rot_hi), (rl, rot_lo))):
                    sp.wait_ge(ready, count(p, i, 1, 1))
                    sp.dma_start(scratch[p, n].rearrange("j c t -> c j t"), part[:]).then_inc(spilled[p], 16)
                freed(sp, scores2, count(p, i, GROUPS * 3, -GROUPS * 3))
                sp.wait_ge(spilled[p], i * 32 + 32)
                for qk, dst, parts in ((0, qs, (0, 1, 0)), (1, ks, (0, 0, 1))):
                    for n, part in enumerate(parts):
                        for j in range(2):
                            src = scratch[p, part, qk * 2 + j].rearrange("(h d) t -> d h t", h=L1H)
                            r0 = n * L1D + j * 8
                            sp.dma_start(dst[p][r0:r0 + 8], src).then_inc(stacked[p], 16)

            def store(p, i):
                sp.wait_ge(acc_done, count(p, i, EXPERTS * 2, EXPERTS * 2))
                sp.dma_start(out[ds((i * 2 + p) * P, P)], acc[p][:]).then_inc(stored[p], 16)

            run(sp, {"load": load, "stack": stack, "store": store})
            for p in R2:
                sp.wait_ge(stored[p], ITERS * 16)

        @block.tensor
        def _(pe):
            def to_channels(out_bank, src):
                for t in range(TILES):
                    for h in range(HALVES):
                        last = nc.tensor.transpose(out_bank[:, h * TOK + t * P:h * TOK + (t + 1) * P],
                                                   src[:, t, h * P:(h + 1) * P], ident)
                return last

            def token_product(out_bank, m, name, w0, width):
                for t in range(TILES):
                    last = split_products(
                        nc, out_bank[:, t * width:(t + 1) * width],
                        [([x[m][:, h, t * P:(t + 1) * P] for x in (ch, cl)],
                          [w[name][:, w0 + h * width:w0 + (h + 1) * width] for w in (hi, lo)])
                         for h in range(HALVES)])
                return last

            def tokens(p, i):
                pe.wait_ge(t0_done, count(p, i, 1, 1))
                for t in range(TILES):
                    for h in range(HALVES):
                        last = nc.tensor.transpose(bank(1 - p, 2)[:, t * C + h * P:t * C + (h + 1) * P],
                                                   xc[:, h, t * P:(t + 1) * P], ident)
                last.then_inc(t0_tr, 1)

            def mlp_channels(p, i):
                pe.wait_ge(ln["norm"][0], count(p, i, 1, 1))
                to_channels(bank(1 - p, 3), tn[0]).then_inc(ln["tr"][0], 1)

            def widen(p, i):
                pe.wait_ge(mlp_lo, count(p, i, 1, 1))
                for m in range(4):
                    last = split_products(
                        nc, bank(1 - p, 2, 2)[:, m * TOK:(m + 1) * TOK],
                        [([w["wfc1"][:, h * HID + m * P:h * HID + (m + 1) * P] for w in (hi, lo)],
                          [x[0][:, h, :] for x in (ch, cl)]) for h in range(HALVES)])
                    if m % 2:
                        last.then_inc(fc1_done, 1)

            def narrow(p, i):
                pe.wait_ge(hid_lo, count(p, i, 1, 1))
                for t in range(TILES):
                    last = split_products(
                        nc, bank(1 - p, 2)[:, t * C:(t + 1) * C],
                        [([x[:, m, t * P:(t + 1) * P] for x in (hh, hl)],
                          [w["wfc2"][:, m * C:(m + 1) * C] for w in (hi, lo)]) for m in range(4)])
                last.then_inc(fc2_done, 1)

            def qkv_channels(p, i):
                pe.wait_ge(ln["norm"][1], count(p, i, 1, 1))
                to_channels(bank(p, 0), tn[1]).then_inc(ln["tr"][1], 1)

            def rotate(p, i, j):
                if j == 0:
                    pe.wait_ge(n2_lo, count(p, i, 1, 1))
                else:
                    pe.wait_ge(rope_b, count(p, i, 4, 2))
                for m in range(HALVES):
                    last = split_products(
                        nc, bank(p, 0)[:, m * TOK:(m + 1) * TOK],
                        [([w["wqkv"][:, (j * 2 + h) * C + m * P:(j * 2 + h) * C + (m + 1) * P] for w in (hi, lo)],
                          [x[1][:, h, :] for x in (ch, cl)]) for h in range(HALVES)])
                last.then_inc(qk2_done, 1)

            def values(p, i):
                pe.wait_ge(rope_b, count(p, i, 4, 4))
                token_product(bank(p, 0), 1, "wqkv", 4 * C, C).then_inc(v2_done, 1)

            def scores(p, i, gr):
                if gr == 0:
                    pe.wait_ge(stacked[p], (i + 1) * 12 * 16)
                    pe.wait_ge(v2_lo, count(p, i, 1, 1))
                    freed(pe, acc_done, count(p, i, EXPERTS * 2, -EXPERTS * 2))
                    n = count(p, i, 1, 2)
                    pe.wait_ge(t2_done, min(n, B) if isinstance(n, int) else n)
                for b, (heads, keys, q0) in enumerate(SCORE_BANKS):
                    if gr:
                        pe.wait_ge(e2_lo, count(p, i, GROUPS * 3, (gr - 1) * 3 + b + 1))
                    mask = maskb[:, P:2 * P] if keys == P else maskb[:]
                    nc.tensor.matmul(bank(p, b).rearrange("p (h m) -> p h m", m=keys), identb[:],
                                     mask.unsqueeze(1).to_broadcast([P, len(heads), keys]), start=True, stop=False)
                    for n, h in enumerate(heads):
                        last = nc.tensor.matmul(bank(p, b)[:, n * keys:(n + 1) * keys],
                                                qs[p][:, gr * GH + h, q0:q0 + P], ks[p][:, gr * GH + h, 0:keys],
                                                start=False, stop=n == len(heads) - 1)
                    last.then_inc(scores2, 1)

            def turn(p, i, gr):
                for b in range(3):
                    pe.wait_ge(exp2, count(p, i, GROUPS * 3, gr * 3 + b + 1))
                    for n in range(4):
                        c0 = b * BANK + n * P
                        last = nc.tensor.transpose(psum[p][:, c0:c0 + P], prob[:, c0:c0 + P], ident)
                    last.then_inc(et2, 1)

            def weigh(p, i, gr):
                pe.wait_ge(e2_lo, count(p, i, GROUPS * 3, gr * 3 + 3))
                if gr:
                    pe.wait_ge(o2_done, count(p, i, GROUPS, gr))
                for t in range(TILES):
                    for h in range(GH):
                        c0 = (t * GH + h) * D1
                        blocks = [h * P] if t == 0 else [BANK + h * TOK, BANK + h * TOK + P]
                        for kt, e0 in enumerate(blocks):
                            for m, (e, v, w) in enumerate(((eh, vh, D1), (eh, vl, L1D), (el, vh, D1))):
                                last = nc.tensor.matmul(bank(p, 3)[:, c0:c0 + w], e[:, e0:e0 + P],
                                                        v[p][:, kt, gr * GH + h, 0:w], start=(kt, m) == (0, 0),
                                                        stop=(kt, m) == (len(blocks) - 1, 2))
                last.then_inc(pv2, 1)

            def out_channels(p, i):
                pe.wait_ge(o2_done, count(p, i, GROUPS, GROUPS))
                to_channels(bank(p, 1), o2).then_inc(o2_tr, 1)

            def out_project(p, i):
                pe.wait_ge(o2_lo, count(p, i, 1, 1))
                token_product(bank(p, 1), 2, "wout", 0, C).then_inc(out_done, 1)

            def norm_channels(p, i):
                pe.wait_ge(ln["norm"][2], count(p, i, 1, 1))
                to_channels(bank(p, 1), tn[2]).then_inc(ln["tr"][2], 1)

            def gate_logits(p, i):
                pe.wait_ge(n3_lo, count(p, i, 1, 1))
                token_product(bank(p, 1), 2, "wgate", 0, EXPERTS).then_inc(logits, 1)

            def expert(p, i, e):
                if e == 0:
                    pe.wait_ge(gate_step, count(p, i, 9, 1))
                elif e < FIRST_IN_3:
                    pe.wait_ge(acc_done, count(p, i, EXPERTS * 2, e * 2))
                elif e > FIRST_IN_3:
                    pe.wait_ge(acc_done, count(p, i, EXPERTS * 2, (e - 1) * 2))
                token_product(bank(p, expert_bank(e)), 2, "wexp", e * 2 * C, C).then_inc(expert_done, 1)

            run(pe, {"tokens": tokens, ("to_channels", MLP): mlp_channels, "widen": widen, "narrow": narrow,
                     ("to_channels", QKV): qkv_channels, "rotate": rotate, "values": values, "scores": scores,
                     "turn": turn, "weigh": weigh, ("to_channels", MOE): out_channels, "out_project": out_project,
                     "norm_channels": norm_channels, "logits": gate_logits, "expert": expert})

        @block.scalar
        def _(act):
            def high_part(m, src, done):
                nc.scalar.activation(flat(ch[m]), src, ACT.Copy).then_inc(done, 1)

            def load(p, i):
                freed(act, t0_done, count(p, i, 1))
                for h in range(HALVES):
                    nc.scalar.activation(relu[:, h, :], z[:, h, ds((i * 2 + p) * TOK, TOK)], ACT.Relu,
                                         scale=bn[:, h, 3:4], bias=bn[:, h, 4:5]).then_inc(relu_done, 1)

            def tokens(p, i):
                freed(act, t2_done, count(p, i, 1))
                act.wait_ge(t0_tr, count(p, i, 1, 1))
                nc.scalar.activation(t1[:].rearrange("p t c -> p (t c)"), bank(1 - p, 2),
                                     ACT.Copy).then_inc(t1_done, 1)

            def mlp_channels(p, i):
                freed(act, hid_lo, count(p, i, 1))
                act.wait_ge(ln["tr"][0], count(p, i, 1, 1))
                for h in range(HALVES):
                    nc.scalar.activation(wide[:, h, :], bank(1 - p, 3)[:, h * TOK:(h + 1) * TOK], ACT.Identity,
                                         scale=col("n3w", h), bias=col("n3b", h)).then_inc(affine2, 1)
                act.wait_ge(affine2, count(p, i, 2, 2))
                nc.scalar.activation(ch[0][:], wide[:, 0:2, :], ACT.Copy).then_inc(mlp_hi, 1)

            def widen(p, i):
                for m in range(4):
                    if m == 0:
                        act.wait_ge(mlp_lo, count(p, i, 1, 1))
                    act.wait_ge(fc1_done, count(p, i, 2, m // 2 + 1))
                    nc.scalar.activation(wide[:, m, :], bank(1 - p, 2, 2)[:, m * TOK:(m + 1) * TOK], ACT.Gelu,
                                         scale=1.0 / S, bias=col("fc1b", m)).then_inc(gelu_done, 1)
                act.wait_ge(gelu_done, count(p, i, 4, 4))
                nc.scalar.activation(hh[:], wide[:], ACT.Copy).then_inc(hid_hi, 1)

            def qkv_channels(p, i):
                act.wait_ge(ln["tr"][1], count(p, i, 1, 1))
                high_part(1, bank(p, 0), n2_hi)
                freed(act, t3_done, count(p, i, 1, -1))
                act.wait_ge(t2_done, count(p, i, 1, 1))
                nc.scalar.activation(res[p][:], t2[:], ACT.Copy).then_inc(res_done, 1)

            def stack(p, i):
                act.wait_ge(rot_done, count(p, i, 1, 1))
                nc.scalar.activation(rh[:], rot[:], ACT.Copy).then_inc(rot_hi, 1)

            def values(p, i):
                if isinstance(i, int) and i == 0:
                    act.wait_ge(ones_set, 2)
                freed(act, pv2, count(p, i, GROUPS, -GROUPS))
                act.wait_ge(v2_done, count(p, i, 1, 1))
                nc.scalar.activation(vh[p][:, :, :, 0:L1D],
                                     bank(p, 0).rearrange("p (t h d) -> p t h d", t=TILES, h=L1H),
                                     ACT.Copy).then_inc(v2_hi, 1)

            def scores(p, i, gr):
                for b, (heads, keys, _) in enumerate(SCORE_BANKS):
                    act.wait_ge(bias2, count(p, i, GROUPS * 3, gr * 3 + b + 1))
                    for n in range(len(heads)):
                        m = (0, 4, 6)[b] + n
                        c0 = b * BANK + n * keys
                        last = nc.scalar.activation(prob[:, c0:c0 + keys], psum[p][:, c0:c0 + keys], ACT.Exp,
                                                    scale=SOFTMAX_SCALE, bias=nmx[:, m:m + 1])
                    last.then_inc(exp2, 1)

            def turn(p, i, gr):
                for b in range(3):
                    act.wait_ge(et2, count(p, i, GROUPS * 3, gr * 3 + b + 1))
                    nc.scalar.activation(eh[:, b * BANK:(b + 1) * BANK], bank(p, b), ACT.Copy).then_inc(e2_hi, 1)

            def out_channels(p, i):
                act.wait_ge(o2_tr, count(p, i, 1, 1))
                high_part(2, bank(p, 1), o2_hi)

            def norm_channels(p, i):
                act.wait_ge(ln["tr"][2], count(p, i, 1, 1))
                high_part(2, bank(p, 1), n3_hi)

            def gate_logits(p, i):
                act.wait_ge(gate_max, count(p, i, 1, 1))
                nc.scalar.activation(gate[:], gate[:], ACT.Exp, scale=1.0 / S).then_inc(gate_exp, 1)

            act.wait_ge(bn_step, 8)
            run(act, {"load": load, "tokens": tokens, ("to_channels", MLP): mlp_channels, "widen": widen,
                      ("to_channels", QKV): qkv_channels, "stack": stack, "values": values, "scores": scores,
                      "turn": turn, ("to_channels", MOE): out_channels, "norm_channels": norm_channels,
                      "logits": gate_logits})

        @block.gpsimd
        def _(pool):
            def load(p, i):
                pool.wait_ge(xc_loaded[p], i * 16 + 16)
                pool.wait_ge(relu_done, count(p, i, 2, 2))
                nc.gpsimd.tensor_tensor(xc[:], xc[:], relu[:], ALU.add).then_inc(t0_done, 1)

            def deviation(m):
                def step(p, i):
                    pool.wait_ge(ln["mv"][m], count(p, i, 1, 1))
                    nc.gpsimd.tensor_tensor(rstd[m][:], mv[m][:, :, 1], eps[:, 0:2], ALU.add)\
                        .then_inc(ln["eps"][m], 1)
                    pool.wait_ge(ln["eps"][m], count(p, i, 1, 1))
                    nc.gpsimd.tensor_tensor(rstd[m][:], rstd[m][:], half[:, 0:2], ALU.pow).then_inc(ln["rstd"][m], 1)
                return step

            def mlp_channels(p, i):
                pool.wait_ge(ln["norm"][0], count(p, i, 1, 1))
                nc.gpsimd.tensor_tensor(t1[:], t1[:], fc2b[:].unsqueeze(1).to_broadcast([P, TILES, C]),
                                        ALU.add).then_inc(fc2_base, 1)
                pool.wait_ge(mlp_hi, count(p, i, 1, 1))
                nc.gpsimd.tensor_tensor(cl[0][:], wide[:, 0:2, :], ch[0][:], ALU.subtract).then_inc(mlp_lo, 1)

            def widen(p, i):
                pool.wait_ge(hid_hi, count(p, i, 1, 1))
                nc.gpsimd.tensor_tensor(hl[:], wide[:], hh[:], ALU.subtract).then_inc(hid_lo, 1)

            def stack(p, i):
                pool.wait_ge(rope_b, count(p, i, 4, 4))
                nc.gpsimd.tensor_tensor(rot[:], rot[:], turned[:], ALU.add).then_inc(rot_done, 1)

            nc.gpsimd.memset(half[:], -0.5).then_inc(half_set, 1)
            nc.gpsimd.memset(eps[:], EPS).then_inc(half_set, 1)
            for p in R2:
                nc.gpsimd.memset(vh[p][:], 1.0).then_inc(ones_set, 1)
            pool.wait_ge(half_set, 2)
            pool.wait_ge(bn_step, 3)
            nc.gpsimd.tensor_tensor(bn[:, :, 2], bn[:, :, 2], half[:, 0:2], ALU.pow).then_inc(bn_step, 1)
            run(pool, {"load": load, "tokens": deviation(0), ("to_channels", MLP): mlp_channels, "widen": widen,
                       ("statistics", QKV): deviation(1), ("statistics", MOE): deviation(2), "stack": stack})

        @block.vector
        def _(dve):
            def statistics(m, src, ready):
                def step(p, i):
                    dve.wait_ge(ready, count(p, i, 1, 1))
                    for t in range(TILES):
                        last = nc.vector.bn_stats(st[m][:, t, :], src[:, t, :])
                    last.then_inc(ln["stats"][m], 1)
                    dve.wait_ge(half_set, 1)
                    dve.wait_ge(ln["stats"][m], count(p, i, 1, 1))
                    for t in range(TILES):
                        last = nc.vector.bn_aggr(mv[m][:, t, :], st[m][:, t, :])
                    last.then_inc(ln["mv"][m], 1)
                return step

            def normalise(p, i, m, src):
                dve.wait_ge(ln["rstd"][m], count(p, i, 1, 1))
                for t in range(TILES):
                    last = nc.vector.tensor_scalar(tn[m][:, t, :], src[:, t, :], mv[m][:, t, 0:1],
                                                   rstd[m][:, t:t + 1], ALU.subtract, ALU.mult)
                last.then_inc(ln["norm"][m], 1)

            def low_part(p, i, m, src, high_done, done):
                dve.wait_ge(high_done, count(p, i, 1, 1))
                nc.vector.tensor_tensor(flat(cl[m]), src, flat(ch[m]), ALU.subtract).then_inc(done, 1)

            def mlp_channels(p, i):
                normalise(p, i, 0, t1)

            def narrow(p, i):
                freed(dve, res_done, count(p, i, 1))
                dve.wait_ge(fc2_base, count(p, i, 1, 1))
                dve.wait_ge(fc2_done, count(p, i, 1, 1))
                nc.vector.scalar_tensor_tensor(t2[:].rearrange("p t c -> p (t c)"), bank(1 - p, 2), 1.0 / S,
                                               t1[:].rearrange("p t c -> p (t c)"), ALU.mult,
                                               ALU.add).then_inc(t2_done, 1)

            def qkv_channels(p, i):
                normalise(p, i, 1, t2)
                low_part(p, i, 1, bank(p, 0), n2_hi, n2_lo)

            def rotate(p, i, j):
                dve.wait_ge(qk2_done, count(p, i, 2, j + 1))
                x = bank(p, 0).rearrange("p (m t) -> p m t", m=2)
                sin = const("sin").rearrange("p (m t) -> p m t", m=2)
                nc.vector.tensor_tensor(rot[:, 2 * j:2 * j + 2, :], x,
                                        const("cos").unsqueeze(1).to_broadcast([P, 2, TOK]),
                                        ALU.mult).then_inc(rope_a, 1)
                for m in range(2):
                    nc.vector.tensor_tensor(turned[:, 2 * j + m, :], x[:, 1 - m, :], sin[:, m, :],
                                            ALU.mult).then_inc(rope_b, 1)

            def stack(p, i):
                dve.wait_ge(rot_hi, count(p, i, 1, 1))
                nc.vector.tensor_tensor(rl[:], rot[:], rh[:], ALU.subtract).then_inc(rot_lo, 1)

            def values(p, i):
                dve.wait_ge(v2_hi, count(p, i, 1, 1))
                nc.vector.tensor_tensor(vl[p][:], bank(p, 0).rearrange("p (t h d) -> p t h d", t=TILES, h=L1H),
                                        vh[p][:, :, :, 0:L1D], ALU.subtract).then_inc(v2_lo, 1)

            def scores(p, i, gr):
                at = (slice(0, 4), slice(4, 6), slice(6, 8))
                for b, (heads, keys, _) in enumerate(SCORE_BANKS):
                    dve.wait_ge(scores2, count(p, i, GROUPS * 3, gr * 3 + b + 1))
                    nc.vector.tensor_reduce(mx[:, at[b]], bank(p, b).rearrange("p (h m) -> p h m", m=keys),
                                            op=ALU.max, axis=AX).then_inc(max2, 1)
                for b in range(3):
                    dve.wait_ge(max2, count(p, i, GROUPS * 3, gr * 3 + b + 1))
                    nc.vector.tensor_scalar(nmx[:, at[b]], mx[:, at[b]], -SOFTMAX_SCALE, None,
                                            ALU.mult).then_inc(bias2, 1)

            def turn(p, i, gr):
                for b in range(3):
                    dve.wait_ge(e2_hi, count(p, i, GROUPS * 3, gr * 3 + b + 1))
                    nc.vector.tensor_tensor(el[:, b * BANK:(b + 1) * BANK], bank(p, b),
                                            eh[:, b * BANK:(b + 1) * BANK], ALU.subtract).then_inc(e2_lo, 1)

            def weigh(p, i, gr):
                dve.wait_ge(pv2, count(p, i, GROUPS, gr + 1))
                pv = bank(p, 3)[:, 0:2 * GH * D1].rearrange("p (t h d) -> p t h d", t=TILES, h=GH)
                sums = rs[:].rearrange("p (t h) -> p t h", t=TILES)
                nc.vector.reciprocal(sums, pv[:, :, :, L1D]).then_inc(recip2, 1)
                dve.wait_ge(recip2, count(p, i, GROUPS, gr + 1))
                nc.vector.tensor_tensor(
                    o2[:, :, gr * GH * L1D:(gr + 1) * GH * L1D].rearrange("p t (h d) -> p t h d", h=GH),
                    pv[:, :, :, 0:L1D], sums.unsqueeze(3).to_broadcast([P, TILES, GH, L1D]),
                    ALU.mult).then_inc(o2_done, 1)

            def out_split(p, i):
                low_part(p, i, 2, bank(p, 1), o2_hi, o2_lo)

            def out_project(p, i):
                dve.wait_ge(res_done, count(p, i, 1, 1))
                dve.wait_ge(out_done, count(p, i, 1, 1))
                nc.vector.scalar_tensor_tensor(t3[:].rearrange("p t c -> p (t c)"), bank(p, 1), 1.0 / (S * S),
                                               res[p][:].rearrange("p t c -> p (t c)"), ALU.mult,
                                               ALU.add).then_inc(t3_done, 1)

            def norm_channels(p, i):
                normalise(p, i, 2, t3)

            def gate_logits(p, i):
                low_part(p, i, 2, bank(p, 1), n3_hi, n3_lo)

                def step(ins, n):
                    ins.then_inc(gate_step, 1)
                    dve.wait_ge(gate_step, count(p, i, 9, n))

                grid = [P, TILES, EXPERTS, EXPERTS]
                of, against = lg[:].unsqueeze(3).to_broadcast(grid), lg[:].unsqueeze(2).to_broadcast(grid)
                pairs = lambda t: t[:].rearrange("p t (e j) -> p t e j", e=EXPERTS)
                before = const("before").unsqueeze(1).to_broadcast([P, TILES, EXPERTS * EXPERTS])
                dve.wait_ge(logits, count(p, i, 1, 1))
                step(nc.vector.tensor_copy(lg[:], bank(p, 1)[:, 0:TILES * EXPERTS]
                                           .rearrange("p (t e) -> p t e", t=TILES)), 1)
                nc.vector.tensor_reduce(g1[:, 0:TILES], lg[:], op=ALU.max, axis=AX)
                nc.vector.tensor_tensor(pairs(cmp), against, of, ALU.is_gt)
                step(nc.vector.tensor_tensor(pairs(eq), against, of, ALU.is_equal), 2)
                nc.vector.tensor_tensor(gate[:], lg[:], g1[:, 0:TILES].unsqueeze(2).to_broadcast([P, TILES, EXPERTS]),
                                        ALU.subtract).then_inc(gate_max, 1)
                step(nc.vector.tensor_tensor(eq[:], eq[:], before, ALU.mult), 3)
                step(nc.vector.tensor_tensor(cmp[:], cmp[:], eq[:], ALU.add), 4)
                step(nc.vector.tensor_reduce(rank[:], pairs(cmp), op=ALU.add, axis=AX), 5)
                dve.wait_ge(gate_exp, count(p, i, 1, 1))
                step(nc.vector.scalar_tensor_tensor(gate[:], rank[:], 2.0, gate[:], ALU.is_lt, ALU.mult), 6)
                step(nc.vector.tensor_reduce(g1[:, 0:TILES], gate[:], op=ALU.add, axis=AX), 7)
                step(nc.vector.reciprocal(g1[:, TILES:2 * TILES], g1[:, 0:TILES]), 8)
                step(nc.vector.scalar_tensor_tensor(
                    gate[:], gate[:], 1.0 / S,
                    g1[:, TILES:2 * TILES].unsqueeze(2).to_broadcast([P, TILES, EXPERTS]), ALU.mult,
                    ALU.mult), 9)

            def expert(p, i, e):
                dve.wait_ge(expert_done, count(p, i, EXPERTS, e + 1))
                if e == 0:
                    freed(dve, stored[p], i * 16)
                for t in range(TILES):
                    if e:
                        dve.wait_ge(acc_done, count(p, i, EXPERTS * 2, (e - 1) * 2 + t + 1))
                    nc.vector.scalar_tensor_tensor(acc[p][:, t, :], bank(p, expert_bank(e))[:, t * C:(t + 1) * C],
                                                   gate[:, t, e:e + 1], (t3 if e == 0 else acc[p])[:, t, :],
                                                   ALU.mult, ALU.add).then_inc(acc_done, 1)

            for h in range(HALVES):
                nc.vector.bn_aggr(bn[:, h, 0:2], zst[:, h].rearrange("p b s -> p (b s)")).then_inc(bn_step, 1)
            dve.wait_ge(bn_step, 2)
            nc.vector.tensor_scalar(bn[:, :, 2], bn[:, :, 1], EPS, None, ALU.add).then_inc(bn_step, 1)
            dve.wait_ge(bn_step, 4)
            nc.vector.tensor_tensor(bn[:, :, 3], bn[:, :, 2], col("bng", 0, 2), ALU.mult).then_inc(bn_step, 1)
            dve.wait_ge(bn_step, 5)
            nc.vector.tensor_tensor(bn[:, :, 5], bn[:, :, 0], bn[:, :, 3], ALU.mult).then_inc(bn_step, 1)
            dve.wait_ge(bn_step, 6)
            nc.vector.tensor_tensor(bn[:, :, 4], col("bnb", 0, 2), bn[:, :, 5], ALU.subtract).then_inc(bn_step, 2)
            run(dve, {"tokens": statistics(0, t1, t1_done), ("to_channels", MLP): mlp_channels, "narrow": narrow,
                      ("statistics", QKV): statistics(1, t2, t2_done), ("to_channels", QKV): qkv_channels,
                      "rotate": rotate, "stack": stack, "values": values, "scores": scores, "turn": turn,
                      "weigh": weigh, "out_split": out_split, "out_project": out_project,
                      ("statistics", MOE): statistics(2, t3, t3_done), "norm_channels": norm_channels,
                      "logits": gate_logits, "expert": expert})


def constants():
    n = np.arange(WS)
    d = np.cos((2 * n[None, :] + 1) * n[:, None] * np.pi / (2 * WS))
    d[0] *= np.sqrt(1.0 / WS)
    d[1:] *= np.sqrt(2.0 / WS)
    d = d.astype(np.float32)
    kr = np.kron(d, d)
    kd = np.kron(np.eye(2, dtype=np.float32), kr)
    c = np.zeros((P, NCST), np.float32)

    def put(name, x):
        c[:, CST[name][0]:CST[name][0] + CST[name][1]] = x

    put("ident", np.eye(P))
    put("dct", kd.T)
    put("idct", kd)
    put("dcsum", kr.astype(np.float64).sum(0)[None, :])
    put("causal", np.where(np.arange(P)[None, :] > np.arange(P)[:, None], -1e30, 0.0))
    put("before", (np.arange(EXPERTS)[None, :] < np.arange(EXPERTS)[:, None]).reshape(1, -1))
    inv = (1.0 / 10000.0 ** (np.arange(0, L1D, 2, dtype=np.float32) / np.float32(L1D))).astype(np.float32)
    ang = np.tile((np.arange(TOK, dtype=np.float32)[None, :] * inv[:, None]).astype(np.float64), (L1H, 1))
    put("cos", np.cos(ang))
    put("sin", np.concatenate([-np.sin(ang), np.sin(ang)], 1))
    return c


def halves(w):
    return w.reshape(-1, P, w.shape[1]).transpose(1, 0, 2)


def layouts(v):
    g = lambda n: np.asarray(v[n])
    L = lambda n: g("L0_conv_" + n)
    cols = lambda x: x.reshape(-1, P).T
    r = {}
    x = g("x")
    xw = x.reshape(B, C, 2, WS, 2, WS).transpose(0, 4, 3, 5, 2, 1)
    r["xw"] = xw.reshape(B * P, TILES, C)
    r["xc"] = x.reshape(B, HALVES, P, TOK).transpose(0, 2, 1, 3).reshape(B * P, HALVES, TOK)
    parts = {"bqk": ["a1_bq", "a1_bk", "a2_bq", "a2_bk"], "nw": ["n2_w", "n1_w"], "nb": ["n2_b", "n1_b"],
             "bv": ["a1_bv", "a2_bv"], "bo": ["a1_bo", "a2_bo"], "c1b": ["c1_b"], "c2b": ["c2_b"], "bng": ["bn_g"],
             "bnb": ["bn_b"], "n3w": ["n3_w"], "n3b": ["n3_b"], "fc1b": ["fc1_b"]}
    r["vec"] = np.concatenate([cols(L(n)) for k in VEC for n in parts[k]], 1)
    stack = lambda ws: np.concatenate([halves(w).reshape(P, -1) for w in ws], 1)
    r["wqk"] = stack([L(n).T for n in ("a1_wq", "a1_wk", "a2_wq", "a2_wk")])
    r["wv"] = stack([L(n).T for n in ("a1_wv", "a2_wv")])
    r["wo"] = stack([L(n) for n in ("a1_wo", "a2_wo")]).reshape(P, 2, 2, C)
    c1 = L("c1_w")[:, :, 0, 0]
    r["c1"] = stack([c1[:, :C].T, c1[:, C:].T]).reshape(P, 2, 2, C)
    c2 = L("c2_w")
    r["wconv"] = stack([c2[:, :, t // 3, t % 3].T for t in range(TAPS)])
    r["wfc1"], r["wfc2"] = stack([L("fc1_w").T]), stack([L("fc2_w").T])
    w = g("L1_attn_w_qkv")
    order = lambda m: m.reshape(C, L1H, 2, 8).transpose(0, 2, 1, 3).reshape(C, C)
    r["wqkv"] = stack([order(w[:, :C]), order(w[:, C:2 * C]), w[:, 2 * C:]])
    r["wout"] = stack([g("L1_attn_w_out")])
    r["wgate"] = stack([g("L1_ffn_gate_w").T])
    r["wexp"] = stack([e.T for e in g("L1_ffn_expert_w")])
    r["fc2b"] = np.tile(L("fc2_b"), (P, 1))
    rel = (np.arange(0, (2 * WS - 1) * WS, 2 * WS - 1)[:, None] + np.arange(WS)[None, :]).reshape(1, -1)
    idx = (rel + rel.T)[:, ::-1]
    tabs = [L(n)[idx].reshape(WTOK, WTOK, 2, 4).transpose(0, 3, 2, 1).reshape(WTOK, 4, P)
            for n in ("a1_bias", "a2_bias")]
    r["relb"] = np.concatenate([np.stack(tabs, 1)] * 2, 0)
    r["cst"] = constants()
    return {n: np.ascontiguousarray(m) for n, m in r.items()}


def kernel(**inputs):
    import concourse.bacc as bacc
    from concourse.bass_utils import run_bass_kernel_spmd as run

    nc = bacc.Bacc("TRN2", target_bir_lowering=False, num_devices=1)
    arrays = layouts(inputs)
    a = {n: nc.dram_tensor("in_" + n, m.shape, mybir.dt.from_np(m.dtype), kind="ExternalInput").ap()
         for n, m in arrays.items()}
    out = nc.dram_tensor("out", (B * P, TILES, C), mybir.dt.float32, kind="ExternalOutput").ap()
    build(nc, a, out)
    r = run(nc, [{"in_" + n: m for n, m in arrays.items()}], core_ids=[0])
    got = r.results[0]["out"].reshape(B, P, TILES, C).transpose(0, 3, 2, 1)
    return np.ascontiguousarray(got).reshape(B, C, HW, HW)
```

```python
from contextlib import ExitStack

import concourse.bass as bass
import numpy as np
from concourse import mybir

B, C, HW = 8, 256, 16
TOK = HW * HW
P = 128
HALVES = C // P
TILES = TOK // P
WS = 8
WTOK = WS * WS
NH, HD = 8, 32
HID = 512
L1H, L1D = 16, 16
EXPERTS = 8
PAD = HW + 2
TAPS = 9
GROUPS, GH = 4, 4
S = 256.0
YS = 16.0
EPS = 1e-5
BANK = 512
ITERS = B // 2

VEC = {}
for _name, _n in (("bqk", 8), ("nw", 4), ("nb", 4), ("bv", 4), ("bo", 4), ("c1b", 2), ("c2b", 2), ("bng", 2),
                  ("bnb", 2), ("n3w", 2), ("n3b", 2), ("fc1b", 4)):
    VEC[_name] = (sum(n for _, n in VEC.values()), _n)
NVEC = sum(n for _, n in VEC.values())
CST = {}
for _name, _n in (("ident", P), ("dct", P), ("idct", P), ("dcsum", WTOK), ("causal", P), ("before", 64),
                  ("cos", TOK), ("sin", 2 * TOK)):
    CST[_name] = (sum(n for _, n in CST.values()), _n)
NCST = sum(n for _, n in CST.values())
W_FIRST = {"wqk": 4 * 2 * C, "wv": 2 * 2 * C}
W_CONV = TAPS * 2 * C
W_SECOND = {"wfc1": 2 * HID, "wfc2": 4 * C, "wqkv": 3 * 2 * C, "wout": 2 * C, "wgate": 2 * EXPERTS,
            "wexp": EXPERTS * 2 * C}
CHUNK = 1024
STAGES = 3
CONV_CHUNKS = 6
CONV_CHUNK = W_CONV // CONV_CHUNKS
SECOND_CHUNKS = B - 2
SECOND_CHUNK = sum(W_SECOND.values()) // SECOND_CHUNKS
assert CONV_CHUNKS * CONV_CHUNK == W_CONV and SECOND_CHUNKS * SECOND_CHUNK == sum(W_SECOND.values())


def build(nc, a, out):
    f32, f16, bf16 = mybir.dt.float32, mybir.dt.float16, mybir.dt.bfloat16
    ALU, ACT, AX = mybir.AluOpType, mybir.ActivationFunctionType, mybir.AxisListType.X
    ds = bass.ds
    scratch = nc.dram_tensor("rope_scratch", [2, 2, 4, P, TOK], f16, kind="Internal").ap()

    keep = ExitStack()
    with keep:
        def sb(stack, name, shape, dt=f32):
            return stack.enter_context(nc.sbuf_tensor(name, shape, dt))

        in_use = []

        def sem(name):
            in_use.append(nc.alloc_semaphore(name=name))
            return in_use[-1]

        def sems(name):
            return [sem(f"{name}{p}") for p in range(2)]

        def release_sems():
            nc.clear_and_free_semaphores(list(in_use))
            in_use.clear()
            nc.all_engine_barrier()

        vec = sb(keep, "vec", [P, NVEC])
        cst = sb(keep, "cst", [P, NCST])
        sbqk = sb(keep, "sbqk", [P, 8])
        identb = sb(keep, "identb", [P, P], bf16)
        maskb = sb(keep, "maskb", [P, P], bf16)
        fc2b = sb(keep, "fc2b", [P, C])
        z = sb(keep, "z", [P, HALVES, B * TOK])
        zst = sb(keep, "zst", [P, HALVES, B, 6])
        small = sb(keep, "small", [P, 64])
        hi, lo = {}, {}
        second = [sb(keep, f"second{x}", [P, SECOND_CHUNKS * SECOND_CHUNK], f16) for x in "hl"]
        c0 = 0
        for name, n in W_SECOND.items():
            hi[name], lo[name] = (x[:, c0:c0 + n] for x in second)
            c0 += n
        psum = [keep.enter_context(nc.psum_tensor(f"ps{p}", [P, 4 * BANK], f32)) for p in range(2)]

        def col(name, k=0, n=1):
            return vec[:, VEC[name][0] + k:VEC[name][0] + k + n]

        def const(name):
            return cst[:, CST[name][0]:CST[name][0] + CST[name][1]]

        ident = const("ident")

        def bank(p, k, n=1):
            return psum[p][:, k * BANK:(k + n) * BANK]

        shared = dict(f32=f32, f16=f16, ALU=ALU, ACT=ACT, AX=AX, ds=ds, hi=hi, lo=lo, psum=psum, sb=sb, sem=sem,
                      sems=sems, col=col, const=const, bank=bank, ident=ident, vec=vec, cst=cst, sbqk=sbqk, identb=identb,
                      maskb=maskb, fc2b=fc2b, z=z, zst=zst, small=small, scratch=scratch)
        first = ExitStack()
        with first:
            for name, n in {**W_FIRST, "wconv": W_CONV, "wfused": 2 * 2 * C}.items():
                hi[name], lo[name] = sb(first, name + "h", [P, n], f16), sb(first, name + "l", [P, n], f16)
            relb = sb(first, "relb", [P, 2, 4, P])
            ybias = sb(first, "ybias", [P, HALVES, WTOK])
            prepare(nc, a, {**shared, "relb": relb, "ybias": ybias})
            release_sems()
            windows(nc, a, {**shared, "relb": relb, "ybias": ybias, "second": second})
            release_sems()
        images(nc, a, out, shared)


FRONT, ATTENTION, BACK = range(3)
WINDOW_AHEAD = (1, 0, -1)
WINDOW_LOOP = (1, ITERS, (-1, 0))
WINDOW_ORDER = [
    (BACK, "out_channels"), (FRONT, "load"), (ATTENTION, "scores"), (BACK, "project"), (FRONT, "dct"),
    (FRONT, "normalise"), (ATTENTION, "turn"), (BACK, "conv", 0), (FRONT, "to_channels"), (BACK, "conv", 1),
    (FRONT, "values", 0), (ATTENTION, "weigh"), (FRONT, "values", 1), (FRONT, "queries", 1),
    (FRONT, "queries", 0), (FRONT, "weights")]
WINDOW_BEFORE = [
    (ATTENTION, "scores"), (BACK, "out_channels"), (FRONT, "load"), (BACK, "project"), (FRONT, "dct"),
    (BACK, "conv", 0), (ATTENTION, "turn"), (FRONT, "normalise"), (FRONT, "to_channels"), (ATTENTION, "weigh"),
    (FRONT, "values", 0), (FRONT, "values", 1), (FRONT, "queries", 1), (FRONT, "queries", 0),
    (FRONT, "weights"), (BACK, "conv", 1)]
WINDOW_AFTER = [
    (FRONT, "load"), (BACK, "out_channels"), (ATTENTION, "scores"), (BACK, "project"), (FRONT, "dct"),
    (FRONT, "normalise"), (FRONT, "to_channels"), (FRONT, "values", 0), (ATTENTION, "turn"), (BACK, "conv", 0),
    (FRONT, "values", 1), (FRONT, "queries", 1), (FRONT, "queries", 0), (FRONT, "weights"),
    (ATTENTION, "weigh"), (BACK, "conv", 1)]
WINDOW_ORDERS = (WINDOW_BEFORE, WINDOW_ORDER, WINDOW_AFTER)
MLP, QKV, CAUSAL, MOE = range(4)
IMAGE_AHEAD = (2, 1, 0, -1)
IMAGE_LOOP = (1, ITERS - 1, (0, 1))
IMAGE_ORDER = [
    (QKV, "statistics"), (MOE, "to_channels"), (MOE, "out_split"), (MLP, "load"), (CAUSAL, "scores", 0),
    (MOE, "out_project"), (QKV, "to_channels"), (MOE, "statistics"), (MLP, "tokens"), (CAUSAL, "turn", 0),
    (QKV, "rotate", 0), (CAUSAL, "scores", 1), (CAUSAL, "weigh", 0), (MOE, "norm_channels"),
    (MLP, "to_channels"), (MOE, "logits"), (CAUSAL, "turn", 1), (MLP, "widen"), (CAUSAL, "scores", 2),
    (MOE, "expert", 0), (QKV, "rotate", 1), (CAUSAL, "weigh", 1), (MOE, "expert", 1), (CAUSAL, "turn", 2),
    (QKV, "stack"), (MLP, "narrow"), (CAUSAL, "scores", 3), (MOE, "expert", 2), (CAUSAL, "weigh", 2),
    (MOE, "expert", 3), (MOE, "expert", 4), (CAUSAL, "turn", 3), (QKV, "values"), (MOE, "expert", 5),
    (CAUSAL, "weigh", 3), (MOE, "expert", 6), (MOE, "expert", 7), (MOE, "store")]
IMAGE_BEFORE = [
    (MOE, "to_channels"), (QKV, "statistics"), (MLP, "load"), (MOE, "out_split"), (CAUSAL, "scores", 0),
    (MOE, "out_project"), (MOE, "statistics"), (MOE, "norm_channels"), (QKV, "to_channels"),
    (CAUSAL, "turn", 0), (MLP, "tokens"), (CAUSAL, "scores", 1), (CAUSAL, "weigh", 0), (MOE, "logits"),
    (QKV, "rotate", 0), (MOE, "expert", 0), (CAUSAL, "turn", 1), (MLP, "to_channels"), (CAUSAL, "scores", 2),
    (QKV, "rotate", 1), (CAUSAL, "weigh", 1), (CAUSAL, "turn", 2), (QKV, "stack"), (MLP, "widen"),
    (CAUSAL, "scores", 3), (MOE, "expert", 1), (CAUSAL, "weigh", 2), (MOE, "expert", 2), (QKV, "values"),
    (CAUSAL, "turn", 3), (MLP, "narrow"), (MOE, "expert", 3), (MOE, "expert", 4), (CAUSAL, "weigh", 3),
    (MOE, "expert", 5), (MOE, "expert", 6), (MOE, "expert", 7), (MOE, "store")]
IMAGE_AFTER = [
    (MOE, "to_channels"), (MOE, "out_split"), (CAUSAL, "scores", 0), (QKV, "statistics"), (MOE, "out_project"),
    (MLP, "load"), (MLP, "tokens"), (MOE, "statistics"), (CAUSAL, "turn", 0), (MOE, "norm_channels"),
    (QKV, "to_channels"), (CAUSAL, "scores", 1), (QKV, "rotate", 0), (CAUSAL, "weigh", 0), (MLP, "to_channels"),
    (MOE, "logits"), (CAUSAL, "turn", 1), (MLP, "widen"), (MOE, "expert", 0), (CAUSAL, "scores", 2),
    (CAUSAL, "weigh", 1), (QKV, "rotate", 1), (MOE, "expert", 1), (CAUSAL, "turn", 2), (MLP, "narrow"),
    (MOE, "expert", 2), (QKV, "stack"), (CAUSAL, "scores", 3), (MOE, "expert", 3), (MOE, "expert", 4),
    (CAUSAL, "weigh", 2), (QKV, "values"), (CAUSAL, "turn", 3), (MOE, "expert", 5), (MOE, "expert", 6),
    (CAUSAL, "weigh", 3), (MOE, "expert", 7), (MOE, "store")]
IMAGE_ORDERS = (IMAGE_BEFORE, IMAGE_ORDER, IMAGE_AFTER)


def pipeline(eng, orders, ahead, loop, steps):
    before, inside, after = orders

    def part(k, c, order):
        for kind, name, *which in order:
            half, p = divmod(c + ahead[kind], 2)
            i = k + half if half else k
            step = steps.get((name, kind), steps.get(name))
            if step and not (isinstance(i, int) and not 0 <= 2 * i + p < B):
                step(p, i, *which)

    first, end, offsets = loop
    for c in range(-max(ahead), 2 * first + offsets[0]):
        part(0, c, before)
    with eng.Fori(first, end) as i:
        for c in offsets:
            part(i, c, inside)
    for c in range(2 * end + offsets[0], B - min(ahead)):
        part(0, c, after)


def freed(eng, semaphore, value):
    if not (isinstance(value, int) and value <= 0):
        eng.wait_ge(semaphore, value)


def split_products(nc, out_ap, pairs):
    n, done = len(pairs) * 3, 0
    for lhs, rhs in pairs:
        for x, w in ((0, 0), (1, 0), (0, 1)):
            last = nc.tensor.matmul(out_ap, lhs[x], rhs[w], start=done == 0, stop=done == n - 1)
            done += 1
    return last


def prepare(nc, a, k):
    f32, ALU, ACT = k["f32"], k["ALU"], k["ACT"]
    hi, lo, vec, cst, small, psum, sem = k["hi"], k["lo"], k["vec"], k["cst"], k["small"], k["psum"], k["sem"]
    col, const, bank = k["col"], k["const"], k["bank"]
    relb, ybias, sbqk, identb, maskb, fc2b = (k[n] for n in ("relb", "ybias", "sbqk", "identb", "maskb", "fc2b"))

    chunks = []
    for name, n in W_FIRST.items():
        for c0 in range(0, n, CHUNK):
            chunks.append((name, c0, min(CHUNK, n - c0)))

    with ExitStack() as own:
        stage = [k["sb"](own, f"stage{s}", [P, CHUNK]) for s in range(STAGES)]
        wo = k["sb"](own, "wo", [P, 2, 2, C])
        c1 = k["sb"](own, "c1", [P, 2, 2, C])
        wf = k["sb"](own, "wf", [P, 2, 2, C])
        chunk_loaded = [sem(f"chunk_loaded{s}") for s in range(STAGES)]
        vec_loaded, cst_loaded, wo_loaded, tiles_loaded = (sem(n) for n in
                                                           ("vec_loaded", "cst_loaded", "wo_loaded", "tiles_loaded"))
        chunk_hi, chunk_lo = sem("chunk_hi"), sem("chunk_lo")
        fused_done, wf_ready, wf_hi, fold_done, const_step = (sem(n) for n in
                                                              ("fused_done", "wf_ready", "wf_hi", "fold_done",
                                                               "const_step"))
        block = own.enter_context(nc.Block())

        @block.sync
        def _(sp):
            sp.dma_start(vec[:], a["vec"]).then_inc(vec_loaded, 16)
            sp.dma_start(wo[:], a["wo"]).then_inc(wo_loaded, 16)
            sp.dma_start(c1[:], a["c1"]).then_inc(wo_loaded, 16)
            for n, (name, c0, w) in enumerate(chunks):
                if n >= STAGES:
                    sp.wait_ge(chunk_lo, n - STAGES + 1)
                sp.dma_start(stage[n % STAGES][:, :w], a[name][:, c0:c0 + w]).then_inc(chunk_loaded[n % STAGES], 16)
            sp.dma_start(cst[:], a["cst"]).then_inc(cst_loaded, 16)
            sp.dma_start(relb[:], a["relb"]).then_inc(tiles_loaded, 16)
            sp.dma_start(fc2b[:], a["fc2b"]).then_inc(tiles_loaded, 16)
            sp.wait_ge(tiles_loaded, 32)

        @block.tensor
        def _(pe):
            pe.wait_ge(wo_loaded, 32)
            for at in range(2):
                for ih in range(HALVES):
                    for jh in range(HALVES):
                        last = nc.tensor.matmul(bank(0, at)[:, ih * C:(ih + 1) * C],
                                                wo[:, at, jh, ih * P:(ih + 1) * P], c1[:, at, jh, :],
                                                start=jh == 0, stop=jh == HALVES - 1)
                last.then_inc(fused_done, 1)
            pe.wait_ge(wf_ready, 2)
            pe.wait_ge(vec_loaded, 16)
            for at in range(2):
                for oh in range(HALVES):
                    o = slice(oh * P, (oh + 1) * P)
                    for n, (w, v) in enumerate([(wf, "bv"), (c1, "bo")]):
                        for h in range(HALVES):
                            last = nc.tensor.matmul(bank(0, 2)[:, at * 2 + oh:at * 2 + oh + 1], w[:, at, h, o],
                                                    col(v, at * 2 + h), start=(n, h) == (0, 0), stop=(n, h) == (1, 1))
            last.then_inc(fold_done, 1)

        @block.scalar
        def _(act):
            act.wait_ge(vec_loaded, 16)
            nc.scalar.activation(sbqk[:], col("bqk", 0, 8), ACT.Copy, scale=S).then_inc(const_step, 1)
            for n, (name, c0, w) in enumerate(chunks):
                act.wait_ge(chunk_loaded[n % STAGES], 16 * (n // STAGES + 1))
                nc.scalar.activation(hi[name][:, c0:c0 + w], stage[n % STAGES][:, :w], ACT.Copy,
                                     scale=S).then_inc(chunk_hi, 1)
            for at in range(2):
                act.wait_ge(fused_done, at + 1)
                nc.scalar.activation(wf[:, at], bank(0, at).rearrange("p (h o) -> p h o", h=HALVES),
                                     ACT.Copy).then_inc(wf_ready, 1)
            act.wait_ge(wf_ready, 2)
            nc.scalar.activation(hi["wfused"][:], wf[:].rearrange("p a h o -> p (a h o)"), ACT.Copy,
                                 scale=S).then_inc(wf_hi, 1)

        @block.vector
        def _(dve):
            for n, (name, c0, w) in enumerate(chunks):
                dve.wait_ge(chunk_hi, n + 1)
                nc.vector.scalar_tensor_tensor(lo[name][:, c0:c0 + w], stage[n % STAGES][:, :w], S,
                                               hi[name][:, c0:c0 + w], ALU.mult, ALU.subtract).then_inc(chunk_lo, 1)
            dve.wait_ge(wf_hi, 1)
            nc.vector.scalar_tensor_tensor(lo["wfused"][:], wf[:].rearrange("p a h o -> p (a h o)"), S,
                                           hi["wfused"][:], ALU.mult, ALU.subtract)
            dve.wait_ge(fold_done, 1)
            fold = small[:, 0:4]
            nc.vector.tensor_scalar(fold, bank(0, 2)[:, 0:4], YS, None, ALU.mult).then_inc(const_step, 1)
            dve.wait_ge(const_step, 2)
            nc.vector.scalar_tensor_tensor(small[:, 4:6], col("c1b", 0, 2), YS, small[:, 2:4], ALU.mult,
                                           ALU.add).then_inc(const_step, 1)
            dve.wait_ge(const_step, 3)
            dve.wait_ge(cst_loaded, 16)
            for oh in range(HALVES):
                nc.vector.tensor_scalar(ybias[:, oh, :], const("dcsum"), small[:, oh:oh + 1],
                                        small[:, 4 + oh:5 + oh], ALU.mult, ALU.add)
            nc.vector.tensor_copy(identb[:], const("ident"))
            nc.vector.tensor_copy(maskb[:], const("causal"))


def windows(nc, a, k):
    f32, f16, ALU, ACT, AX, ds = k["f32"], k["f16"], k["ALU"], k["ACT"], k["AX"], k["ds"]
    hi, lo, psum, sems, sb, sem = k["hi"], k["lo"], k["psum"], k["sems"], k["sb"], k["sem"]
    col, const, bank, ident = k["col"], k["const"], k["bank"], k["ident"]
    relb, ybias, sbqk, z, zst = (k[n] for n in ("relb", "ybias", "sbqk", "z", "zst"))
    R2 = range(2)
    SRC_Q = [0, 1, 1, 0]
    SRC_V = [1, 0]

    with ExitStack() as own:
        def pair(name, shape, dt=f32):
            return [sb(own, f"{name}{p}", shape, dt) for p in R2]

        def one(name, shape, dt=f32):
            return sb(own, name, shape, dt)

        xw = pair("xw", [P, TILES, C])
        st, mv, rstd = one("st", [P, 4, 6]), one("mv", [P, 4, 2]), one("rstd", [P, 4])
        xn = one("xn", [P, 2, TILES, C])
        affine = one("affine", [P, 2, HALVES, TOK])
        xh, xl = one("xh", [P, 2, HALVES, TOK], f16), one("xl", [P, 2, HALVES, TOK], f16)
        qkh, qkl = pair("qkh", [P, 4, HALVES, TOK], f16), pair("qkl", [P, 4, HALVES, TOK], f16)
        vh, vl = pair("vh", [P, 2, TILES, 4, 2 * HD], f16), pair("vl", [P, 2, TILES, 4, 2 * HD], f16)
        prob = one("prob", [P, 4 * BANK])
        mx = one("mx", [P, 32])
        eh, el = one("eh", [P, 4 * BANK], f16), one("el", [P, 4 * BANK], f16)
        sums, rs = one("sums", [P, 32]), one("rs", [P, 32])
        o = one("o", [P, 2, TILES, C])
        och, ocl = one("och", [P, 2 * BANK], f16), one("ocl", [P, 2 * BANK], f16)
        y = one("y", [P, HALVES, TOK])
        yh, yl = one("yh", [P, HALVES, PAD, PAD], f16), one("yl", [P, HALVES, PAD, PAD], f16)
        half, eps = sb(own, "half", [P, 4]), sb(own, "eps", [P, 4])
        stage = pair("weights_stage", [P, SECOND_CHUNK])

        (x_loaded, dct_done, stats_done, mv_done, eps_added, rstd_done, norm_done, tr_done, affine_done, xh_done,
         xl_done, qk_done, qkh_done, qkl_done, v_done, vh_done, vl_done, scores_done, biased, max_done, shifted,
         exp_done, et_done, eh_done, el_done, pv_done, recip_done, o_done, oc_done, och_done, ocl_done, y_done,
         y32_done, yh_done, yl_done, conv_done, z_done) = (
            sems(n) for n in ("x_loaded", "dct_done", "stats_done", "mv_done", "eps_added", "rstd_done", "norm_done",
                              "tr_done", "affine_done", "xh_done", "xl_done", "qk_done", "qkh_done", "qkl_done",
                              "v_done", "vh_done", "vl_done", "scores_done", "biased", "max_done", "shifted",
                              "exp_done", "et_done", "eh_done", "el_done", "pv_done", "recip_done", "o_done",
                              "oc_done", "och_done", "ocl_done", "y_done", "y32_done", "yh_done", "yl_done",
                              "conv_done", "z_done"))
        sum_done = sems("sum_done")
        pads_set, half_set = sem("pads_set"), sem("half_set")
        weights_loaded = sems("weights_loaded")
        weights_high, weights_split = sem("weights_high"), sem("weights_split")

        def weight_chunks(p, i):
            if isinstance(i, int) and i == 0:
                each = CONV_CHUNKS // 2
                for n in range(p * each, (p + 1) * each):
                    cols = slice(n * CONV_CHUNK, (n + 1) * CONV_CHUNK)
                    yield n, n % 2, n // 2, CONV_CHUNK, a["wconv"][:, cols], hi["wconv"][:, cols], lo["wconv"][:, cols]
            else:
                cols = ds(i * (2 * SECOND_CHUNK) + (p - 2) * SECOND_CHUNK, SECOND_CHUNK)
                yield (i * 2 + (p - 2 + CONV_CHUNKS), p, i + (CONV_CHUNKS // 2 - 1), SECOND_CHUNK,
                       a["second"][ds(i * (2 * P) + (p - 2) * P, P)],
                       k["second"][0][:, cols], k["second"][1][:, cols])

        def v_bank(p, at, t):
            return bank(p, at)[:, t * TOK:(t + 1) * TOK].rearrange("p (w r d) -> p w r d", w=2, r=4)

        def by_window(v, p, at, t):
            return v[p][:, at, t].rearrange("p r (w d) -> p w r d", w=2)

        def image(im, oh, wi):
            return im[:, oh, 1 + wi * WS:1 + (wi + 1) * WS, 1:1 + HW].rearrange("p x (j y) -> p j x y", j=2)

        def window_rows(t, oh, wi):
            return t[:, oh, wi * P:(wi + 1) * P].rearrange("p (j x y) -> p j x y", j=2, x=WS)

        block = own.enter_context(nc.Block())

        @block.sync
        def _(sp):
            def load(p, i):
                freed(sp, dct_done[p], i)
                freed(sp, norm_done[p], i)
                sp.dma_start(xw[p][:], a["xw"][ds((i * 2 + p) * P, P)]).then_inc(x_loaded[p], 16)

            def load_weights(p, i):
                for n, slot, _, width, src, _, _ in weight_chunks(p, i):
                    freed(sp, weights_split, n - 1)
                    sp.dma_start(stage[slot][:, 0:width], src).then_inc(weights_loaded[slot], 16)

            pipeline(sp, WINDOW_ORDERS, WINDOW_AHEAD, WINDOW_LOOP, {"load": load, "weights": load_weights})

        @block.tensor
        def _(pe):
            def dct(p, i):
                pe.wait_ge(x_loaded[p], i * 16 + 16)
                freed(pe, ocl_done[p], i)
                for t in range(TILES):
                    last = nc.tensor.matmul(bank(p, 0)[:, t * C:(t + 1) * C], const("dct"), xw[p][:, t, :],
                                            start=True, stop=True)
                last.then_inc(dct_done[p], 1)

            def to_channels(p, i):
                pe.wait_ge(norm_done[p], i + 1)
                for s in range(2):
                    for t in range(TILES):
                        for h in range(HALVES):
                            last = nc.tensor.transpose(bank(p, 1 - s)[:, h * TOK + t * P:h * TOK + (t + 1) * P],
                                                       xn[:, s, t, h * P:(h + 1) * P], ident)
                last.then_inc(tr_done[p], 1)

            def values(p, i, at):
                pe.wait_ge(xl_done[p], i + 1)
                for w in range(4):
                    for hh in range(2):
                        last = split_products(
                            nc, bank(p, at)[64 * hh:64 * hh + 64, w * P:(w + 1) * P],
                            [([x[:, SRC_V[at], h, w * WTOK:(w + 1) * WTOK] for x in (xh, xl)],
                              [wt["wv"][:, (at * 2 + h) * C + hh * P:(at * 2 + h) * C + (hh + 1) * P]
                               for wt in (hi, lo)]) for h in range(HALVES)])
                last.then_inc(v_done[p], 1)

            def queries(p, i, at):
                if at:
                    freed(pe, z_done[p], i * 2)
                for j in (2 * at, 2 * at + 1):
                    if at == 0:
                        pe.wait_ge(vl_done[p], i * 2 + j + 1)
                    for oh in range(HALVES):
                        last = split_products(
                            nc, bank(p, j)[:, oh * TOK:(oh + 1) * TOK],
                            [([w["wqk"][:, (j * 2 + h) * C + oh * P:(j * 2 + h) * C + (oh + 1) * P]
                               for w in (hi, lo)], [x[:, SRC_Q[j], h, :] for x in (xh, xl)])
                             for h in range(HALVES)])
                    last.then_inc(qk_done[p], 1)

            def scores(p, i):
                pe.wait_ge(qkl_done[p], i * 8 + 8)
                for at in range(2):
                    for t in range(TILES):
                        for w in range(2):
                            tok = slice(t * P + w * WTOK, t * P + (w + 1) * WTOK)
                            for hh in range(2):
                                c0 = (at * 2 + t) * P + hh * WTOK
                                for n, (q, kk) in enumerate([(qkh, qkh), (qkl, qkh), (qkh, qkl)]):
                                    for r in range(4):
                                        rows = slice(32 * r, 32 * r + 32)
                                        last = nc.tensor.matmul(
                                            bank(p, r)[64 * w:64 * w + 64, c0:c0 + WTOK],
                                            q[p][rows, at * 2, hh, tok], kk[p][rows, at * 2 + 1, hh, tok],
                                            start=n == 0, stop=n == 2)
                last.then_inc(scores_done[p], 1)

            def turn(p, i):
                pe.wait_ge(biased[p], i * 4 + 4)
                for at in range(2):
                    pe.wait_ge(exp_done[p], i * 2 + at + 1)
                    for t in range(TILES):
                        for r in range(4):
                            c0 = (at * 2 + t) * BANK + r * P
                            last = nc.tensor.transpose(psum[p][:, c0:c0 + P], prob[:, c0:c0 + P], ident)
                        last.then_inc(et_done[p], 1)

            def weigh(p, i):
                pe.wait_ge(half_set, 1)
                pe.wait_ge(el_done[p], i * 4 + 4)
                for at in range(2):
                    for t in range(TILES):
                        for r in range(4):
                            for n, (e, v) in enumerate([(eh, vh), (eh, vl), (el, vh)]):
                                for hh in range(2):
                                    rows = slice(64 * hh, 64 * hh + 64)
                                    c0 = (at * 2 + t) * BANK + r * P
                                    d0 = (t * 4 + r) * 2 * HD
                                    last = nc.tensor.matmul(bank(p, at * 2 + hh)[:, d0:d0 + 2 * HD],
                                                            e[rows, c0:c0 + P], v[p][rows, at, t, r],
                                                            start=n == 0, stop=n == 2)
                    last.then_inc(pv_done[p], 1)

            def out_channels(p, i):
                pe.wait_ge(o_done[p], i * 8 + 8)
                for h in range(HALVES):
                    for t in range(TILES):
                        nc.tensor.matmul(bank(p, 0)[:, h * TOK + t * P:h * TOK + (t + 1) * P],
                                         o[:, 0, t, h * P:(h + 1) * P], const("idct"), start=True, stop=True)
                for h in range(HALVES):
                    for t in range(TILES):
                        last = nc.tensor.transpose(bank(p, 1)[:, h * TOK + t * P:h * TOK + (t + 1) * P],
                                                   o[:, 1, t, h * P:(h + 1) * P], ident)
                last.then_inc(oc_done[p], 1)

            def project(p, i):
                pe.wait_ge(ocl_done[p], i + 1)
                for oh in range(HALVES):
                    last = split_products(
                        nc, bank(p, 2)[:, oh * TOK:(oh + 1) * TOK],
                        [([w["wfused"][:, n * C + oh * P:n * C + (oh + 1) * P] for w in (hi, lo)],
                          [x[:, n * TOK:(n + 1) * TOK] for x in (och, ocl)]) for n in range(4)])
                last.then_inc(y_done[p], 1)

            def conv(p, i, oh):
                if oh == 0:
                    pe.wait_ge(weights_split, CONV_CHUNKS)
                    pe.wait_ge(yl_done[p], i * 4 + 4)
                prods = []
                for tap in range(TAPS):
                    dy, dx = divmod(tap, 3)
                    for h in range(HALVES):
                        c0 = (tap * 2 + h) * C + oh * P
                        prods.append(([w["wconv"][:, c0:c0 + P] for w in (hi, lo)],
                                      [im[:, h, dy:dy + HW, dx:dx + HW] for im in (yh, yl)]))
                split_products(nc, bank(p, 2 + oh)[:, 0:TOK], prods).then_inc(conv_done[p], 1)

            pipeline(pe, WINDOW_ORDERS, WINDOW_AHEAD, WINDOW_LOOP, {
                "dct": dct, "to_channels": to_channels, "values": values, "queries": queries, "scores": scores,
                "turn": turn, "weigh": weigh, "out_channels": out_channels, "project": project, "conv": conv})

        @block.scalar
        def _(act):
            def to_channels(p, i):
                act.wait_ge(tr_done[p], i + 1)
                for s in range(2):
                    for h in range(HALVES):
                        nc.scalar.activation(affine[:, s, h, :], bank(p, 1 - s)[:, h * TOK:(h + 1) * TOK],
                                             ACT.Identity, scale=col("nw", s * 2 + h),
                                             bias=col("nb", s * 2 + h)).then_inc(affine_done[p], 1)
                act.wait_ge(affine_done[p], i * 4 + 4)
                nc.scalar.activation(xh[:], affine[:], ACT.Copy).then_inc(xh_done[p], 1)

            def values(p, i, at):
                act.wait_ge(v_done[p], i * 2 + at + 1)
                for t in range(TILES):
                    nc.scalar.activation(by_window(vh, p, at, t), v_bank(p, at, t), ACT.Copy)\
                        .then_inc(vh_done[p], 1)

            def queries(p, i, at):
                for j in (2 * at, 2 * at + 1):
                    act.wait_ge(qk_done[p], i * 4 + (j + 2) % 4 + 1)
                    for oh in range(HALVES):
                        nc.scalar.activation(qkh[p][:, j, oh, :], bank(p, j)[:, oh * TOK:(oh + 1) * TOK],
                                             ACT.Identity,
                                             bias=sbqk[:, j * 2 + oh:j * 2 + oh + 1]).then_inc(qkh_done[p], 1)

            def scores(p, i):
                for at in range(2):
                    act.wait_ge(shifted[p], i * 2 + at + 1)
                    e = prob[:, at * 2 * BANK:(at + 1) * 2 * BANK]
                    nc.scalar.activation(e, e, ACT.Exp).then_inc(exp_done[p], 1)

            def turn(p, i):
                for n in range(4):
                    act.wait_ge(et_done[p], i * 4 + n + 1)
                    nc.scalar.activation(eh[:, n * BANK:(n + 1) * BANK], bank(p, n), ACT.Copy)\
                        .then_inc(eh_done[p], 1)

            def out_channels(p, i):
                act.wait_ge(oc_done[p], i + 1)
                nc.scalar.activation(och[:], bank(p, 0, 2), ACT.Copy).then_inc(och_done[p], 1)

            def project(p, i):
                act.wait_ge(y32_done[p], i * 2 + 2)
                for oh in range(HALVES):
                    for wi in range(2):
                        nc.scalar.activation(image(yh, oh, wi), window_rows(y, oh, wi), ACT.Copy)\
                            .then_inc(yh_done[p], 1)

            def conv(p, i, oh):
                act.wait_ge(conv_done[p], i * 2 + oh + 1)
                nc.scalar.activation(z[:, oh, ds((i * 2 + p) * TOK, TOK)], bank(p, 2 + oh)[:, 0:TOK], ACT.Identity,
                                     scale=1.0 / (S * YS), bias=col("c2b", oh)).then_inc(z_done[p], 1)

            def weights(p, i):
                for _, slot, before, width, _, high, _ in weight_chunks(p, i):
                    act.wait_ge(weights_loaded[slot], before * 16 + 16)
                    nc.scalar.activation(high, stage[slot][:, 0:width], ACT.Copy,
                                         scale=S).then_inc(weights_high, 1)

            pipeline(act, WINDOW_ORDERS, WINDOW_AHEAD, WINDOW_LOOP, {
                "weights": weights,
                "to_channels": to_channels, "values": values, "queries": queries, "scores": scores, "turn": turn,
                "out_channels": out_channels, "project": project, "conv": conv})

        @block.gpsimd
        def _(pool):
            nc.gpsimd.memset(yh[:], 0.0).then_inc(pads_set, 1)
            nc.gpsimd.memset(yl[:], 0.0).then_inc(pads_set, 1)
            nc.gpsimd.memset(half[:], -0.5).then_inc(half_set, 1)
            nc.gpsimd.memset(eps[:], EPS).then_inc(half_set, 1)
            pool.wait_ge(half_set, 2)

            def dct(p, i):
                pool.wait_ge(mv_done[p], i + 1)
                nc.gpsimd.tensor_tensor(rstd[:], mv[:, :, 1], eps[:], ALU.add).then_inc(eps_added[p], 1)
                pool.wait_ge(eps_added[p], i + 1)
                nc.gpsimd.tensor_tensor(rstd[:], rstd[:], half[:], ALU.pow).then_inc(rstd_done[p], 1)

            pipeline(pool, WINDOW_ORDERS, WINDOW_AHEAD, WINDOW_LOOP, {"dct": dct})

        @block.vector
        def _(dve):
            dve.wait_ge(pads_set, 2)

            def tokens(p, s, t):
                return xw[p][:, t, :] if s == 0 else bank(p, 0)[:, t * C:(t + 1) * C]

            def dct(p, i):
                dve.wait_ge(x_loaded[p], i * 16 + 16)
                for s in range(2):
                    if s:
                        dve.wait_ge(dct_done[p], i + 1)
                    for t in range(TILES):
                        last = nc.vector.bn_stats(st[:, s * 2 + t, :], tokens(p, s, t))
                last.then_inc(stats_done[p], 1)
                dve.wait_ge(half_set, 1)
                dve.wait_ge(stats_done[p], i + 1)
                for n in range(4):
                    last = nc.vector.bn_aggr(mv[:, n, :], st[:, n, :])
                last.then_inc(mv_done[p], 1)

            def normalise(p, i):
                dve.wait_ge(rstd_done[p], i + 1)
                for s in range(2):
                    for t in range(TILES):
                        n = s * 2 + t
                        last = nc.vector.tensor_scalar(xn[:, s, t, :], tokens(p, s, t), mv[:, n, 0:1],
                                                       rstd[:, n:n + 1], ALU.subtract, ALU.mult)
                last.then_inc(norm_done[p], 1)

            def to_channels(p, i):
                dve.wait_ge(xh_done[p], i + 1)
                nc.vector.tensor_tensor(xl[:], affine[:], xh[:], ALU.subtract).then_inc(xl_done[p], 1)

            def values(p, i, at):
                dve.wait_ge(vh_done[p], i * 4 + at * 2 + 2)
                for t in range(TILES):
                    last = nc.vector.tensor_tensor(by_window(vl, p, at, t), v_bank(p, at, t),
                                                   by_window(vh, p, at, t), ALU.subtract)
                last.then_inc(vl_done[p], 1)

            def queries(p, i, at):
                for j in (2 * at, 2 * at + 1):
                    dve.wait_ge(qkh_done[p], i * 8 + (j + 2) % 4 * 2 + 2)
                    for oh in range(HALVES):
                        m = j * 2 + oh
                        nc.vector.scalar_tensor_tensor(qkl[p][:, j, oh, :], bank(p, j)[:, oh * TOK:(oh + 1) * TOK],
                                                       sbqk[:, m:m + 1], qkh[p][:, j, oh, :], ALU.add,
                                                       ALU.subtract).then_inc(qkl_done[p], 1)

            def scores(p, i):
                banks = psum[p][:].rearrange("p (r c) -> p r c", r=4)
                dve.wait_ge(scores_done[p], i + 1)
                for n in range(4):
                    nc.vector.scalar_tensor_tensor(
                        prob[:, n * BANK:(n + 1) * BANK].rearrange("p (r c) -> p r c", r=4),
                        banks[:, :, n * P:(n + 1) * P], HD ** -0.5 / (S * S), relb[:, n // 2], ALU.mult,
                        ALU.add).then_inc(biased[p], 1)
                rows = prob[:].rearrange("p (a g m) -> p a g m", a=2, m=WTOK)
                for at in range(2):
                    dve.wait_ge(biased[p], i * 4 + at * 2 + 2)
                    nc.vector.tensor_reduce(mx[:, at * 16:(at + 1) * 16], rows[:, at], op=ALU.max,
                                            axis=AX).then_inc(max_done[p], 1)
                for at in range(2):
                    dve.wait_ge(max_done[p], i * 2 + at + 1)
                    nc.vector.tensor_tensor(rows[:, at], rows[:, at],
                                            mx[:, at * 16:(at + 1) * 16].unsqueeze(2).to_broadcast([P, 16, WTOK]),
                                            ALU.subtract).then_inc(shifted[p], 1)

            def turn(p, i):
                rows = prob[:].rearrange("p (g m) -> p g m", m=WTOK)
                dve.wait_ge(exp_done[p], i * 2 + 2)
                nc.vector.tensor_reduce(sums[:], rows, op=ALU.add, axis=AX).then_inc(sum_done[p], 1)
                dve.wait_ge(sum_done[p], i + 1)
                nc.vector.reciprocal(rs[:], sums[:]).then_inc(recip_done[p], 1)
                for n in range(4):
                    dve.wait_ge(eh_done[p], i * 4 + n + 1)
                    nc.vector.tensor_tensor(el[:, n * BANK:(n + 1) * BANK], bank(p, n),
                                            eh[:, n * BANK:(n + 1) * BANK], ALU.subtract).then_inc(el_done[p], 1)

            def weigh(p, i):
                dve.wait_ge(recip_done[p], i + 1)
                inverse = rs[:].rearrange("p (a t r h) -> p a t r h", a=2, t=2, r=4)
                for at in range(2):
                    dve.wait_ge(pv_done[p], i * 2 + at + 1)
                    for hh in range(2):
                        pv = bank(p, at * 2 + hh).rearrange("p (t r w d) -> p t r w d", t=2, r=4, w=2)
                        for w in range(2):
                            rows = slice(64 * w, 64 * w + 64)
                            nc.vector.tensor_tensor(
                                o[rows, at, :, hh * P:(hh + 1) * P].rearrange("p t (r d) -> p t r d", r=4),
                                pv[rows, :, :, w, :],
                                inverse[rows, at, :, :, hh].unsqueeze(3).to_broadcast([64, 2, 4, HD]),
                                ALU.mult).then_inc(o_done[p], 1)

            def out_channels(p, i):
                dve.wait_ge(och_done[p], i + 1)
                nc.vector.tensor_tensor(ocl[:], bank(p, 0, 2), och[:], ALU.subtract).then_inc(ocl_done[p], 1)

            def project(p, i):
                dve.wait_ge(y_done[p], i + 1)
                for oh in range(HALVES):
                    nc.vector.scalar_tensor_tensor(
                        y[:, oh, :].rearrange("p (w t) -> p w t", w=4),
                        bank(p, 2)[:, oh * TOK:(oh + 1) * TOK].rearrange("p (w t) -> p w t", w=4), YS / (S * S),
                        ybias[:, oh, :].unsqueeze(1).to_broadcast([P, 4, WTOK]), ALU.mult,
                        ALU.add).then_inc(y32_done[p], 1)
                for oh in range(HALVES):
                    for wi in range(2):
                        dve.wait_ge(yh_done[p], i * 4 + oh * 2 + wi + 1)
                        nc.vector.tensor_tensor(image(yl, oh, wi), window_rows(y, oh, wi),
                                                image(yh, oh, wi), ALU.subtract).then_inc(yl_done[p], 1)

            def weights(p, i):
                for n, slot, _, width, _, high, low in weight_chunks(p, i):
                    dve.wait_ge(weights_high, n + 1)
                    nc.vector.scalar_tensor_tensor(low, stage[slot][:, 0:width], S, high, ALU.mult,
                                                   ALU.subtract).then_inc(weights_split, 1)

            def conv(p, i, oh):
                dve.wait_ge(z_done[p], i * 2 + oh + 1)
                nc.vector.bn_stats(zst[:, oh, ds(i * 2 + p, 1), :], z[:, oh, ds((i * 2 + p) * TOK, TOK)])

            pipeline(dve, WINDOW_ORDERS, WINDOW_AHEAD, WINDOW_LOOP, {
                "dct": dct, "normalise": normalise, "to_channels": to_channels, "values": values, "queries": queries,
                "scores": scores, "turn": turn, "weigh": weigh, "out_channels": out_channels, "project": project,
                "conv": conv, "weights": weights})


def images(nc, a, out, k):
    f32, f16, ALU, ACT, AX, ds = k["f32"], k["f16"], k["ALU"], k["ACT"], k["AX"], k["ds"]
    hi, lo, psum, sems, sb, sem = k["hi"], k["lo"], k["psum"], k["sems"], k["sb"], k["sem"]
    col, const, bank, ident = k["col"], k["const"], k["bank"], k["ident"]
    z, zst, identb, maskb, fc2b, scratch = (k[n] for n in ("z", "zst", "identb", "maskb", "fc2b", "scratch"))
    R2 = range(2)
    KSTACK = 3 * L1D
    GW = 3 * BANK
    D1 = L1D + 1
    SOFTMAX_SCALE = L1D ** -0.5 / (S * S)
    FIRST_IN_3 = 3
    LNS = {MLP: 0, QKV: 1, MOE: 2}

    def expert_bank(e):
        return 3 if e >= FIRST_IN_3 and e % 2 else 1

    def count(p, i, per, plus=0):
        return i * (2 * per) + (p * per + plus)

    with ExitStack() as own:
        def pair(name, shape, dt=f32):
            return [sb(own, f"{name}{p}", shape, dt) for p in R2]

        def one(name, shape, dt=f32):
            return sb(own, name, shape, dt)

        xc = one("xc", [P, HALVES, TOK])
        relu = one("relu", [P, HALVES, TOK])
        t1, t2, t3 = (one(n, [P, TILES, C]) for n in ("t1", "t2", "t3"))
        res, acc = pair("res", [P, TILES, C]), pair("acc", [P, TILES, C])
        tn = [one(f"tn{m}", [P, TILES, C]) for m in range(3)]
        st = [one(f"st2{m}", [P, 2, 6]) for m in range(3)]
        mv = [one(f"mv2{m}", [P, 2, 2]) for m in range(3)]
        rstd = [one(f"rstd2{m}", [P, 2]) for m in range(3)]
        ch = [one(f"ch{m}", [P, HALVES, TOK], f16) for m in range(3)]
        cl = [one(f"cl{m}", [P, HALVES, TOK], f16) for m in range(3)]
        wide = one("wide", [P, 4, TOK])
        hh, hl = one("hh", [P, 4, TOK], f16), one("hl", [P, 4, TOK], f16)
        rot, turned = one("rot", [P, 4, TOK]), one("turned", [P, 4, TOK])
        rh, rl = one("rh", [P, 4, TOK], f16), one("rl", [P, 4, TOK], f16)
        qs, ks = pair("qs", [KSTACK, L1H, TOK], f16), pair("ks", [KSTACK, L1H, TOK], f16)
        vh, vl = pair("v2h", [P, TILES, L1H, D1], f16), pair("v2l", [P, TILES, L1H, L1D], f16)
        prob = one("prob2", [P, GW])
        eh, el = one("e2h", [P, GW], f16), one("e2l", [P, GW], f16)
        mx, nmx, rs = (one(n, [P, 2 * GH]) for n in ("mx2", "nmx2", "rs2"))
        o2 = one("o2", [P, TILES, C])
        lg, gate, rank = (one(n, [P, TILES, EXPERTS]) for n in ("lg", "gate", "rank"))
        cmp, eq = (one(n, [P, TILES, EXPERTS * EXPERTS]) for n in ("cmp", "eq"))
        g1 = one("g1", [P, 2 * TILES])
        half, eps = one("half2", [P, 4]), one("eps2", [P, 4])
        bn = one("bn", [P, HALVES, 6])

        xc_loaded, spilled, stacked, stored = (sems(n) for n in ("xc_loaded", "spilled", "stacked", "stored"))
        ln = {n: [sem(f"ln_{n}{m}_") for m in range(3)] for n in ("stats", "mv", "eps", "rstd", "norm", "tr")}
        (relu_done, t0_done, t0_tr, t1_done, fc2_base, affine2, mlp_hi, mlp_lo, fc1_done, gelu_done, hid_hi, hid_lo,
         fc2_done, t2_done, res_done, n2_hi, n2_lo, qk2_done, v2_done, v2_hi, v2_lo, rope_a, rope_b, rot_done,
         rot_hi, rot_lo, scores2, max2, bias2, exp2, et2, e2_hi, e2_lo, pv2, recip2, o2_done, o2_tr, o2_hi, o2_lo,
         out_done, t3_done, n3_hi, n3_lo, logits, gate_step, gate_max, gate_exp, expert_done, acc_done, bn_step,
         half_set, ones_set) = (sem(n) for n in (
             "relu_done", "t0_done", "t0_tr", "t1_done", "fc2_base", "affine2", "mlp_hi", "mlp_lo", "fc1_done",
             "gelu_done", "hid_hi", "hid_lo", "fc2_done", "t2_done", "res_done", "n2_hi", "n2_lo", "qk2_done",
             "v2_done", "v2_hi", "v2_lo", "rope_a", "rope_b", "rot_done", "rot_hi", "rot_lo", "scores2", "max2",
             "bias2", "exp2", "et2", "e2_hi", "e2_lo", "pv2", "recip2", "o2_done", "o2_tr", "o2_hi", "o2_lo",
             "out_done", "t3_done", "n3_hi", "n3_lo", "logits", "gate_step", "gate_max", "gate_exp",
             "expert_done", "acc_done", "bn_step", "half_set2", "ones_set2"))

        def run(eng, steps):
            pipeline(eng, IMAGE_ORDERS, IMAGE_AHEAD, IMAGE_LOOP, steps)

        flat = lambda t: t[:].rearrange("p h t -> p (h t)")
        SCORE_BANKS = [((0, 1, 2, 3), P, 0), ((0, 1), TOK, P), ((2, 3), TOK, P)]

        block = own.enter_context(nc.Block())

        @block.sync
        def _(sp):
            def load(p, i):
                freed(sp, t0_tr, count(p, i, 1))
                sp.dma_start(xc[:], a["xc"][ds((i * 2 + p) * P, P)]).then_inc(xc_loaded[p], 16)

            def stack(p, i):
                for n, (part, ready) in enumerate(((rh, rot_hi), (rl, rot_lo))):
                    sp.wait_ge(ready, count(p, i, 1, 1))
                    sp.dma_start(scratch[p, n].rearrange("j c t -> c j t"), part[:]).then_inc(spilled[p], 16)
                freed(sp, scores2, count(p, i, GROUPS * 3, -GROUPS * 3))
                sp.wait_ge(spilled[p], i * 32 + 32)
                for qk, dst, parts in ((0, qs, (0, 1, 0)), (1, ks, (0, 0, 1))):
                    for n, part in enumerate(parts):
                        for j in range(2):
                            src = scratch[p, part, qk * 2 + j].rearrange("(h d) t -> d h t", h=L1H)
                            r0 = n * L1D + j * 8
                            sp.dma_start(dst[p][r0:r0 + 8], src).then_inc(stacked[p], 16)

            def store(p, i):
                sp.wait_ge(acc_done, count(p, i, EXPERTS * 2, EXPERTS * 2))
                sp.dma_start(out[ds((i * 2 + p) * P, P)], acc[p][:]).then_inc(stored[p], 16)

            run(sp, {"load": load, "stack": stack, "store": store})
            for p in R2:
                sp.wait_ge(stored[p], ITERS * 16)

        @block.tensor
        def _(pe):
            def to_channels(out_bank, src):
                for t in range(TILES):
                    for h in range(HALVES):
                        last = nc.tensor.transpose(out_bank[:, h * TOK + t * P:h * TOK + (t + 1) * P],
                                                   src[:, t, h * P:(h + 1) * P], ident)
                return last

            def token_product(out_bank, m, name, w0, width):
                for t in range(TILES):
                    last = split_products(
                        nc, out_bank[:, t * width:(t + 1) * width],
                        [([x[m][:, h, t * P:(t + 1) * P] for x in (ch, cl)],
                          [w[name][:, w0 + h * width:w0 + (h + 1) * width] for w in (hi, lo)])
                         for h in range(HALVES)])
                return last

            def tokens(p, i):
                pe.wait_ge(t0_done, count(p, i, 1, 1))
                for t in range(TILES):
                    for h in range(HALVES):
                        last = nc.tensor.transpose(bank(1 - p, 2)[:, t * C + h * P:t * C + (h + 1) * P],
                                                   xc[:, h, t * P:(t + 1) * P], ident)
                last.then_inc(t0_tr, 1)

            def mlp_channels(p, i):
                pe.wait_ge(ln["norm"][0], count(p, i, 1, 1))
                to_channels(bank(1 - p, 3), tn[0]).then_inc(ln["tr"][0], 1)

            def widen(p, i):
                pe.wait_ge(mlp_lo, count(p, i, 1, 1))
                for m in range(4):
                    last = split_products(
                        nc, bank(1 - p, 2, 2)[:, m * TOK:(m + 1) * TOK],
                        [([w["wfc1"][:, h * HID + m * P:h * HID + (m + 1) * P] for w in (hi, lo)],
                          [x[0][:, h, :] for x in (ch, cl)]) for h in range(HALVES)])
                    if m % 2:
                        last.then_inc(fc1_done, 1)

            def narrow(p, i):
                pe.wait_ge(hid_lo, count(p, i, 1, 1))
                for t in range(TILES):
                    last = split_products(
                        nc, bank(1 - p, 2)[:, t * C:(t + 1) * C],
                        [([x[:, m, t * P:(t + 1) * P] for x in (hh, hl)],
                          [w["wfc2"][:, m * C:(m + 1) * C] for w in (hi, lo)]) for m in range(4)])
                last.then_inc(fc2_done, 1)

            def qkv_channels(p, i):
                pe.wait_ge(ln["norm"][1], count(p, i, 1, 1))
                to_channels(bank(p, 0), tn[1]).then_inc(ln["tr"][1], 1)

            def rotate(p, i, j):
                if j == 0:
                    pe.wait_ge(n2_lo, count(p, i, 1, 1))
                else:
                    pe.wait_ge(rope_b, count(p, i, 4, 2))
                for m in range(HALVES):
                    last = split_products(
                        nc, bank(p, 0)[:, m * TOK:(m + 1) * TOK],
                        [([w["wqkv"][:, (j * 2 + h) * C + m * P:(j * 2 + h) * C + (m + 1) * P] for w in (hi, lo)],
                          [x[1][:, h, :] for x in (ch, cl)]) for h in range(HALVES)])
                last.then_inc(qk2_done, 1)

            def values(p, i):
                pe.wait_ge(rope_b, count(p, i, 4, 4))
                token_product(bank(p, 0), 1, "wqkv", 4 * C, C).then_inc(v2_done, 1)

            def scores(p, i, gr):
                if gr == 0:
                    pe.wait_ge(stacked[p], (i + 1) * 12 * 16)
                    pe.wait_ge(v2_lo, count(p, i, 1, 1))
                    freed(pe, acc_done, count(p, i, EXPERTS * 2, -EXPERTS * 2))
                    n = count(p, i, 1, 2)
                    pe.wait_ge(t2_done, min(n, B) if isinstance(n, int) else n)
                for b, (heads, keys, q0) in enumerate(SCORE_BANKS):
                    if gr:
                        pe.wait_ge(e2_lo, count(p, i, GROUPS * 3, (gr - 1) * 3 + b + 1))
                    for n, h in enumerate(heads):
                        nc.tensor.matmul(bank(p, b)[:, n * keys:(n + 1) * keys], qs[p][:, gr * GH + h, q0:q0 + P],
                                         ks[p][:, gr * GH + h, 0:keys], start=True, stop=False)
                        last = nc.tensor.matmul(bank(p, b)[:, (n + 1) * keys - P:(n + 1) * keys], identb[:],
                                                maskb[:], start=False, stop=True)
                    last.then_inc(scores2, 1)

            def turn(p, i, gr):
                for b in range(3):
                    pe.wait_ge(exp2, count(p, i, GROUPS * 3, gr * 3 + b + 1))
                    for n in range(4):
                        c0 = b * BANK + n * P
                        last = nc.tensor.transpose(psum[p][:, c0:c0 + P], prob[:, c0:c0 + P], ident)
                    last.then_inc(et2, 1)

            def weigh(p, i, gr):
                pe.wait_ge(e2_lo, count(p, i, GROUPS * 3, gr * 3 + 3))
                if gr:
                    pe.wait_ge(o2_done, count(p, i, GROUPS, gr))
                for t in range(TILES):
                    for h in range(GH):
                        c0 = (t * GH + h) * D1
                        blocks = [h * P] if t == 0 else [BANK + h * TOK, BANK + h * TOK + P]
                        for kt, e0 in enumerate(blocks):
                            for m, (e, v, w) in enumerate(((eh, vh, D1), (eh, vl, L1D), (el, vh, D1))):
                                last = nc.tensor.matmul(bank(p, 3)[:, c0:c0 + w], e[:, e0:e0 + P],
                                                        v[p][:, kt, gr * GH + h, 0:w], start=(kt, m) == (0, 0),
                                                        stop=(kt, m) == (len(blocks) - 1, 2))
                last.then_inc(pv2, 1)

            def out_channels(p, i):
                pe.wait_ge(o2_done, count(p, i, GROUPS, GROUPS))
                to_channels(bank(p, 1), o2).then_inc(o2_tr, 1)

            def out_project(p, i):
                pe.wait_ge(o2_lo, count(p, i, 1, 1))
                token_product(bank(p, 1), 2, "wout", 0, C).then_inc(out_done, 1)

            def norm_channels(p, i):
                pe.wait_ge(ln["norm"][2], count(p, i, 1, 1))
                to_channels(bank(p, 1), tn[2]).then_inc(ln["tr"][2], 1)

            def gate_logits(p, i):
                pe.wait_ge(n3_lo, count(p, i, 1, 1))
                token_product(bank(p, 1), 2, "wgate", 0, EXPERTS).then_inc(logits, 1)

            def expert(p, i, e):
                if e == 0:
                    pe.wait_ge(gate_step, count(p, i, 9, 1))
                elif e < FIRST_IN_3:
                    pe.wait_ge(acc_done, count(p, i, EXPERTS * 2, e * 2))
                elif e > FIRST_IN_3:
                    pe.wait_ge(acc_done, count(p, i, EXPERTS * 2, (e - 1) * 2))
                token_product(bank(p, expert_bank(e)), 2, "wexp", e * 2 * C, C).then_inc(expert_done, 1)

            run(pe, {"tokens": tokens, ("to_channels", MLP): mlp_channels, "widen": widen, "narrow": narrow,
                     ("to_channels", QKV): qkv_channels, "rotate": rotate, "values": values, "scores": scores,
                     "turn": turn, "weigh": weigh, ("to_channels", MOE): out_channels, "out_project": out_project,
                     "norm_channels": norm_channels, "logits": gate_logits, "expert": expert})

        @block.scalar
        def _(act):
            def high_part(m, src, done):
                nc.scalar.activation(flat(ch[m]), src, ACT.Copy).then_inc(done, 1)

            def load(p, i):
                freed(act, t0_done, count(p, i, 1))
                for h in range(HALVES):
                    nc.scalar.activation(relu[:, h, :], z[:, h, ds((i * 2 + p) * TOK, TOK)], ACT.Relu,
                                         scale=bn[:, h, 3:4], bias=bn[:, h, 4:5]).then_inc(relu_done, 1)

            def tokens(p, i):
                freed(act, t2_done, count(p, i, 1))
                act.wait_ge(t0_tr, count(p, i, 1, 1))
                nc.scalar.activation(t1[:].rearrange("p t c -> p (t c)"), bank(1 - p, 2),
                                     ACT.Copy).then_inc(t1_done, 1)

            def mlp_channels(p, i):
                freed(act, hid_lo, count(p, i, 1))
                act.wait_ge(ln["tr"][0], count(p, i, 1, 1))
                for h in range(HALVES):
                    nc.scalar.activation(wide[:, h, :], bank(1 - p, 3)[:, h * TOK:(h + 1) * TOK], ACT.Identity,
                                         scale=col("n3w", h), bias=col("n3b", h)).then_inc(affine2, 1)
                act.wait_ge(affine2, count(p, i, 2, 2))
                nc.scalar.activation(ch[0][:], wide[:, 0:2, :], ACT.Copy).then_inc(mlp_hi, 1)

            def widen(p, i):
                for m in range(4):
                    if m == 0:
                        act.wait_ge(mlp_lo, count(p, i, 1, 1))
                    act.wait_ge(fc1_done, count(p, i, 2, m // 2 + 1))
                    nc.scalar.activation(wide[:, m, :], bank(1 - p, 2, 2)[:, m * TOK:(m + 1) * TOK], ACT.Gelu,
                                         scale=1.0 / S, bias=col("fc1b", m)).then_inc(gelu_done, 1)
                act.wait_ge(gelu_done, count(p, i, 4, 4))
                nc.scalar.activation(hh[:], wide[:], ACT.Copy).then_inc(hid_hi, 1)

            def qkv_channels(p, i):
                act.wait_ge(ln["tr"][1], count(p, i, 1, 1))
                high_part(1, bank(p, 0), n2_hi)
                freed(act, t3_done, count(p, i, 1, -1))
                act.wait_ge(t2_done, count(p, i, 1, 1))
                nc.scalar.activation(res[p][:], t2[:], ACT.Copy).then_inc(res_done, 1)

            def stack(p, i):
                act.wait_ge(rot_done, count(p, i, 1, 1))
                nc.scalar.activation(rh[:], rot[:], ACT.Copy).then_inc(rot_hi, 1)

            def values(p, i):
                if isinstance(i, int) and i == 0:
                    act.wait_ge(ones_set, 2)
                freed(act, pv2, count(p, i, GROUPS, -GROUPS))
                act.wait_ge(v2_done, count(p, i, 1, 1))
                nc.scalar.activation(vh[p][:, :, :, 0:L1D],
                                     bank(p, 0).rearrange("p (t h d) -> p t h d", t=TILES, h=L1H),
                                     ACT.Copy).then_inc(v2_hi, 1)

            def scores(p, i, gr):
                for b, (heads, keys, _) in enumerate(SCORE_BANKS):
                    act.wait_ge(bias2, count(p, i, GROUPS * 3, gr * 3 + b + 1))
                    for n in range(len(heads)):
                        m = (0, 4, 6)[b] + n
                        c0 = b * BANK + n * keys
                        last = nc.scalar.activation(prob[:, c0:c0 + keys], psum[p][:, c0:c0 + keys], ACT.Exp,
                                                    scale=SOFTMAX_SCALE, bias=nmx[:, m:m + 1])
                    last.then_inc(exp2, 1)

            def turn(p, i, gr):
                for b in range(3):
                    act.wait_ge(et2, count(p, i, GROUPS * 3, gr * 3 + b + 1))
                    nc.scalar.activation(eh[:, b * BANK:(b + 1) * BANK], bank(p, b), ACT.Copy).then_inc(e2_hi, 1)

            def out_channels(p, i):
                act.wait_ge(o2_tr, count(p, i, 1, 1))
                high_part(2, bank(p, 1), o2_hi)

            def norm_channels(p, i):
                act.wait_ge(ln["tr"][2], count(p, i, 1, 1))
                high_part(2, bank(p, 1), n3_hi)

            def gate_logits(p, i):
                act.wait_ge(gate_max, count(p, i, 1, 1))
                nc.scalar.activation(gate[:], gate[:], ACT.Exp, scale=1.0 / S).then_inc(gate_exp, 1)

            act.wait_ge(bn_step, 8)
            run(act, {"load": load, "tokens": tokens, ("to_channels", MLP): mlp_channels, "widen": widen,
                      ("to_channels", QKV): qkv_channels, "stack": stack, "values": values, "scores": scores,
                      "turn": turn, ("to_channels", MOE): out_channels, "norm_channels": norm_channels,
                      "logits": gate_logits})

        @block.gpsimd
        def _(pool):
            def load(p, i):
                pool.wait_ge(xc_loaded[p], i * 16 + 16)
                pool.wait_ge(relu_done, count(p, i, 2, 2))
                nc.gpsimd.tensor_tensor(xc[:], xc[:], relu[:], ALU.add).then_inc(t0_done, 1)

            def deviation(m):
                def step(p, i):
                    pool.wait_ge(ln["mv"][m], count(p, i, 1, 1))
                    nc.gpsimd.tensor_tensor(rstd[m][:], mv[m][:, :, 1], eps[:, 0:2], ALU.add)\
                        .then_inc(ln["eps"][m], 1)
                    pool.wait_ge(ln["eps"][m], count(p, i, 1, 1))
                    nc.gpsimd.tensor_tensor(rstd[m][:], rstd[m][:], half[:, 0:2], ALU.pow).then_inc(ln["rstd"][m], 1)
                return step

            def mlp_channels(p, i):
                pool.wait_ge(ln["norm"][0], count(p, i, 1, 1))
                nc.gpsimd.tensor_tensor(t1[:], t1[:], fc2b[:].unsqueeze(1).to_broadcast([P, TILES, C]),
                                        ALU.add).then_inc(fc2_base, 1)
                pool.wait_ge(mlp_hi, count(p, i, 1, 1))
                nc.gpsimd.tensor_tensor(cl[0][:], wide[:, 0:2, :], ch[0][:], ALU.subtract).then_inc(mlp_lo, 1)

            def widen(p, i):
                pool.wait_ge(hid_hi, count(p, i, 1, 1))
                nc.gpsimd.tensor_tensor(hl[:], wide[:], hh[:], ALU.subtract).then_inc(hid_lo, 1)

            def stack(p, i):
                pool.wait_ge(rope_b, count(p, i, 4, 4))
                nc.gpsimd.tensor_tensor(rot[:], rot[:], turned[:], ALU.add).then_inc(rot_done, 1)

            nc.gpsimd.memset(half[:], -0.5).then_inc(half_set, 1)
            nc.gpsimd.memset(eps[:], EPS).then_inc(half_set, 1)
            for p in R2:
                nc.gpsimd.memset(vh[p][:], 1.0).then_inc(ones_set, 1)
            pool.wait_ge(half_set, 2)
            pool.wait_ge(bn_step, 3)
            nc.gpsimd.tensor_tensor(bn[:, :, 2], bn[:, :, 2], half[:, 0:2], ALU.pow).then_inc(bn_step, 1)
            run(pool, {"load": load, "tokens": deviation(0), ("to_channels", MLP): mlp_channels, "widen": widen,
                       ("statistics", QKV): deviation(1), ("statistics", MOE): deviation(2), "stack": stack})

        @block.vector
        def _(dve):
            def statistics(m, src, ready):
                def step(p, i):
                    dve.wait_ge(ready, count(p, i, 1, 1))
                    for t in range(TILES):
                        last = nc.vector.bn_stats(st[m][:, t, :], src[:, t, :])
                    last.then_inc(ln["stats"][m], 1)
                    dve.wait_ge(half_set, 1)
                    dve.wait_ge(ln["stats"][m], count(p, i, 1, 1))
                    for t in range(TILES):
                        last = nc.vector.bn_aggr(mv[m][:, t, :], st[m][:, t, :])
                    last.then_inc(ln["mv"][m], 1)
                return step

            def normalise(p, i, m, src):
                dve.wait_ge(ln["rstd"][m], count(p, i, 1, 1))
                for t in range(TILES):
                    last = nc.vector.tensor_scalar(tn[m][:, t, :], src[:, t, :], mv[m][:, t, 0:1],
                                                   rstd[m][:, t:t + 1], ALU.subtract, ALU.mult)
                last.then_inc(ln["norm"][m], 1)

            def low_part(p, i, m, src, high_done, done):
                dve.wait_ge(high_done, count(p, i, 1, 1))
                nc.vector.tensor_tensor(flat(cl[m]), src, flat(ch[m]), ALU.subtract).then_inc(done, 1)

            def mlp_channels(p, i):
                normalise(p, i, 0, t1)

            def narrow(p, i):
                freed(dve, res_done, count(p, i, 1))
                dve.wait_ge(fc2_base, count(p, i, 1, 1))
                dve.wait_ge(fc2_done, count(p, i, 1, 1))
                nc.vector.scalar_tensor_tensor(t2[:].rearrange("p t c -> p (t c)"), bank(1 - p, 2), 1.0 / S,
                                               t1[:].rearrange("p t c -> p (t c)"), ALU.mult,
                                               ALU.add).then_inc(t2_done, 1)

            def qkv_channels(p, i):
                normalise(p, i, 1, t2)
                low_part(p, i, 1, bank(p, 0), n2_hi, n2_lo)

            def rotate(p, i, j):
                dve.wait_ge(qk2_done, count(p, i, 2, j + 1))
                x = bank(p, 0).rearrange("p (m t) -> p m t", m=2)
                sin = const("sin").rearrange("p (m t) -> p m t", m=2)
                nc.vector.tensor_tensor(rot[:, 2 * j:2 * j + 2, :], x,
                                        const("cos").unsqueeze(1).to_broadcast([P, 2, TOK]),
                                        ALU.mult).then_inc(rope_a, 1)
                for m in range(2):
                    nc.vector.tensor_tensor(turned[:, 2 * j + m, :], x[:, 1 - m, :], sin[:, m, :],
                                            ALU.mult).then_inc(rope_b, 1)

            def stack(p, i):
                dve.wait_ge(rot_hi, count(p, i, 1, 1))
                nc.vector.tensor_tensor(rl[:], rot[:], rh[:], ALU.subtract).then_inc(rot_lo, 1)

            def values(p, i):
                dve.wait_ge(v2_hi, count(p, i, 1, 1))
                nc.vector.tensor_tensor(vl[p][:], bank(p, 0).rearrange("p (t h d) -> p t h d", t=TILES, h=L1H),
                                        vh[p][:, :, :, 0:L1D], ALU.subtract).then_inc(v2_lo, 1)

            def scores(p, i, gr):
                at = (slice(0, 4), slice(4, 6), slice(6, 8))
                for b, (heads, keys, _) in enumerate(SCORE_BANKS):
                    dve.wait_ge(scores2, count(p, i, GROUPS * 3, gr * 3 + b + 1))
                    nc.vector.tensor_reduce(mx[:, at[b]], bank(p, b).rearrange("p (h m) -> p h m", m=keys),
                                            op=ALU.max, axis=AX).then_inc(max2, 1)
                for b in range(3):
                    dve.wait_ge(max2, count(p, i, GROUPS * 3, gr * 3 + b + 1))
                    nc.vector.tensor_scalar(nmx[:, at[b]], mx[:, at[b]], -SOFTMAX_SCALE, None,
                                            ALU.mult).then_inc(bias2, 1)

            def turn(p, i, gr):
                for b in range(3):
                    dve.wait_ge(e2_hi, count(p, i, GROUPS * 3, gr * 3 + b + 1))
                    nc.vector.tensor_tensor(el[:, b * BANK:(b + 1) * BANK], bank(p, b),
                                            eh[:, b * BANK:(b + 1) * BANK], ALU.subtract).then_inc(e2_lo, 1)

            def weigh(p, i, gr):
                dve.wait_ge(pv2, count(p, i, GROUPS, gr + 1))
                pv = bank(p, 3)[:, 0:2 * GH * D1].rearrange("p (t h d) -> p t h d", t=TILES, h=GH)
                sums = rs[:].rearrange("p (t h) -> p t h", t=TILES)
                nc.vector.reciprocal(sums, pv[:, :, :, L1D]).then_inc(recip2, 1)
                dve.wait_ge(recip2, count(p, i, GROUPS, gr + 1))
                nc.vector.tensor_tensor(
                    o2[:, :, gr * GH * L1D:(gr + 1) * GH * L1D].rearrange("p t (h d) -> p t h d", h=GH),
                    pv[:, :, :, 0:L1D], sums.unsqueeze(3).to_broadcast([P, TILES, GH, L1D]),
                    ALU.mult).then_inc(o2_done, 1)

            def out_split(p, i):
                low_part(p, i, 2, bank(p, 1), o2_hi, o2_lo)

            def out_project(p, i):
                dve.wait_ge(res_done, count(p, i, 1, 1))
                dve.wait_ge(out_done, count(p, i, 1, 1))
                nc.vector.scalar_tensor_tensor(t3[:].rearrange("p t c -> p (t c)"), bank(p, 1), 1.0 / (S * S),
                                               res[p][:].rearrange("p t c -> p (t c)"), ALU.mult,
                                               ALU.add).then_inc(t3_done, 1)

            def norm_channels(p, i):
                normalise(p, i, 2, t3)

            def gate_logits(p, i):
                low_part(p, i, 2, bank(p, 1), n3_hi, n3_lo)

                def step(ins, n):
                    ins.then_inc(gate_step, 1)
                    dve.wait_ge(gate_step, count(p, i, 9, n))

                grid = [P, TILES, EXPERTS, EXPERTS]
                of, against = lg[:].unsqueeze(3).to_broadcast(grid), lg[:].unsqueeze(2).to_broadcast(grid)
                pairs = lambda t: t[:].rearrange("p t (e j) -> p t e j", e=EXPERTS)
                before = const("before").unsqueeze(1).to_broadcast([P, TILES, EXPERTS * EXPERTS])
                dve.wait_ge(logits, count(p, i, 1, 1))
                step(nc.vector.tensor_copy(lg[:], bank(p, 1)[:, 0:TILES * EXPERTS]
                                           .rearrange("p (t e) -> p t e", t=TILES)), 1)
                nc.vector.tensor_reduce(g1[:, 0:TILES], lg[:], op=ALU.max, axis=AX)
                nc.vector.tensor_tensor(pairs(cmp), against, of, ALU.is_gt)
                step(nc.vector.tensor_tensor(pairs(eq), against, of, ALU.is_equal), 2)
                nc.vector.tensor_tensor(gate[:], lg[:], g1[:, 0:TILES].unsqueeze(2).to_broadcast([P, TILES, EXPERTS]),
                                        ALU.subtract).then_inc(gate_max, 1)
                step(nc.vector.tensor_tensor(eq[:], eq[:], before, ALU.mult), 3)
                step(nc.vector.tensor_tensor(cmp[:], cmp[:], eq[:], ALU.add), 4)
                step(nc.vector.tensor_reduce(rank[:], pairs(cmp), op=ALU.add, axis=AX), 5)
                dve.wait_ge(gate_exp, count(p, i, 1, 1))
                step(nc.vector.scalar_tensor_tensor(gate[:], rank[:], 2.0, gate[:], ALU.is_lt, ALU.mult), 6)
                step(nc.vector.tensor_reduce(g1[:, 0:TILES], gate[:], op=ALU.add, axis=AX), 7)
                step(nc.vector.reciprocal(g1[:, TILES:2 * TILES], g1[:, 0:TILES]), 8)
                step(nc.vector.scalar_tensor_tensor(
                    gate[:], gate[:], 1.0 / S,
                    g1[:, TILES:2 * TILES].unsqueeze(2).to_broadcast([P, TILES, EXPERTS]), ALU.mult,
                    ALU.mult), 9)

            def expert(p, i, e):
                dve.wait_ge(expert_done, count(p, i, EXPERTS, e + 1))
                if e == 0:
                    freed(dve, stored[p], i * 16)
                for t in range(TILES):
                    if e:
                        dve.wait_ge(acc_done, count(p, i, EXPERTS * 2, (e - 1) * 2 + t + 1))
                    nc.vector.scalar_tensor_tensor(acc[p][:, t, :], bank(p, expert_bank(e))[:, t * C:(t + 1) * C],
                                                   gate[:, t, e:e + 1], (t3 if e == 0 else acc[p])[:, t, :],
                                                   ALU.mult, ALU.add).then_inc(acc_done, 1)

            for h in range(HALVES):
                nc.vector.bn_aggr(bn[:, h, 0:2], zst[:, h].rearrange("p b s -> p (b s)")).then_inc(bn_step, 1)
            dve.wait_ge(bn_step, 2)
            nc.vector.tensor_scalar(bn[:, :, 2], bn[:, :, 1], EPS, None, ALU.add).then_inc(bn_step, 1)
            dve.wait_ge(bn_step, 4)
            nc.vector.tensor_tensor(bn[:, :, 3], bn[:, :, 2], col("bng", 0, 2), ALU.mult).then_inc(bn_step, 1)
            dve.wait_ge(bn_step, 5)
            nc.vector.tensor_tensor(bn[:, :, 5], bn[:, :, 0], bn[:, :, 3], ALU.mult).then_inc(bn_step, 1)
            dve.wait_ge(bn_step, 6)
            nc.vector.tensor_tensor(bn[:, :, 4], col("bnb", 0, 2), bn[:, :, 5], ALU.subtract).then_inc(bn_step, 2)
            run(dve, {"tokens": statistics(0, t1, t1_done), ("to_channels", MLP): mlp_channels, "narrow": narrow,
                      ("statistics", QKV): statistics(1, t2, t2_done), ("to_channels", QKV): qkv_channels,
                      "rotate": rotate, "stack": stack, "values": values, "scores": scores, "turn": turn,
                      "weigh": weigh, "out_split": out_split, "out_project": out_project,
                      ("statistics", MOE): statistics(2, t3, t3_done), "norm_channels": norm_channels,
                      "logits": gate_logits, "expert": expert})


def constants():
    n = np.arange(WS)
    d = np.cos((2 * n[None, :] + 1) * n[:, None] * np.pi / (2 * WS))
    d[0] *= np.sqrt(1.0 / WS)
    d[1:] *= np.sqrt(2.0 / WS)
    d = d.astype(np.float32)
    kr = np.kron(d, d)
    kd = np.kron(np.eye(2, dtype=np.float32), kr)
    c = np.zeros((P, NCST), np.float32)

    def put(name, x):
        c[:, CST[name][0]:CST[name][0] + CST[name][1]] = x

    put("ident", np.eye(P))
    put("dct", kd.T)
    put("idct", kd)
    put("dcsum", kr.astype(np.float64).sum(0)[None, :])
    put("causal", np.where(np.arange(P)[None, :] > np.arange(P)[:, None], -1e30, 0.0))
    put("before", (np.arange(EXPERTS)[None, :] < np.arange(EXPERTS)[:, None]).reshape(1, -1))
    inv = (1.0 / 10000.0 ** (np.arange(0, L1D, 2, dtype=np.float32) / np.float32(L1D))).astype(np.float32)
    ang = np.tile((np.arange(TOK, dtype=np.float32)[None, :] * inv[:, None]).astype(np.float64), (L1H, 1))
    put("cos", np.cos(ang))
    put("sin", np.concatenate([-np.sin(ang), np.sin(ang)], 1))
    return c


def halves(w):
    return w.reshape(-1, P, w.shape[1]).transpose(1, 0, 2)


def layouts(v):
    g = lambda n: np.asarray(v[n])
    L = lambda n: g("L0_conv_" + n)
    cols = lambda x: x.reshape(-1, P).T
    r = {}
    x = g("x")
    xw = x.reshape(B, C, 2, WS, 2, WS).transpose(0, 4, 3, 5, 2, 1)
    r["xw"] = xw.reshape(B * P, TILES, C)
    r["xc"] = x.reshape(B, HALVES, P, TOK).transpose(0, 2, 1, 3).reshape(B * P, HALVES, TOK)
    parts = {"bqk": ["a1_bq", "a1_bk", "a2_bq", "a2_bk"], "nw": ["n2_w", "n1_w"], "nb": ["n2_b", "n1_b"],
             "bv": ["a1_bv", "a2_bv"], "bo": ["a1_bo", "a2_bo"], "c1b": ["c1_b"], "c2b": ["c2_b"], "bng": ["bn_g"],
             "bnb": ["bn_b"], "n3w": ["n3_w"], "n3b": ["n3_b"], "fc1b": ["fc1_b"]}
    r["vec"] = np.concatenate([cols(L(n)) for k in VEC for n in parts[k]], 1)
    stack = lambda ws: np.concatenate([halves(w).reshape(P, -1) for w in ws], 1)
    r["wqk"] = stack([L(n).T for n in ("a1_wq", "a1_wk", "a2_wq", "a2_wk")])
    r["wv"] = stack([L(n).T for n in ("a1_wv", "a2_wv")])
    r["wo"] = stack([L(n) for n in ("a1_wo", "a2_wo")]).reshape(P, 2, 2, C)
    c1 = L("c1_w")[:, :, 0, 0]
    r["c1"] = stack([c1[:, :C].T, c1[:, C:].T]).reshape(P, 2, 2, C)
    c2 = L("c2_w")
    r["wconv"] = stack([c2[:, :, t // 3, t % 3].T for t in range(TAPS)])
    second = {"wfc1": stack([L("fc1_w").T]), "wfc2": stack([L("fc2_w").T])}
    w = g("L1_attn_w_qkv")
    order = lambda m: m.reshape(C, L1H, 2, 8).transpose(0, 2, 1, 3).reshape(C, C)
    second["wqkv"] = stack([order(w[:, :C]), order(w[:, C:2 * C]), w[:, 2 * C:]])
    second["wout"] = stack([g("L1_attn_w_out")])
    second["wgate"] = stack([g("L1_ffn_gate_w").T])
    second["wexp"] = stack([e.T for e in g("L1_ffn_expert_w")])
    r["second"] = np.concatenate([second[n] for n in W_SECOND], 1).reshape(P, SECOND_CHUNKS, SECOND_CHUNK)\
        .transpose(1, 0, 2).reshape(-1, SECOND_CHUNK)
    r["fc2b"] = np.tile(L("fc2_b"), (P, 1))
    rel = (np.arange(0, (2 * WS - 1) * WS, 2 * WS - 1)[:, None] + np.arange(WS)[None, :]).reshape(1, -1)
    idx = (rel + rel.T)[:, ::-1]
    tabs = [L(n)[idx].reshape(WTOK, WTOK, 2, 4).transpose(0, 3, 2, 1).reshape(WTOK, 4, P)
            for n in ("a1_bias", "a2_bias")]
    r["relb"] = np.concatenate([np.stack(tabs, 1)] * 2, 0)
    r["cst"] = constants()
    return {n: np.ascontiguousarray(m) for n, m in r.items()}


def kernel(**inputs):
    import concourse.bacc as bacc
    from concourse.bass_utils import run_bass_kernel_spmd as run

    nc = bacc.Bacc("TRN2", target_bir_lowering=False, num_devices=1)
    arrays = layouts(inputs)
    a = {n: nc.dram_tensor("in_" + n, m.shape, mybir.dt.from_np(m.dtype), kind="ExternalInput").ap()
         for n, m in arrays.items()}
    out = nc.dram_tensor("out", (B * P, TILES, C), mybir.dt.float32, kind="ExternalOutput").ap()
    build(nc, a, out)
    r = run(nc, [{"in_" + n: m for n, m in arrays.items()}], core_ids=[0])
    got = r.results[0]["out"].reshape(B, P, TILES, C).transpose(0, 3, 2, 1)
    return np.ascontiguousarray(got).reshape(B, C, HW, HW)
```
